# Optimizing a Trainium2 kernel written in Bass

```python
import numpy as np
import jax
import jax.numpy as jnp

def _softmax(x, axis=-1):
    return jax.nn.softmax(x, axis=axis)

def _gelu(x):
    return jax.nn.gelu(x, approximate=True)

def _silu(x):
    return jax.nn.silu(x)

def _sigmoid(x):
    return jax.nn.sigmoid(x)

def _layernorm(x, axis=-1, eps=1e-05):
    m = jnp.mean(x, axis=axis, keepdims=True)
    v = jnp.var(x, axis=axis, keepdims=True)
    return (x - m) / jnp.sqrt(v + eps)

def _scatter_add(tgt, idx, src, axis=0):
    return tgt.at[idx].add(src)

def _segment_sum(src, seg, n):
    return jax.ops.segment_sum(src, seg, n)
kernel_name = 'mk_early_fusion_d1_tok_img1024_r4_722d51'

def setup_inputs(seed: int=0):
    np.random.seed(seed)
    _w = jnp.asarray

    def _rec_inputs():
        import jax
        import jax.numpy as jnp
        _rk = jax.random.key(seed)
        x = -0.00150118 + 0.499729 * jax.random.normal(jax.random.fold_in(_rk, 1), (8, 256, 64, 2), jnp.float32)
        txt = 0.00326275 + 2.8086 * jax.random.normal(jax.random.fold_in(_rk, 2), (8, 128, 256), jnp.float32)
        return (x, txt)
    x, txt = _rec_inputs()

    def _L0_tok_setup():
        import jax, jax.numpy as jnp
        import numpy as np
        import math
        H = 256
        N = 64
        CH = 1
        SEQ_L = 256
        key = jax.random.key(seed)
        k1, k2, k3, k4 = jax.random.split(key, 4)
        log_dt = jax.random.uniform(k1, (H,), dtype=jnp.float32, minval=math.log(0.001), maxval=math.log(0.1))
        inv_A_real = jnp.log(0.5 * jnp.ones((H, N), jnp.float32)) + 0.1 * jax.random.normal(k2, (H, N), dtype=jnp.float32)
        A_imag = jnp.broadcast_to(math.pi * jnp.arange(N, dtype=jnp.float32), (H, N)).copy()
        B_ri = jax.random.normal(k3, (H, N, 2), dtype=jnp.float32) * 0.5
        C_ri = jax.random.normal(k4, (CH, H, N, 2), dtype=jnp.float32) * 0.5
        return {'log_dt': log_dt, 'inv_A_real': inv_A_real, 'A_imag': A_imag, 'B_ri': B_ri, 'C_ri': C_ri, 'L': SEQ_L}
    _L0_tok_all = _L0_tok_setup()
    _L0_tok_in = {k: v for k, v in _L0_tok_all.items() if k in ('log_dt', 'inv_A_real', 'A_imag', 'B_ri')}
    del _L0_tok_all

    def _L0_attn_setup():
        import jax, jax.numpy as jnp
        import numpy as np
        H = 256
        F = 1024
        B, S = (4, 1024)
        EPS = 1e-05

        def _layernorm(x, scale, bias):
            mu = jnp.mean(x, axis=-1, keepdims=True)
            var = jnp.var(x, axis=-1, keepdims=True)
            return (x - mu) * jax.lax.rsqrt(var + EPS) * scale + bias
        key = jax.random.key(seed)
        ks = jax.random.split(key, 4)
        x = jax.random.normal(ks[0], (B, S, H), dtype=jnp.float32)
        W_ret = jax.random.normal(ks[1], (H, H), dtype=jnp.float32) * 0.02
        b_ret = jnp.zeros((H,), dtype=jnp.float32)
        ln1_scale = jnp.ones((H,), dtype=jnp.float32)
        ln1_bias = jnp.zeros((H,), dtype=jnp.float32)
        W1 = jax.random.normal(ks[2], (H, F), dtype=jnp.float32) * 0.02
        b1 = jnp.zeros((F,), dtype=jnp.float32)
        W2 = jax.random.normal(ks[3], (F, H), dtype=jnp.float32) * 0.02
        b2 = jnp.zeros((H,), dtype=jnp.float32)
        ln2_scale = jnp.ones((H,), dtype=jnp.float32)
        ln2_bias = jnp.zeros((H,), dtype=jnp.float32)
        return {'x': x, 'W_ret': W_ret, 'b_ret': b_ret, 'ln1_scale': ln1_scale, 'ln1_bias': ln1_bias, 'W1': W1, 'b1': b1, 'W2': W2, 'b2': b2, 'ln2_scale': ln2_scale, 'ln2_bias': ln2_bias}
    _L0_attn_all = _L0_attn_setup()
    _L0_attn_in = {k: v for k, v in _L0_attn_all.items() if k in ('W_ret', 'b_ret', 'ln1_scale', 'ln1_bias', 'W1', 'b1', 'W2', 'b2', 'ln2_scale', 'ln2_bias')}
    del _L0_attn_all

    def _L0_ffn_setup():
        import math
        import jax, jax.numpy as jnp
        import numpy as np
        B, S, H = (4, 512, 256)
        E, K, I = (8, 2, 256)
        NSH = 2
        CF, RSF = (1.25, 1.0)
        key = jax.random.key(seed)
        ks = jax.random.split(key, 8)
        w = lambda k, sh: jax.random.normal(k, sh, dtype=jnp.float32) * 0.02
        return {'hidden_states': jax.random.normal(ks[0], (B, S, H), dtype=jnp.float32), 'gate_w': w(ks[1], (E, H)), 'we_gate': w(ks[2], (E, I, H)), 'we_up': w(ks[3], (E, I, H)), 'we_down': w(ks[4], (E, H, I)), 'ws_gate': w(ks[5], (NSH * I, H)), 'ws_up': w(ks[6], (NSH * I, H)), 'ws_down': w(ks[7], (H, NSH * I))}
    _L0_ffn_all = _L0_ffn_setup()
    _L0_ffn_in = {k: v for k, v in _L0_ffn_all.items() if k in ('gate_w', 'we_gate', 'we_up', 'we_down', 'ws_gate', 'ws_up', 'ws_down')}
    del _L0_ffn_all
    return {'x': x, 'txt': txt, 'L0_tok_log_dt': _L0_tok_in['log_dt'], 'L0_tok_inv_A_real': _L0_tok_in['inv_A_real'], 'L0_tok_A_imag': _L0_tok_in['A_imag'], 'L0_tok_B_ri': _L0_tok_in['B_ri'], 'L0_attn_W_ret': _L0_attn_in['W_ret'], 'L0_attn_b_ret': _L0_attn_in['b_ret'], 'L0_attn_ln1_scale': _L0_attn_in['ln1_scale'], 'L0_attn_ln1_bias': _L0_attn_in['ln1_bias'], 'L0_attn_W1': _L0_attn_in['W1'], 'L0_attn_b1': _L0_attn_in['b1'], 'L0_attn_W2': _L0_attn_in['W2'], 'L0_attn_b2': _L0_attn_in['b2'], 'L0_attn_ln2_scale': _L0_attn_in['ln2_scale'], 'L0_attn_ln2_bias': _L0_attn_in['ln2_bias'], 'L0_ffn_gate_w': _L0_ffn_in['gate_w'], 'L0_ffn_we_gate': _L0_ffn_in['we_gate'], 'L0_ffn_we_up': _L0_ffn_in['we_up'], 'L0_ffn_we_down': _L0_ffn_in['we_down'], 'L0_ffn_ws_gate': _L0_ffn_in['ws_gate'], 'L0_ffn_ws_up': _L0_ffn_in['ws_up'], 'L0_ffn_ws_down': _L0_ffn_in['ws_down']}

def reference(x, txt, L0_tok_log_dt, L0_tok_inv_A_real, L0_tok_A_imag, L0_tok_B_ri, L0_attn_W_ret, L0_attn_b_ret, L0_attn_ln1_scale, L0_attn_ln1_bias, L0_attn_W1, L0_attn_b1, L0_attn_W2, L0_attn_b2, L0_attn_ln2_scale, L0_attn_ln2_bias, L0_ffn_gate_w, L0_ffn_we_gate, L0_ffn_we_up, L0_ffn_we_down, L0_ffn_ws_gate, L0_ffn_ws_up, L0_ffn_ws_down):
    import jax
    import jax.numpy as jnp

    def _L0_tok_ref(log_dt, inv_A_real, A_imag, B_ri, C_ri, L):
        import jax, jax.numpy as jnp
        import numpy as np
        import math
        H = 256
        N = 64
        CH = 1
        SEQ_L = 256
        dt = jnp.exp(log_dt)
        A = -jnp.exp(inv_A_real) + 1j * A_imag
        B = B_ri[..., 0] + 1j * B_ri[..., 1]
        C = C_ri[..., 0] + 1j * C_ri[..., 1]
        dtA = A * dt[:, None]
        dA = (1.0 + dtA / 2) / (1.0 - dtA / 2)
        C_term = C * B[None]
        log_dA = jnp.log(dA)
        V = jnp.exp(log_dA[:, :, None] * jnp.arange(L))
        K = 2.0 * jnp.einsum('chn,hnl->chl', C_term, V).real
        return K.astype(jnp.float32)

    def _L0_attn_ref(x, W_ret, b_ret, ln1_scale, ln1_bias, W1, b1, W2, b2, ln2_scale, ln2_bias):
        import jax, jax.numpy as jnp
        import numpy as np
        H = 256
        F = 1024
        B, S = (4, 1024)
        EPS = 1e-05

        def _layernorm(x, scale, bias):
            mu = jnp.mean(x, axis=-1, keepdims=True)
            var = jnp.var(x, axis=-1, keepdims=True)
            return (x - mu) * jax.lax.rsqrt(var + EPS) * scale + bias
        sig = jax.nn.sigmoid(jnp.einsum('bsh,hk->bsk', x, W_ret) + b_ret)

        def ema_step(carry, s_t):
            xi = 0.5 * s_t + 0.5 * carry
            return (xi, xi)
        _, ret = jax.lax.scan(ema_step, jnp.zeros((x.shape[0], x.shape[2]), x.dtype), jnp.transpose(sig, (1, 0, 2)))
        retention_output = jnp.transpose(ret, (1, 0, 2))
        h = _layernorm(x + retention_output, ln1_scale, ln1_bias)
        ffn = jnp.einsum('bsf,fh->bsh', jax.nn.gelu(jnp.einsum('bsh,hf->bsf', h, W1) + b1), W2) + b2
        out = _layernorm(h + ffn, ln2_scale, ln2_bias)
        return out

    def _L0_ffn_ref(hidden_states, gate_w, we_gate, we_up, we_down, ws_gate, ws_up, ws_down):
        import math
        import jax, jax.numpy as jnp
        import numpy as np
        B, S, H = (4, 512, 256)
        E, K, I = (8, 2, 256)
        NSH = 2
        CF, RSF = (1.25, 1.0)
        orig_shape = hidden_states.shape
        x = hidden_states.reshape(-1, H)
        N = x.shape[0]
        logits = x.astype(jnp.float32) @ gate_w.astype(jnp.float32).T
        scores = jax.nn.softmax(logits, axis=-1)
        topk_w, topk_idx = jax.lax.top_k(scores, K)
        topk_w = topk_w / (topk_w.sum(-1, keepdims=True) + 1e-20) * RSF
        capacity = math.ceil(CF * N * K / E)
        flat = topk_idx.reshape(-1)
        one_hot = jax.nn.one_hot(flat, E, dtype=jnp.int32)
        pos = jnp.cumsum(one_hot, axis=0) - 1
        pos_tok = jnp.take_along_axis(pos, flat[:, None], axis=1)[:, 0]
        keep = (pos_tok < capacity).reshape(N, K)
        topk_w = topk_w * keep.astype(topk_w.dtype)
        comb = jnp.zeros((N, E), jnp.float32).at[jnp.arange(N)[:, None], topk_idx].add(topk_w)
        g = jnp.einsum('nh,eih->nei', x, we_gate)
        u = jnp.einsum('nh,eih->nei', x, we_up)
        eo = jnp.einsum('nei,ehi->neh', jax.nn.silu(g) * u, we_down)
        y = jnp.einsum('neh,ne->nh', eo, comb)
        sh = jax.nn.silu(x @ ws_gate.T) * (x @ ws_up.T) @ ws_down.T
        return (y + sh).reshape(orig_shape)
    h = _L0_tok_ref(L0_tok_log_dt, L0_tok_inv_A_real, L0_tok_A_imag, L0_tok_B_ri, x, 256)
    h = jnp.concatenate([h, txt], axis=1)
    h = h + _L0_attn_ref(_layernorm(h, axis=-1), L0_attn_W_ret, L0_attn_b_ret, L0_attn_ln1_scale, L0_attn_ln1_bias, L0_attn_W1, L0_attn_b1, L0_attn_W2, L0_attn_b2, L0_attn_ln2_scale, L0_attn_ln2_bias)
    h = h + _L0_ffn_ref(_layernorm(h, axis=-1), L0_ffn_gate_w, L0_ffn_we_gate, L0_ffn_we_up, L0_ffn_we_down, L0_ffn_ws_gate, L0_ffn_ws_up, L0_ffn_ws_down)
    return h

_drawn_inputs = setup_inputs


def setup_inputs(seed=0):
    import zlib

    import numpy as np

    out = dict(_drawn_inputs(seed))
    spreads = {'L0_attn_b_ret': (0.0, 0.8),
     'L0_attn_ln1_scale': (1.0, 0.2),
     'L0_attn_ln1_bias': (0.0, 0.388),
     'L0_attn_b1': (0.0, 0.8),
     'L0_attn_b2': (0.0, 0.365),
     'L0_attn_ln2_scale': (1.0, 0.2),
     'L0_attn_ln2_bias': (0.0, 0.396)}
    factors = {'L0_attn_W_ret': 5.943,
     'L0_ffn_gate_w': 8.0,
     'L0_ffn_we_gate': 8.0,
     'L0_ffn_we_up': 8.0,
     'L0_ffn_we_down': 8.0,
     'L0_ffn_ws_gate': 8.0,
     'L0_ffn_ws_up': 8.0,
     'L0_ffn_ws_down': 8.0}
    for name, (base, spread) in spreads.items():
        noise = np.random.default_rng([zlib.crc32(name.encode()), seed]).standard_normal(out[name].shape)
        drawn = base * np.exp(spread * noise) if base else spread * noise
        out[name] = jnp.asarray(drawn.astype(out[name].dtype))
    for name, factor in factors.items():
        out[name] = (out[name] * factor).astype(out[name].dtype)
    return out
```

```python
from contextlib import ExitStack
import math

import concourse.bass as bass
from concourse import mybir

ALU = mybir.AluOpType
ACT = mybir.ActivationFunctionType
AX = mybir.AxisListType
F32 = mybir.dt.float32
FR = mybir.dt.float32r
BF16 = mybir.dt.bfloat16
I32 = mybir.dt.int32
U32 = mybir.dt.uint32
P = 128

B, S_SSM, N_STATE = 8, 256, 64
S_TXT, D = 128, 256
SEQ = S_SSM + S_TXT
TB = SEQ // P
NT = B * TB
DC = D // P

NA, NB = 4, 64
HP = S_SSM // 2
HC = 16
NCHUNK = HP // HC
POOL_CHUNKS = 2
CA = B * NA

F_ATT = 1024
FB = F_ATT // P
NE = 8
EPS = 1e-5
RSQRT_SEED = float(0xdf3759df)

TOK = B * SEQ
TOPK = 2
CAP = math.ceil(1.25 * TOK * TOPK / NE)
HALF = CAP // 2
XP = 120
XT = HALF // XP
I_EXP, I_SH = 256, 512
EB, SB = I_EXP // P, I_SH // P
OUT_OF_RANGE = 1 << 17
SH_FIRST = 4
ZERO_PARTS = 10
assert XT * XP == HALF and 2 * HALF == CAP


def ssm_phase(nc, io, scratch, per, xs):
    with ExitStack() as ctx:
        sb = lambda name, shape, dt=F32: ctx.enter_context(nc.sbuf_tensor(name, shape, dt))
        sem = lambda name: ctx.enter_context(nc.semaphore(name))
        dt_bc = sb("dt_bc", [P, HP])
        inv_a = sb("inv_a", [P, HP])
        a_im = sb("a_im", [P, HP])
        b_re = sb("b_re", [P, HP])
        b_im = sb("b_im", [P, HP])
        c_in = sb("c_in", [P, 2, HP, B])
        u = sb("u", [P, HP])
        v = sb("v", [P, HP])
        s1 = sb("s1", [P, HP])
        s2 = sb("s2", [P, HP])
        s3 = sb("s3", [P, HP])
        s4 = sb("s4", [P, HP])
        pw_re = sb("pw_re", [P, HP, NB + 1])
        pw_im = sb("pw_im", [P, HP, NB + 1])
        w_re = sb("w_re", [P, HP, NA])
        w_im = sb("w_im", [P, HP, NA])
        g_re = sb("g_re", [P, HP, B])
        g_im = sb("g_im", [P, HP, B])
        gn_re = sb("gn_re", [P, HP, B])
        gn_im = sb("gn_im", [P, HP, B])
        l_re = sb("l_re", [P, HP, B, NA])
        l_im = sb("l_im", [P, HP, B, NA])
        tv = [sb(f"tv{j}", [P, HP * 8]) for j in range(4)]
        tp = [sb(f"tp{j}", [P, HC * 32]) for j in range(4)]
        k_out = sb("k_out", [P, 2, 2, HC * NB // 4])
        psK = ctx.enter_context(nc.psum_tensor("psK", [P, 2, 4, 512], F32))

        ident, raw = per["ident"], per["raw"]
        zero = sb("zero", [P, NE * CAP * D // P // ZERO_PARTS])

        raw_loaded, zero_made, zeroed = sem("raw_loaded"), sem("zero_made"), sem("zeroed")
        ident_made = sem("ident_made")
        loads = [sem(f"ssm_load{j}") for j in range(6)]
        exps = sem("exps")
        base = sem("base")
        dve_c = sem("dve_chain")
        pool_c = sem("pool_chain")
        tab = [sem(f"tables{k}") for k in range(NCHUNK)]
        summed = sem("summed")
        evac = sem("evac")
        stored = [sem(f"k_stored{q}") for q in range(2)]
        block = ctx.enter_context(nc.Block())

        def cmul(eng, link, wait, tmp, ore, oim, are, aim, bre, bim):
            t = tmp
            link(eng.tensor_tensor(t[0], are, bre, ALU.mult))
            link(eng.tensor_tensor(t[1], aim, bim, ALU.mult))
            link(eng.tensor_tensor(t[2], are, bim, ALU.mult))
            link(eng.tensor_tensor(t[3], aim, bre, ALU.mult))
            wait()
            link(eng.tensor_tensor(ore, t[0], t[1], ALU.subtract))
            link(eng.tensor_tensor(oim, t[2], t[3], ALU.add))
            wait()

        def powers(eng, link, wait, tmp, h, k, n):
            tt = [x[:, 0:n * k].rearrange("p (h k) -> p h k", h=n) for x in tmp]
            cre = pw_re[:, h, k:k + 1].to_broadcast([P, n, k])
            cim = pw_im[:, h, k:k + 1].to_broadcast([P, n, k])
            cmul(eng, link, wait, tt, pw_re[:, h, k + 1:2 * k + 1], pw_im[:, h, k + 1:2 * k + 1],
                 pw_re[:, h, 1:k + 1], pw_im[:, h, 1:k + 1], cre, cim)

        def tables(eng, link, wait, tmp, k):
            h = slice(k * HC, (k + 1) * HC)
            for w in (8, 16, 32):
                powers(eng, link, wait, tmp, h, w, HC)
            s = [x[:, 0:HC].rearrange("p (h k) -> p h k", k=1) for x in tmp]
            one, two, three = slice(1, 2), slice(2, 3), slice(3, 4)
            link(eng.tensor_copy(w_re[:, h, one], pw_re[:, h, NB:NB + 1]))
            link(eng.tensor_copy(w_im[:, h, one], pw_im[:, h, NB:NB + 1]))
            wait()
            cmul(eng, link, wait, s, w_re[:, h, two], w_im[:, h, two], w_re[:, h, one], w_im[:, h, one],
                 w_re[:, h, one], w_im[:, h, one])
            cmul(eng, link, wait, s, w_re[:, h, three], w_im[:, h, three], w_re[:, h, two], w_im[:, h, two],
                 w_re[:, h, one], w_im[:, h, one])
            t4 = [x[:, 0:HC * 32].rearrange("p (h c a) -> p h c a", h=HC, c=B) for x in tmp]
            gb = lambda g: g[:, h, :].unsqueeze(3).to_broadcast([P, HC, B, NA])
            wb = lambda w: w[:, h, :].unsqueeze(2).to_broadcast([P, HC, B, NA])
            link(eng.tensor_tensor(t4[0], gb(g_re), wb(w_re), ALU.mult))
            link(eng.tensor_tensor(t4[1], gb(g_im), wb(w_im), ALU.mult))
            link(eng.tensor_tensor(t4[2], gb(gn_re), wb(w_im), ALU.mult))
            link(eng.tensor_tensor(t4[3], gb(gn_im), wb(w_re), ALU.mult))
            wait()
            eng.tensor_tensor(l_re[:, h], t4[0], t4[1], ALU.subtract).then_inc(tab[k], 1)
            link(eng.tensor_tensor(l_im[:, h], t4[2], t4[3], ALU.add))
            wait()

        @block.sync
        def _(sp):
            sp.dma_start(dt_bc[0:64, :], io["log_dt"][0:1, 0:HP].to_broadcast([64, HP])).then_inc(loads[0], 16)
            sp.dma_start(dt_bc[64:128, :], io["log_dt"][0:1, HP:2 * HP].to_broadcast([64, HP])).then_inc(loads[0], 16)
            sp.dma_start(inv_a[:], io["inv_a"]).then_inc(loads[1], 16)
            sp.dma_start(a_im[:], io["a_im"]).then_inc(loads[2], 16)
            sp.dma_start(b_re[:], io["b_ri"][0]).then_inc(loads[3], 16)
            sp.dma_start(b_im[:], io["b_ri"][1]).then_inc(loads[4], 16)
            sp.dma_start(c_in[:], io["c_ri"].rearrange("p r h c -> p (r h c)")).then_inc(loads[5], 16)
            sp.dma_start(raw[:], io["raw_w"]).then_inc(raw_loaded, 16)
            sp.wait_ge(zero_made, 1)
            xs_flat = xs.rearrange("(p r) d -> p (r d)", p=P)
            w = xs_flat.shape[1] // ZERO_PARTS
            for j in range(ZERO_PARTS):
                sp.dma_start(xs_flat[:, j * w:(j + 1) * w], zero[:]).then_inc(zeroed, 16)
            for k in range(NCHUNK):
                sp.wait_ge(evac, 2 * (k + 1))
                for half in range(2):
                    h0 = half * HP + k * HC
                    dst = scratch[h0:h0 + HC].rearrange("(g j) c (a b) -> (j c a) g b", j=4, b=NB)
                    sp.dma_start(dst, k_out[:, k % 2, half, :].rearrange("p (g b) -> p g b", b=NB)).then_inc(stored[k % 2], 16)
            for q in range(2):
                sp.wait_ge(stored[q], 16 * NCHUNK)
            sp.wait_ge(raw_loaded, 16)
            sp.wait_ge(zeroed, 16 * ZERO_PARTS)

        @block.scalar
        def _(act):
            act.wait_ge(loads[0], 32)
            nc.scalar.activation(dt_bc[:], dt_bc[:], ACT.Exp).then_inc(exps, 1)
            act.wait_ge(loads[1], 16)
            nc.scalar.activation(inv_a[:], inv_a[:], ACT.Exp).then_inc(exps, 1)
            for k in range(NCHUNK):
                for half in range(2):
                    act.wait_ge(summed, 2 * k + half + 1)
                    if k >= 2:
                        act.wait_ge(stored[k % 2], 32 * (k // 2))
                    nc.scalar.activation(k_out[:, k % 2, half, :], psK[:, half, k % 4, 0:HC * NB // 4], ACT.Copy).then_inc(evac, 1)

        @block.vector
        def _(dve):
            n = [0]

            def link(ins):
                n[0] += 1
                ins.then_inc(dve_c, 1)

            def wait():
                dve.wait_ge(dve_c, n[0])

            V = nc.vector
            link(V.memset(pw_re[:, :, 0:1], 1.0))
            link(V.memset(pw_im[:, :, 0:1], 0.0))
            link(V.memset(w_re[:, :, 0:1], 1.0))
            link(V.memset(w_im[:, :, 0:1], 0.0))
            dve.wait_ge(exps, 2)
            dve.wait_ge(loads[2], 16)
            link(V.scalar_tensor_tensor(out=u[:], in0=inv_a[:], scalar=-0.5, in1=dt_bc[:], op0=ALU.mult, op1=ALU.mult))
            link(V.scalar_tensor_tensor(out=v[:], in0=a_im[:], scalar=0.5, in1=dt_bc[:], op0=ALU.mult, op1=ALU.mult))
            wait()
            link(V.tensor_tensor(s1[:], u[:], u[:], ALU.mult))
            link(V.tensor_tensor(s2[:], v[:], v[:], ALU.mult))
            link(V.tensor_scalar(s3[:], u[:], -1.0, 1.0, ALU.mult, ALU.add))
            wait()
            link(V.tensor_tensor(s1[:], s1[:], s2[:], ALU.add))
            link(V.tensor_tensor(s4[:], s3[:], s3[:], ALU.mult))
            wait()
            link(V.tensor_tensor(s4[:], s4[:], s2[:], ALU.add))
            link(V.tensor_scalar(s1[:], s1[:], -1.0, 1.0, ALU.mult, ALU.add))
            wait()
            link(V.reciprocal(s4[:], s4[:]))
            wait()
            one = lambda x: x[:].unsqueeze(2)
            link(V.tensor_tensor(pw_re[:, :, 1:2], one(s1), one(s4), ALU.mult))
            link(V.scalar_tensor_tensor(out=pw_im[:, :, 1:2], in0=one(v), scalar=2.0, in1=one(s4), op0=ALU.mult, op1=ALU.mult))
            for j in range(3, 6):
                dve.wait_ge(loads[j], 16)
            link(V.tensor_scalar(b_re[:], b_re[:], 2.0, None, ALU.mult))
            link(V.tensor_scalar(b_im[:], b_im[:], 2.0, None, ALU.mult))
            wait()
            bb = lambda x: x[:].unsqueeze(2).to_broadcast([P, HP, B])
            t8 = [x[:].rearrange("p (h c) -> p h c", c=B) for x in tv]
            cmul(V, link, wait, t8, g_re[:], g_im[:], c_in[:, 0], c_in[:, 1], bb(b_re), bb(b_im))
            link(V.tensor_scalar(gn_re[:], g_re[:], -1.0, None, ALU.mult))
            link(V.tensor_scalar(gn_im[:], g_im[:], -1.0, None, ALU.mult))
            for k in (1, 2, 4):
                powers(V, link, wait, tv, slice(0, HP), k, HP)
            dve.sem_inc(base, 1)
            for k in range(NCHUNK - POOL_CHUNKS):
                tables(V, link, wait, tv, k)
                dve.sem_inc(tab[k], 1)

        @block.gpsimd
        def _(pool):
            n = [0]

            def link(ins):
                n[0] += 1
                ins.then_inc(pool_c, 1)

            def wait():
                pool.wait_ge(pool_c, n[0])

            nc.gpsimd.memset(zero[:], 0.0).then_inc(zero_made, 1)
            nc.gpsimd.memset(ident[:], 0.0).then_inc(ident_made, 1)
            pool.wait_ge(ident_made, 1)
            nc.gpsimd.affine_select(out=ident[:], in_=ident[:], compare_op=ALU.not_equal, fill=1.0, base=0,
                                    pattern=[[-1, P]], channel_multiplier=1).then_inc(ident_made, 1)
            pool.wait_ge(base, 1)
            for k in range(NCHUNK - POOL_CHUNKS, NCHUNK):
                tables(nc.gpsimd, link, wait, tp, k)
                pool.sem_inc(tab[k], 1)

        @block.tensor
        def _(pe):
            for k in range(NCHUNK):
                pe.wait_ge(tab[k], 2)
                if k >= 4:
                    pe.wait_ge(evac, 2 * (k - 3))
                for half in range(2):
                    r = slice(64 * half, 64 * half + 64)
                    for i in range(HC):
                        h, j, g = k * HC + i, i % 4, i // 4
                        out = psK[32 * j:32 * j + 32, half, k % 4, g * NB:(g + 1) * NB]
                        pe.matmul(out, l_re[r, h].rearrange("p c a -> p (c a)"), pw_re[r, h, 0:NB],
                                  start=True, stop=False)
                        mm = pe.matmul(out, l_im[r, h].rearrange("p c a -> p (c a)"), pw_im[r, h, 0:NB],
                                       start=False, stop=True)
                    mm.then_inc(summed, 1)


def ln_stats(V, dve, sem, seen, tiles, st, mv, rstd, nmr, fillers=()):
    n = len(tiles)
    fillers = list(fillers)
    rstd, nmr = rstd[:, 0:n], nmr[:, 0:n]
    diff, total, sq, var, half = (mv[:, j, 0:n] for j in range(5))
    mean_e, sq_e, mean_o, sq_o = (st[:, 0:n, j] for j in (1, 2, 4, 5))
    for j, x in enumerate(tiles):
        V.bn_stats(st[:, j, :], x).then_inc(sem, 1)

    def after_last(k):
        if fillers:
            fillers.pop(0)()
        dve.wait_ge(sem, seen + k)

    after_last(n)
    V.tensor_tensor(diff, mean_e, mean_o, ALU.subtract).then_inc(sem, 1)
    V.tensor_tensor(total, mean_e, mean_o, ALU.add).then_inc(sem, 1)
    V.tensor_tensor(sq, sq_e, sq_o, ALU.add).then_inc(sem, 1)
    after_last(n + 3)
    V.scalar_tensor_tensor(out=diff, in0=diff, scalar=0.25, in1=diff, op0=ALU.mult, op1=ALU.mult).then_inc(sem, 1)
    V.tensor_scalar(sq, sq, 1.0 / D, EPS, ALU.mult, ALU.add).then_inc(sem, 1)
    k = n + 5
    after_last(k)
    V.tensor_tensor(var, sq, diff, ALU.add).then_inc(sem, 1)
    after_last(k + 1)
    V.tensor_scalar(half.bitcast(I32), var.bitcast(I32), 1, None, ALU.logical_shift_right).then_inc(sem, 1)
    after_last(k + 2)
    V.tensor_scalar(rstd.bitcast(U32), half.bitcast(I32), -1.0, RSQRT_SEED, ALU.mult, ALU.add).then_inc(sem, 1)
    k += 3
    for _ in range(3):
        after_last(k)
        V.scalar_tensor_tensor(out=half, in0=rstd, scalar=0.5, in1=rstd, op0=ALU.mult, op1=ALU.mult).then_inc(sem, 1)
        after_last(k + 1)
        V.tensor_tensor(half, half, var, ALU.mult).then_inc(sem, 1)
        after_last(k + 2)
        V.scalar_tensor_tensor(out=rstd, in0=half, scalar=1.5, in1=rstd, op0=ALU.subtract, op1=ALU.mult).then_inc(sem, 1)
        k += 3
    after_last(k)
    V.scalar_tensor_tensor(out=nmr, in0=total, scalar=-0.5, in1=rstd, op0=ALU.mult, op1=ALU.mult).then_inc(sem, 1)
    assert k + 1 == ln_signals(n) and not fillers


def ln_signals(n):
    return n + 18


ONE, TWO = ln_signals(TB), ln_signals(2 * TB)


def attn_phase(nc, io, scratch, per):
    H, zT, LGT, ident = per["H"], per["zT"], per["LGT"], per["ident"]
    rz, nmz = per["rz"], per["nmz"]
    with ExitStack() as ctx:
        sb = lambda name, shape, dt=F32: ctx.enter_context(nc.sbuf_tensor(name, shape, dt))
        sem = lambda name: ctx.enter_context(nc.semaphore(name))
        raw = per["raw"]
        ret_raw, w1_raw, w2_raw = (raw[:, a:b].rearrange("p (k n) -> p k n", n=n)
                                   for a, b, n in ((0, 512, D), (512, 2560, F_ATT), (2560, 4608, D)))
        ret_w = [sb(f"ret_w{j}", [P, DC, D], FR) for j in range(2)]
        w1 = [sb(f"w1_{j}", [P, DC, F_ATT], FR) for j in range(2)]
        w2 = [sb(f"w2_{j}", [P, FB, D], FR) for j in range(2)]
        gate_w = sb("gate_w", [P, DC, NE])
        cols = sb("cols", [P, 5, DC])
        b1 = sb("b1", [P, FB])
        ln2s = sb("ln2s", [P, D])
        ln2b = sb("ln2b", [P, D])
        halves = sb("halves", [P, SEQ])
        primer = sb("primer", [1, 1])
        xn = sb("xn", [P, TB, D])
        xT = sb("xT", [P, DC, SEQ])
        x_hi = sb("x_hi", [P, DC, SEQ], FR)
        x_lo = sb("x_lo", [P, DC, SEQ], FR)
        th = sb("th", [P, DC, SEQ])
        ret = sb("ret", [P, DC, SEQ])
        h1n = sb("h1n", [P, TB, D])
        h1T = sb("h1T", [P, DC, SEQ])
        h1_hi = sb("h1_hi", [P, DC, SEQ], FR)
        h1_lo = sb("h1_lo", [P, DC, SEQ], FR)
        NG = 6
        g = [sb(f"g{j}", [P, SEQ]) for j in range(NG)]
        g_hi = sb("g_hi", [P, FB, SEQ], FR)
        g_lo = sb("g_lo", [P, FB, SEQ], FR)
        r2T = sb("r2T", [P, DC, SEQ])
        n2 = sb("n2", [P, TB, D])
        zn = sb("zn", [P, TB, D])
        st = [sb(f"st{j}", [P, 2 * TB, 6]) for j in range(2)]
        mv = [sb(f"mv{j}", [P, 5, 2 * TB]) for j in range(2)]
        rs = [sb(f"rs{j}", [P, 2 * TB]) for j in range(2)]
        nm = [sb(f"nm{j}", [P, 2 * TB]) for j in range(2)]

        pm = lambda name: ctx.enter_context(nc.psum_tensor(name, [P, 2, 512], F32))
        psX, psY, psF, psG = pm("psX"), pm("psY"), pm("psF"), pm("psG")
        rowsY = psY[:].rearrange("p a b -> p (a b)")
        tokY = [rowsY[:, D * t:D * (t + 1)] for t in range(TB)]
        X = psX[:, :, 0:SEQ]
        Y = psY[:, :, 0:SEQ]

        consts = [sem(f"const{j}") for j in range(9)]
        h_loaded = sem("h_loaded")
        w_split = sem("w_split")
        w_pool = sem("w_pool")
        half_b = sem("half_b")
        ln_a, ln_b, kept = sem("ln_a"), sem("ln_b"), sem("kept")
        x_ready, t1, x_copied, x_split = sem("x_ready"), sem("t1"), sem("x_copied"), sem("x_split")
        ret_mm, tanh_done, scan, r_ready = sem("ret_mm"), sem("tanh_done"), sem("scan"), sem("r_ready")
        t2, h1n_ready, t3, h1_copied = sem("t2"), sem("h1n_ready"), sem("t3"), sem("h1_copied")
        h1_hi_s, h1_lo_s = sem("h1_hi_s"), sem("h1_lo_s")
        w1_mm, gelu, g_hi_s, g_lo_s = sem("w1_mm"), sem("gelu"), sem("g_hi_s"), sem("g_lo_s")
        w2_mm, r2, t4, n2_ready = sem("w2_mm"), sem("r2"), sem("t4"), sem("n2_ready")
        n2_scaled, h_biased, h_new = sem("n2_scaled"), sem("h_biased"), sem("h_new")
        z_ready, t5, z_copied, lg_mm, lg_copied = (sem("z_ready"), sem("t5"), sem("z_copied"), sem("lg_mm"),
                                                   sem("lg_copied"))
        block = ctx.enter_context(nc.Block())
        V, A, G, T = nc.vector, nc.scalar, nc.gpsimd, nc.tensor

        Ht = lambda b, t: H[:, bass.ds(b * TB + t, 1), :].rearrange("p o d -> p (o d)")
        Hb = lambda b: H[:, bass.ds(b * TB, TB), :]

        slice_of = lambda x, b: x[:, bass.ds(b * TB, TB)]

        def iterations(eng, step):
            step(0), step(1), step(2)
            with eng.Fori(3, B - 1) as i:
                step(i)
            for i in range(B - 1, B + 3):
                step(i)

        def parts(i):
            if type(i) is not int:
                return (True,) * 5
            return tuple(0 <= i + d < B for d in (0, -1, -2, -3, 1))

        def signals_a(i):
            if type(i) is not int:
                return i * TWO + (2 * ONE - 2 * TWO)
            return sum(ln_signals(TB * (parts(j)[0] + parts(j)[2])) if parts(j)[0] or parts(j)[2] else 0
                       for j in range(i))

        def signals_b(i):
            if type(i) is not int:
                return i * TWO + (3 * ONE - 2 * TWO)
            return ONE + sum(ln_signals(TB * (parts(j)[4] + parts(j)[2])) if parts(j)[4] or parts(j)[2] else 0
                             for j in range(i))

        @block.sync
        def _(sp):
            sp.dma_start(ln2s[:], io["ln2_scale"].to_broadcast([P, D])).then_inc(consts[0], 16)
            for b in range(B):
                for t in range(S_SSM // P):
                    sp.dma_start(H[:, b * TB + t, :], scratch[t * P:(t + 1) * P, b, :]).then_inc(h_loaded, 16)
                sp.dma_start(H[:, b * TB + TB - 1, :], io["txt"][b]).then_inc(h_loaded, 16)
                sp.wait_ge(h_loaded, 16 * TB * (b + 1))
                if b == 0:
                    sp.dma_start(ln2b[:], io["ln2_bias"].to_broadcast([P, D])).then_inc(consts[1], 16)

        @block.gpsimd
        def _(pool):
            G.memset(halves[:], 0.5).then_inc(w_pool, 1)
            pool.wait_ge(w_split, 3)
            G.tensor_tensor(w2[1][:], w2_raw, w2[0][:].bitcast(F32), ALU.subtract).then_inc(w_pool, 1)
            pool.wait_ge(consts[0], 16)
            pool.wait_ge(consts[1], 16)

            def step(i):
                front, mid, tail, last, more = parts(i)
                f, m, t = i, i - 1, i - 2
                if front:
                    pool.wait_ge(x_ready, f + 1)
                    pool.wait_ge(consts[1], 16)
                    G.tensor_tensor(Hb(f), Hb(f), ln2b[:].unsqueeze(1).to_broadcast([P, TB, D]), ALU.add)\
                        .then_inc(h_biased, 1)
                if tail:
                    pool.wait_ge(n2_ready, t + 1)
                    G.tensor_tensor(n2[:], n2[:], ln2s[:].unsqueeze(1).to_broadcast([P, TB, D]), ALU.mult)\
                        .then_inc(n2_scaled, 1)

            iterations(pool, step)

        @block.vector
        def _(dve):
            dve.wait_ge(w_split, 1)
            V.tensor_tensor(ret_w[1][:], ret_raw, ret_w[0][:].bitcast(F32), ALU.subtract).then_inc(half_b, 1)
            dve.wait_ge(w_split, 2)
            V.tensor_tensor(w1[1][:], w1_raw, w1[0][:].bitcast(F32), ALU.subtract).then_inc(half_b, 1)
            dve.wait_ge(consts[2], 16)
            V.tensor_scalar(cols[:, 4, :], cols[:, 0, :], 0.5, None, ALU.mult).then_inc(half_b, 1)

            def g_low(b, f):
                dve.wait_ge(gelu, b * (2 * FB) + (2 * f + 2))
                V.tensor_tensor(g_lo[:, f, :], g[f % NG][:], g_hi[:, f, :].bitcast(F32), ALU.subtract)\
                    .then_inc(g_lo_s, 1)

            def residual(b, k):
                dve.wait_ge(w2_mm, b * DC + k + 1)
                V.scalar_tensor_tensor(out=r2T[:, k, :], in0=psG[:, k, 0:SEQ], scalar=cols[:, 3, k:k + 1],
                                       in1=h1T[:, k, :], op0=ALU.add, op1=ALU.add).then_inc(r2, 1)

            def step(i):
                front, mid, tail, last, more = parts(i)
                f, m, t = i, i - 1, i - 2
                if front:
                    dve.wait_ge(x_copied, (f + 1) * 2)
                    V.tensor_tensor(x_lo[:], xT[:], x_hi[:].bitcast(F32), ALU.subtract).then_inc(x_split, 1)
                lows = [lambda k=k: g_low(m, k) for k in range(FB)] if mid else []
                if tail or more:
                    tiles = []
                    if tail:
                        dve.wait_ge(t4, t + 1)
                        tiles += tokY
                    if more:
                        dve.wait_ge(h_loaded, (f + 2) * (16 * TB))
                        tiles += [Ht(f + 1, j) for j in range(TB)]
                    fill = [lows.pop(0) for _ in range(3)] if mid else []
                    ln_stats(V, dve, ln_b, signals_b(i), tiles, st[1], mv[1], rs[1], nm[1], fill)
                if front:
                    dve.wait_ge(tanh_done, (f + 1) * DC)
                    V.tensor_scalar(th[:], th[:], 0.25, 0.25, ALU.mult, ALU.add).then_inc(scan, 1)
                    dve.wait_ge(scan, f * 3 + 1)
                    for k in range(DC):
                        V.tensor_tensor_scan(ret[:, k, :], halves[:], th[:, k, :], 0.0, ALU.mult, ALU.add).then_inc(scan, 1)
                    dve.wait_ge(scan, f * 3 + 3)
                    V.tensor_tensor(ret[:], ret[:], xT[:], ALU.add).then_inc(r_ready, 1)
                for low in lows:
                    low()
                if tail:
                    dve.wait_ge(n2_scaled, t + 1)
                    dve.wait_ge(h_biased, t + 1)
                    V.tensor_tensor(Hb(t), Hb(t), n2[:], ALU.add).then_inc(h_new, 1)
                if front or tail:
                    tiles = []
                    if front:
                        dve.wait_ge(t2, f + 1)
                        tiles += tokY
                    if tail:
                        tiles += [Ht(t, j) for j in range(TB)]
                        dve.wait_ge(w_pool, 1)
                        dve.wait_ge(h_new, t + 1)
                    ln_stats(V, dve, ln_a, signals_a(i), tiles, st[0], mv[0], rs[0], nm[0])
                if mid:
                    residual(m, 0)
                if tail:
                    o = TB if front else 0
                    dve.wait_ge(ln_a, signals_a(i) + (TWO if front else ONE))
                    V.tensor_copy(slice_of(rz, t), rs[0][:, o:o + TB])
                    V.tensor_copy(slice_of(nmz, t), nm[0][:, o:o + TB]).then_inc(kept, 1)
                if mid:
                    residual(m, 1)
                if front:
                    dve.wait_ge(h1_copied, (f + 1) * (2 * DC))
                    V.tensor_tensor(h1_lo[:], h1T[:], h1_hi[:].bitcast(F32), ALU.subtract).then_inc(h1_lo_s, 1)

            dve.wait_ge(w_pool, 1)
            dve.wait_ge(h_loaded, 16 * TB)
            ln_stats(V, dve, ln_b, 0, [Ht(0, j) for j in range(TB)], st[1], mv[1], rs[1], nm[1])
            iterations(dve, step)

        @block.scalar
        def _(act):
            act.dma_start(cols[:, 0:4, :], io["cols"]).then_inc(consts[2], 16)
            act.dma_start(b1[:], io["b1"]).then_inc(consts[3], 16)
            act.dma_start(gate_w[:], io["gate_w"]).then_inc(consts[4], 16)
            A.activation(primer[:], ident[0:1, 0:1], ACT.Gelu_apprx_tanh)
            A.activation(ret_w[0][:], ret_raw, ACT.Copy).then_inc(w_split, 1)
            A.activation(w1[0][:], w1_raw, ACT.Copy).then_inc(w_split, 1)
            A.activation(w2[0][:], w2_raw, ACT.Copy).then_inc(w_split, 1)

            def normalise(out, src, group, j):
                return A.activation(out, src, ACT.Identity, bias=nm[group][:, j:j + 1], scale=rs[group][:, j:j + 1])

            def x_of(b, signals, o):
                act.wait_ge(ln_b, signals)
                if type(b) is not int or b >= 1:
                    act.wait_ge(t1, b)
                for j in range(TB):
                    a = normalise(xn[:, j, :], Ht(b, j), 1, o + j)
                a.then_inc(x_ready, 1)

            def gelu_of(b, f, first):
                act.wait_ge(w1_mm, b * FB + f + 1)
                if f >= NG or not first:
                    act.wait_ge(g_lo_s, b * FB + (f - NG + 1))
                for out in (g[f % NG][:], g_hi[:, f, :]):
                    A.activation(out, psF[:, f % 2, 0:SEQ], ACT.Gelu_apprx_tanh, bias=b1[:, f:f + 1]).then_inc(gelu, 1)

            def step(i):
                front, mid, tail, last, more = parts(i)
                f, m, t = i, i - 1, i - 2
                first = type(i) is int and i == 1
                if front:
                    act.wait_ge(t1, f + 1)
                    if type(i) is not int or i >= 1:
                        act.wait_ge(r_ready, f)
                    A.activation(xT[:], X, ACT.Copy).then_inc(x_copied, 1)
                    A.activation(x_hi[:], X, ACT.Copy).then_inc(x_copied, 1)
                if mid:
                    for k in range(3):
                        gelu_of(m, k, first)
                if tail:
                    act.wait_ge(ln_b, signals_b(i) + (TWO if more else ONE))
                    for j in range(TB):
                        a = normalise(n2[:, j, :], tokY[j], 1, j)
                    a.then_inc(n2_ready, 1)
                if last:
                    act.wait_ge(lg_mm, t)
                    A.activation(LGT[0:NE, bass.ds((t - 1) * SEQ, SEQ)], psG[0:NE, 0, 0:SEQ], ACT.Copy).then_inc(lg_copied, 1)
                if front:
                    act.wait_ge(ret_mm, f + 1)
                    for k in range(DC):
                        A.activation(th[:, k, :], Y[:, k, :], ACT.Tanh, bias=cols[:, 4, k:k + 1], scale=0.5)\
                            .then_inc(tanh_done, 1)
                if mid:
                    for k in range(3, FB):
                        gelu_of(m, k, first)
                if more:
                    x_of(f + 1, signals_b(i) + (TWO if tail else ONE), TB if tail else 0)
                if front:
                    act.wait_ge(ln_a, signals_a(i) + (TWO if tail else ONE))
                    for j in range(TB):
                        a = normalise(h1n[:, j, :], tokY[j], 0, j)
                    a.then_inc(h1n_ready, 1)
                if tail:
                    if not front:
                        act.wait_ge(ln_a, signals_a(i) + ONE)
                    if type(i) is not int or i >= 3:
                        act.wait_ge(t5, t)
                    for j in range(TB):
                        a = normalise(zn[:, j, :], Ht(t, j), 0, (TB if front else 0) + j)
                    a.then_inc(z_ready, 1)
                if front:
                    act.wait_ge(t3, f + 1)
                    if mid:
                        act.wait_ge(r2, (m + 1) * DC)
                    for k in range(DC):
                        for out in (h1T[:, k, :], h1_hi[:, k, :]):
                            A.activation(out, X[:, k, :], ACT.Identity, bias=cols[:, 2, k:k + 1],
                                         scale=cols[:, 1, k:k + 1]).then_inc(h1_copied, 1)
                if tail:
                    act.wait_ge(t5, t + 1)
                    A.activation(zT[:, :, bass.ds(t * SEQ, SEQ)], Y, ACT.Copy).then_inc(z_copied, 1)

            act.wait_ge(half_b, 3)
            for j in (3, 4):
                act.wait_ge(consts[j], 16)
            x_of(0, ONE, 0)
            iterations(act, step)

        @block.tensor
        def _(pe):
            def to_features(src, ps):
                for t in range(TB):
                    for k in range(DC):
                        mm = T.transpose(ps[:, k, t * P:(t + 1) * P], src[:, t, k * P:(k + 1) * P], ident[:])
                return mm

            def to_tokens(src):
                for t in range(TB):
                    for k in range(DC):
                        mm = T.transpose(rowsY[:, t * D + k * P:t * D + (k + 1) * P], src[:, k, t * P:(t + 1) * P], ident[:])
                return mm

            def product(out, w, cols_, act_hi, act_lo, first, last):
                T.matmul(out, w[0][cols_], act_hi, start=first, stop=False)
                T.matmul(out, w[0][cols_], act_lo, start=False, stop=False)
                return T.matmul(out, w[1][cols_], act_hi, start=False, stop=last)

            def hidden(b, f, first):
                if f >= 2 or not first:
                    pe.wait_ge(gelu, b * (2 * FB) + (2 * f - 2))
                for k in range(DC):
                    mm = product(psF[:, f % 2, 0:SEQ], w1, (slice(None), k, slice(f * P, (f + 1) * P)),
                                 h1_hi[:, k, :], h1_lo[:, k, :], k == 0, k == DC - 1)
                mm.then_inc(w1_mm, 1)

            def down(b, n, first):
                for k in range(FB):
                    if n == 0:
                        pe.wait_ge(g_lo_s, b * FB + k + 1)
                    mm = product(psG[:, n, 0:SEQ], w2, (slice(None), k, slice(n * P, (n + 1) * P)),
                                 g_hi[:, k, :], g_lo[:, k, :], k == 0, k == FB - 1)
                mm.then_inc(w2_mm, 1)

            def step(i):
                front, mid, tail, last, more = parts(i)
                f, m, t = i, i - 1, i - 2
                first = type(i) is int and i == 1
                if tail:
                    pe.wait_ge(r2, (t + 1) * DC)
                    if type(i) is not int or i >= 3:
                        pe.wait_ge(z_copied, t)
                    elif mid:
                        pe.wait_ge(h1n_ready, t + 2)
                    to_tokens(r2T).then_inc(t4, 1)
                if front:
                    pe.wait_ge(x_ready, f + 1)
                    if type(i) is not int or i >= 1:
                        pe.wait_ge(h1_copied, f * (2 * DC))
                    to_features(xn, psX).then_inc(t1, 1)
                if last:
                    pe.wait_ge(z_copied, t)
                    pe.wait_ge(r2, t * DC)
                    for k in range(DC):
                        mm = T.matmul(psG[0:NE, 0, 0:SEQ], gate_w[:, k, :], zT[:, k, bass.ds((t - 1) * SEQ, SEQ)],
                                      start=(k == 0), stop=(k == DC - 1))
                    mm.then_inc(lg_mm, 1)
                if mid:
                    pe.wait_ge(h1_lo_s, m + 1)
                    for k in range(3):
                        hidden(m, k, first)
                if front:
                    pe.wait_ge(x_split, f + 1)
                    if tail:
                        pe.wait_ge(n2_ready, t + 1)
                    elif mid:
                        pe.wait_ge(h1n_ready, f)
                    for n in range(DC):
                        for k in range(DC):
                            mm = product(psY[:, n, 0:SEQ], ret_w, (slice(None), k, slice(n * P, (n + 1) * P)),
                                         x_hi[:, k, :], x_lo[:, k, :], k == 0, k == DC - 1)
                    mm.then_inc(ret_mm, 1)
                if mid:
                    for k in range(3, FB):
                        hidden(m, k, first)
                if front:
                    pe.wait_ge(r_ready, f + 1)
                    to_tokens(ret).then_inc(t2, 1)
                if mid:
                    if last:
                        pe.wait_ge(lg_copied, t)
                    down(m, 0, first)
                    down(m, 1, first)
                if front:
                    pe.wait_ge(h1n_ready, f + 1)
                    to_features(h1n, psX).then_inc(t3, 1)
                if tail:
                    pe.wait_ge(z_ready, t + 1)
                    pe.wait_ge(n2_ready, t + 1)
                    to_features(zn, psY).then_inc(t5, 1)

            pe.wait_ge(half_b, 2)
            pe.wait_ge(consts[4], 16)
            pe.wait_ge(w_pool, 2)
            iterations(pe, step)


def moe_phase(nc, io, per, xs, eo, out):
    H, zT, LGT, ident, raw = per["H"], per["zT"], per["LGT"], per["ident"], per["raw"]
    rz, nmz = per["rz"], per["nmz"]
    with ExitStack() as ctx:
        sb = lambda name, shape, dt=F32: ctx.enter_context(nc.sbuf_tensor(name, shape, dt))
        sem = lambda name: ctx.enter_context(nc.semaphore(name))
        ps = lambda name, n: ctx.enter_context(nc.psum_tensor(name, [P, n, 512], F32))
        psGU, psX, psO = ps("psGU", 4), ps("psX2", 2), ps("psO", 2)
        rowsO = psO[:].rearrange("p a b -> p (a b)")

        NSH = (2 * DC * I_SH + SB * D)
        sh_w = [sb(f"sh_w{j}", [P, NSH], FR) for j in range(2)]
        NEX = (2 * DC * I_EXP + EB * D)
        ex_w = [[sb(f"ex_w{q}{j}", [P, NEX], FR) for j in range(2)] for q in range(2)]
        sh_raw, ex_raw = raw[:, 0:NSH], raw[:, NSH:NSH + NEX]

        xin = [sb(f"xin{q}", [XP, 2 * XT, D]) for q in range(2)]
        x_hi = sb("mx_hi", [P, DC, HALF], FR)
        x_lo = sb("mx_lo", [P, DC, HALF], FR)
        act_s = [sb(f"act_s{q}", [P, HALF]) for q in range(2)]
        act_a = [sb(f"act_a{q}", [P, HALF]) for q in range(2)]
        a_hi = sb("a_hi", [P, SB, HALF], FR)
        a_lo = sb("a_lo", [P, SB, HALF], FR)
        y_out = [sb(f"y_out{q}", [XP, XT, D]) for q in range(2)]
        ring = [sb(f"ring{q}", [P, TB, TOPK, D]) for q in range(2)]

        lg = sb("lg", [P, NT, NE])
        sc = sb("sc", [P, NT, NE])
        tmp = sb("r_tmp", [P, NT, NE])
        oh = [sb(f"oh{k}", [P, NT, NE]) for k in range(TOPK)]
        desc = sb("desc", [P, NT, NE])
        cnt = sb("cnt", [P, NT, NE], BF16)
        below = sb("below", [P, P], BF16)
        ones = sb("ones", [P, P], BF16)
        col = lambda name: sb(name, [P, NT])
        mx, sm, m1, m2, r1, r2_, den = (col(f"r_{n}") for n in ("mx", "sm", "m1", "m2", "r1", "r2", "den"))
        pos = [col(f"pos{k}") for k in range(TOPK)]
        keep = [col(f"keep{k}") for k in range(TOPK)]
        wgt = [col(f"wgt{k}") for k in range(TOPK)]
        slot_in = sb("slot_in", [P, TOPK, NT], U32)
        slot_out = sb("slot_out", [P, TOPK, NT], U32)

        sh_ready, ex_loaded = sem("sh_raw_loaded"), sem("ex_raw_loaded")
        sh_split, ex_hi, ex_lo = sem("sh_split"), sem("ex_hi"), sem("ex_lo")
        made, lg_t, route, r_exp, counted, prefix = (sem("made"), sem("lg_t"), sem("route"), sem("r_exp"),
                                                     sem("counted"), sem("prefix"))
        routed = sem("routed")
        z_tile = sem("z_tile")
        scat = [sem(f"scat{q}") for q in range(2)]
        s_hi, s_lo, s_mm, s_silu, s_a, s_ahi, s_alo, s_dn, s_add = (
            sem(f"s_{n}") for n in ("hi", "lo", "mm", "silu", "a", "ahi", "alo", "dn", "add"))
        e_load = [sem(f"e_load{q}") for q in range(2)]
        e_t, e_hi, e_lo, e_mm, e_silu, e_a, e_ahi, e_alo, e_dn, e_y = (
            sem(f"e_{n}") for n in ("t", "hi", "lo", "mm", "silu", "a", "ahi", "alo", "dn", "y"))
        e_store = [sem(f"e_store{q}") for q in range(2)]
        gath = [sem(f"gath{q}") for q in range(2)]
        comb = sem("comb")
        stored = sem("out_stored")
        block = ctx.enter_context(nc.Block())
        V, A, G, T = nc.vector, nc.scalar, nc.gpsimd, nc.tensor
        slots = [xs, eo]
        zs = slice(None)
        gate = lambda w, n: w[:, 0:DC * n].rearrange("p (k i) -> p k i", k=DC)
        up = lambda w, n: w[:, DC * n:2 * DC * n].rearrange("p (k i) -> p k i", k=DC)
        down = lambda w, n: w[:, 2 * DC * n:].rearrange("p (k d) -> p k d", d=D)
        Ht = lambda b, t: H[:, bass.ds(b * TB + t, 1), :].rearrange("p o d -> p (o d)")
        N_UNITS = 2 * NE
        xs_rows = xs.rearrange("(e t p) d -> e p t d", p=XP, t=2 * XT)
        eo_rows = eo.rearrange("(u t p) d -> u p t d", p=XP, t=XT)

        @block.sync
        def _(sp):
            def load_weights(e):
                if e >= 1:
                    sp.wait_ge(ex_lo, e)
                sp.dma_start(ex_raw, io["ex_w"][e]).then_inc(ex_loaded, 16)

            def load_tokens(e):
                if e >= 2:
                    sp.wait_ge(e_t, 2 * (e - 1))
                sp.dma_start(xin[e % 2][:], xs_rows[e]).then_inc(e_load[e % 2], 16)

            sp.dma_start(sh_raw, io["sh_w"]).then_inc(sh_ready, 16)
            load_weights(0)
            load_weights(1)
            for q in range(2):
                sp.wait_ge(scat[q], 16 * TB * TOPK * (B // 2))
            load_tokens(0)
            load_tokens(1)
            for e in range(2, NE):
                load_weights(e)
                load_tokens(e)
            for b in range(B):
                sp.wait_ge(comb, TB * TOPK * (b + 1))
                sp.dma_start(out[b].rearrange("(t p) d -> p t d", p=P), H[:, b * TB:(b + 1) * TB, :]).then_inc(stored, 16)
            sp.wait_ge(stored, 16 * B)

        @block.gpsimd
        def _(pool):
            G.memset(below[:], 1.0).then_inc(made, 1)
            G.memset(ones[:], 1.0).then_inc(made, 1)
            for e in range(NE):
                G.memset(desc[:, :, e:e + 1], float(NE - e)).then_inc(made, 1)
            pool.wait_ge(made, 1)
            G.affine_select(out=below[:], in_=below[:], compare_op=ALU.is_gt, fill=0.0, base=0,
                            pattern=[[1, P]], channel_multiplier=-1).then_inc(made, 1)
            pool.wait_ge(ex_hi, 1)
            G.tensor_tensor(ex_w[0][1][:], ex_raw, ex_w[0][0][:].bitcast(F32), ALU.subtract).then_inc(ex_lo, 1)
            pool.wait_ge(routed, 1)
            for b in range(B):
                pool.wait_ge(z_tile, b + 1)
                for t in range(TB):
                    for k in range(TOPK):
                        G.indirect_dma_start(
                            out=xs[:, :], out_offset=bass.IndirectOffsetOnAxis(ap=slot_in[:, k, b * TB + t:b * TB + t + 1], axis=0),
                            in_=ring[b % 2][:, t, 0, :], in_offset=None,
                            bounds_check=NE * CAP - 1, oob_is_err=False).then_inc(scat[b % 2], 16)
            for e in range(1, NE):
                pool.wait_ge(ex_hi, e + 1)
                G.tensor_tensor(ex_w[e % 2][1][:], ex_raw, ex_w[e % 2][0][:].bitcast(F32), ALU.subtract).then_inc(ex_lo, 1)
            for q in range(2):
                pool.wait_ge(e_store[q], 16 * (N_UNITS // 2))
            for b in range(B):
                if b >= 2:
                    pool.wait_ge(comb, TB * TOPK * (b - 1))
                for t in range(TB):
                    for k in range(TOPK):
                        G.indirect_dma_start(
                            out=ring[b % 2][:, t, k, :], out_offset=None,
                            in_=eo[:, :], in_offset=bass.IndirectOffsetOnAxis(ap=slot_out[:, k, b * TB + t:b * TB + t + 1], axis=0))\
                            .then_inc(gath[b % 2], 16)

        @block.vector
        def _(dve):
            n = [0]

            def link(ins):
                n[0] += 1
                ins.then_inc(route, 1)
                dve.wait_ge(route, n[0])

            bc = lambda x: x[:].unsqueeze(2).to_broadcast([P, NT, NE])
            dve.wait_ge(sh_split, 1)
            V.tensor_tensor(sh_w[1][:], sh_raw, sh_w[0][:].bitcast(F32), ALU.subtract).then_inc(sh_split, 1)
            dve.wait_ge(lg_t, 1)
            link(V.tensor_copy(lg[:].rearrange("p t e -> p (t e)"), psX[:, 0, 0:NT * NE]))
            link(V.tensor_reduce(mx[:], lg[:], AX.X, ALU.max))
            link(V.tensor_tensor(lg[:], lg[:], bc(mx), ALU.subtract))
            dve.wait_ge(r_exp, 1)
            link(V.tensor_reduce(sm[:], sc[:], AX.X, ALU.add))
            link(V.reciprocal(sm[:], sm[:]))
            link(V.tensor_tensor(sc[:], sc[:], bc(sm), ALU.mult))
            dve.wait_ge(made, 3 + NE)
            for k, (m, r) in enumerate(((m1, r1), (m2, r2_))):
                link(V.tensor_reduce(m[:], sc[:], AX.X, ALU.max))
                link(V.tensor_tensor(tmp[:], sc[:], bc(m), ALU.is_equal))
                link(V.tensor_tensor(tmp[:], tmp[:], desc[:], ALU.mult))
                link(V.tensor_reduce(r[:], tmp[:], AX.X, ALU.max))
                link(V.tensor_tensor(oh[k][:], tmp[:], bc(r), ALU.is_equal))
                if k == 0:
                    link(V.scalar_tensor_tensor(out=sc[:], in0=oh[0][:], scalar=-2.0, in1=sc[:], op0=ALU.mult, op1=ALU.add))
            V.tensor_tensor(cnt[:], oh[0][:], oh[1][:], ALU.add).then_inc(counted, 1)
            link(V.tensor_tensor(den[:], m1[:], m2[:], ALU.add))
            link(V.tensor_scalar(den[:], den[:], 1e-20, None, ALU.add))
            link(V.reciprocal(den[:], den[:]))
            dve.wait_ge(prefix, 1)
            for k, (m, r) in enumerate(((m1, r1), (m2, r2_))):
                link(V.tensor_tensor(tmp[:], oh[k][:], psX[:, 1, 0:NT * NE].rearrange("p (t e) -> p t e", e=NE), ALU.mult))
                link(V.tensor_reduce(pos[k][:], tmp[:], AX.X, ALU.add))
                link(V.tensor_scalar(keep[k][:], pos[k][:], float(CAP), None, ALU.is_lt))
                link(V.tensor_tensor(wgt[k][:], m[:], den[:], ALU.mult))
                link(V.tensor_tensor(wgt[k][:], wgt[k][:], keep[k][:], ALU.mult))
                link(V.scalar_tensor_tensor(out=pos[k][:], in0=r[:], scalar=-float(CAP), in1=pos[k][:], op0=ALU.mult, op1=ALU.add))
                link(V.tensor_scalar(pos[k][:], pos[k][:], float(NE * CAP), None, ALU.add))
                link(V.tensor_tensor(pos[k][:], pos[k][:], keep[k][:], ALU.mult))
                link(V.tensor_scalar(keep[k][:], keep[k][:], -float(OUT_OF_RANGE), float(OUT_OF_RANGE), ALU.mult, ALU.add))
                link(V.tensor_copy(slot_out[:, k, :], pos[k][:]))
                link(V.tensor_tensor(slot_in[:, k, :], pos[k][:], keep[k][:], ALU.add))
            dve.sem_inc(routed, 1)

            def low(x_sem, hi_sem, lo_sem, count, out, src, hi):
                dve.wait_ge(hi_sem, count)
                V.tensor_tensor(out, src, hi.bitcast(F32), ALU.subtract).then_inc(lo_sem, 1)

            def hidden(u, j, nb, w, silu, a_sem, ahi, alo):
                dve.wait_ge(silu, u * nb + (j + 1))
                V.tensor_tensor(act_a[j % 2][:, 0:w], act_s[j % 2][:, 0:w], psGU[:, 2 * (j % 2) + 1, 0:w], ALU.mult).then_inc(a_sem, 1)
                dve.wait_ge(a_sem, u * nb + (j + 1))
                V.tensor_copy(a_hi[:, j, 0:w], act_a[j % 2][:, 0:w]).then_inc(ahi, 1)
                dve.wait_ge(ahi, u * nb + (j + 1))
                V.tensor_tensor(a_lo[:, j, 0:w], act_a[j % 2][:, 0:w], a_hi[:, j, 0:w].bitcast(F32), ALU.subtract).then_inc(alo, 1)

            def shared(b):
                dve.wait_ge(s_hi, b + 1)
                V.tensor_tensor(x_lo[:, :, 0:SEQ], zT[:, :, bass.ds(b * SEQ, SEQ)], x_hi[:, :, 0:SEQ].bitcast(F32), ALU.subtract)\
                    .then_inc(s_lo, 1)
                for j in range(SB):
                    hidden(b, j, SB, SEQ, s_silu, s_a, s_ahi, s_alo)
                dve.wait_ge(s_dn, b + 1)
                for t in range(TB):
                    a = V.tensor_tensor(Ht(b, t), Ht(b, t), rowsO[:, t * D:(t + 1) * D], ALU.add)
                a.then_inc(s_add, 1)

            def x_low(u):
                dve.wait_ge(e_hi, u + 1)
                V.tensor_tensor(x_lo[:], psX[:, :, 0:HALF], x_hi[:].bitcast(F32), ALU.subtract).then_inc(e_lo, 1)

            def combine(b):
                dve.wait_ge(gath[b % 2], 16 * TB * TOPK * (b // 2 + 1))
                for k in range(TOPK):
                    if k:
                        dve.wait_ge(comb, TB * (TOPK * b + k))
                    for t in range(TB):
                        V.scalar_tensor_tensor(out=Ht(b, t), in0=ring[b % 2][:, t, k, :], scalar=wgt[k][:, b * TB + t:b * TB + t + 1],
                                               in1=Ht(b, t), op0=ALU.mult, op1=ALU.add).then_inc(comb, 1)

            for b in range(SH_FIRST):
                shared(b)
            for u in range(N_UNITS):
                x_low(u)
                for j in range(EB):
                    hidden(u, j, EB, HALF, e_silu, e_a, e_ahi, e_alo)
            for b in range(SH_FIRST, B):
                shared(b)
                dve.wait_ge(s_add, b + 1)
                if b == SH_FIRST:
                    pass
                combine(b - SH_FIRST)
            for b in range(SH_FIRST, B):
                combine(b)

        @block.scalar
        def _(act):
            act.wait_ge(sh_ready, 16)
            A.activation(sh_w[0][:], sh_raw, ACT.Copy).then_inc(sh_split, 1)

            def split_weights(e):
                act.wait_ge(ex_loaded, 16 * (e + 1))
                if e >= 2:
                    act.wait_ge(e_dn, 2 * (e - 1))
                A.activation(ex_w[e % 2][0][:], ex_raw, ACT.Copy).then_inc(ex_hi, 1)

            split_weights(0)
            act.wait_ge(route, 3)
            A.activation(sc[:], lg[:], ACT.Exp).then_inc(r_exp, 1)

            def z_of(b):
                if b >= 2:
                    act.wait_ge(scat[b % 2], 16 * TB * TOPK * (b // 2))
                for t in range(TB):
                    i = b * TB + t
                    a = A.activation(ring[b % 2][:, t, 0, :], H[:, i, :], ACT.Identity, bias=nmz[:, i:i + 1], scale=rz[:, i:i + 1])
                a.then_inc(z_tile, 1)

            def hidden(u, nb, w, mm, silu, a_sem, alo):
                for j in range(nb):
                    act.wait_ge(mm, u * nb + (j + 1))
                    if type(u) is not int or u * nb + j >= 2:
                        act.wait_ge(a_sem, u * nb + (j - 1))
                    A.activation(act_s[j % 2][:, 0:w], psGU[:, 2 * (j % 2), 0:w], ACT.Silu).then_inc(silu, 1)

            def shared(b):
                if b >= 1:
                    act.wait_ge(s_mm, b * SB)
                A.activation(x_hi[:, :, 0:SEQ], zT[:, :, bass.ds(b * SEQ, SEQ)], ACT.Copy).then_inc(s_hi, 1)
                hidden(b, SB, SEQ, s_mm, s_silu, s_a, s_alo)

            def x_high(u):
                act.wait_ge(e_t, u + 1)
                if u == 0:
                    act.wait_ge(s_mm, SH_FIRST * SB)
                    act.wait_ge(s_a, SH_FIRST * SB)
                else:
                    act.wait_ge(e_mm, u * EB)
                A.activation(x_hi[:], psX[:, :, 0:HALF], ACT.Copy).then_inc(e_hi, 1)

            def y_of(u):
                act.wait_ge(e_dn, u + 1)
                if u >= 2:
                    act.wait_ge(e_store[u % 2], 16 * (u // 2))
                A.activation(y_out[u % 2][:].rearrange("p t d -> p (t d)"), rowsO[0:XP, 0:XT * D], ACT.Copy).then_inc(e_y, 1)
                act.wait_ge(e_y, u + 1)
                act.dma_start(eo_rows[u], y_out[u % 2][:]).then_inc(e_store[u % 2], 16)

            z_of(0)
            z_of(1)
            for b in range(SH_FIRST):
                shared(b)
                z_of(b + 2)
            z_of(SH_FIRST + 2)
            z_of(SH_FIRST + 3)
            for u in range(N_UNITS):
                x_high(u)
                hidden(u, EB, HALF, e_mm, e_silu, e_a, e_alo)
                if u % 2 == 0 and u // 2 + 1 < NE:
                    split_weights(u // 2 + 1)
                y_of(u)
            act.wait_ge(e_mm, N_UNITS * EB)
            act.wait_ge(e_a, N_UNITS * EB)
            for b in range(SH_FIRST, B):
                shared(b)

        @block.tensor
        def _(pe):
            def product(out, w, at, hi, lo, first, last):
                T.matmul(out, w[0][at], hi, start=first, stop=False)
                T.matmul(out, w[0][at], lo, start=False, stop=False)
                return T.matmul(out, w[1][at], hi, start=False, stop=last)

            def hidden(u, nb, n, w, ws, mm_sem, a_sem):
                for j in range(nb):
                    if type(u) is not int or u * nb + j >= 2:
                        pe.wait_ge(a_sem, u * nb + (j - 1))
                    for o, part in ((0, gate), (1, up)):
                        wg = [part(x, n) for x in ws]
                        for k in range(DC):
                            mm = product(psGU[:, 2 * (j % 2) + o, 0:w], wg, (zs, k, slice(j * P, (j + 1) * P)),
                                         x_hi[:, k, 0:w], x_lo[:, k, 0:w], k == 0, k == DC - 1)
                    mm.then_inc(mm_sem, 1)

            def down_rows(u, nb, n, ws, tiles, rows, alo, dn):
                wd = [down(x, n) for x in ws]
                pe.wait_ge(alo, (u + 1) * nb)
                for t in range(tiles):
                    r = slice(t * rows, (t + 1) * rows)
                    o = rowsO[0:rows, t * D:(t + 1) * D]
                    for k in range(nb):
                        T.matmul(o, a_hi[:, k, r], wd[0][:, k, :], start=(k == 0), stop=False)
                        T.matmul(o, a_lo[:, k, r], wd[0][:, k, :], start=False, stop=False)
                        mm = T.matmul(o, a_hi[:, k, r], wd[1][:, k, :], start=False, stop=(k == nb - 1))
                mm.then_inc(dn, 1)

            def shared(b):
                pe.wait_ge(s_lo, b + 1)
                hidden(b, SB, I_SH, SEQ, sh_w, s_mm, s_a)
                if b >= 1:
                    pe.wait_ge(s_add, b)
                down_rows(b, SB, I_SH, sh_w, TB, P, s_alo, s_dn)

            for t in range(NT):
                mm = T.transpose(psX[:, 0, t * NE:(t + 1) * NE], LGT[0:NE, t * P:(t + 1) * P], ident[0:NE, 0:NE])
            mm.then_inc(lg_t, 1)
            pe.wait_ge(counted, 1)
            flat = cnt[:].rearrange("p t e -> p (t e)")
            T.matmul(psX[:, 1, 0:NT * NE], below[:], flat, start=True, stop=False)
            for t in range(NT - 1):
                mm = T.matmul(psX[:, 1, (t + 1) * NE:NT * NE], ones[:], cnt[:, t:t + 1, :].to_broadcast([P, NT - 1 - t, NE]),
                              start=False, stop=(t == NT - 2))
            mm.then_inc(prefix, 1)
            pe.wait_ge(sh_split, 2)
            for b in range(SH_FIRST):
                shared(b)

            def turn(u):
                e = u // 2
                if u % 2 == 0:
                    pe.wait_ge(e_load[e % 2], 16 * (e // 2 + 1))
                if u >= 1:
                    pe.wait_ge(e_lo, u)
                for t in range(XT):
                    for k in range(DC):
                        mm = T.transpose(psX[:, k, t * XP:(t + 1) * XP], xin[e % 2][:, (u % 2) * XT + t, k * P:(k + 1) * P],
                                         ident[0:XP, 0:XP])
                mm.then_inc(e_t, 1)

            turn(0)
            for u in range(N_UNITS):
                e = u // 2
                pe.wait_ge(e_lo, u + 1)
                if u % 2 == 0:
                    pe.wait_ge(ex_lo, e + 1)
                if u == 0:
                    pe.wait_ge(s_a, SH_FIRST * SB)
                hidden(u, EB, I_EXP, HALF, ex_w[e % 2], e_mm, e_a)
                if u + 1 < N_UNITS:
                    turn(u + 1)
                if u == 0:
                    pe.wait_ge(s_add, SH_FIRST)
                else:
                    pe.wait_ge(e_y, u)
                down_rows(u, EB, I_EXP, ex_w[e % 2], XT, XP, e_alo, e_dn)
            pe.wait_ge(e_y, N_UNITS)
            pe.wait_ge(e_a, N_UNITS * EB)
            for b in range(SH_FIRST, B):
                shared(b)


def fusion_program(nc, log_dt, inv_a, a_im, b_ri, c_ri, txt, raw_w, cols, b1, ln2_scale, ln2_bias, gate_w,
                   sh_w, ex_w, out):
    io = dict(log_dt=log_dt, inv_a=inv_a, a_im=a_im, b_ri=b_ri, c_ri=c_ri, txt=txt, raw_w=raw_w, cols=cols, b1=b1,
              ln2_scale=ln2_scale, ln2_bias=ln2_bias, gate_w=gate_w, sh_w=sh_w, ex_w=ex_w)
    scratch = nc.dram_tensor("ssm_kernel", (S_SSM, B, D), F32, kind="Internal").ap()
    xs = nc.dram_tensor("expert_rows", (NE * CAP, D), F32, kind="Internal").ap()
    eo = nc.dram_tensor("expert_out", (NE * CAP, D), F32, kind="Internal").ap()
    with ExitStack() as ctx:
        sb = lambda name, shape: ctx.enter_context(nc.sbuf_tensor(name, shape, F32))
        per = dict(ident=sb("ident", [P, P]), raw=sb("raw", [P, 4608]), H=sb("H", [P, NT, D]))
        ssm_phase(nc, io, scratch, per, xs)
        per.update(zT=sb("zT", [P, DC, TOK]), LGT=sb("LGT", [NE, TOK]), rz=sb("rz", [P, NT]), nmz=sb("nmz", [P, NT]))
        attn_phase(nc, io, scratch, per)
        moe_phase(nc, io, per, xs, eo, out)


def _half(a):
    return a.reshape(2, HP, N_STATE).transpose(0, 2, 1).reshape(P, HP)


def _blocks(w):
    return w.reshape(-1, P, w.shape[-1]).transpose(1, 0, 2).reshape(P, -1)


def kernel(**inputs):
    import numpy as np
    import concourse.bacc as bacc
    from concourse.bass_utils import run_bass_kernel_spmd

    a = {k: np.asarray(v) for k, v in inputs.items()}
    tok = lambda n: a["L0_tok_" + n]
    att = lambda n: a["L0_attn_" + n]
    ffn = lambda n: a["L0_ffn_" + n]
    column = lambda v: v.reshape(-1, P).T
    swiglu = lambda g, u, d: np.concatenate([_blocks(g.T), _blocks(u.T), _blocks(d.T)], 1)
    laid = dict(
        log_dt=tok("log_dt")[None],
        inv_a=_half(tok("inv_A_real")),
        a_im=_half(tok("A_imag")),
        b_ri=np.stack([_half(tok("B_ri")[..., i]) for i in range(2)]),
        c_ri=a["x"].reshape(B, 2, HP, N_STATE, 2).transpose(1, 3, 4, 2, 0).reshape(P, 2, HP, B),
        txt=a["txt"],
        raw_w=np.concatenate([_blocks(att(n)) for n in ("W_ret", "W1", "W2")], 1),
        cols=np.stack([column(att(n)) for n in ("b_ret", "ln1_scale", "ln1_bias", "b2")], 1),
        b1=column(att("b1")),
        ln2_scale=att("ln2_scale")[None],
        ln2_bias=att("ln2_bias")[None],
        gate_w=_blocks(ffn("gate_w").T).reshape(P, DC, NE),
        sh_w=swiglu(ffn("ws_gate"), ffn("ws_up"), ffn("ws_down")),
        ex_w=np.stack([swiglu(ffn("we_gate")[e], ffn("we_up")[e], ffn("we_down")[e]) for e in range(NE)]),
    )
    nc = bacc.Bacc("TRN2", target_bir_lowering=False, num_devices=1)
    arrays, args = {}, []
    for name, v in laid.items():
        v = np.ascontiguousarray(v)
        arrays[f"in_{name}"] = v
        args.append(nc.dram_tensor(f"in_{name}", v.shape, mybir.dt.from_np(v.dtype), kind="ExternalInput").ap())
    args.append(nc.dram_tensor("out_0", (B, SEQ, D), F32, kind="ExternalOutput").ap())
    fusion_program(nc, *args)
    r = run_bass_kernel_spmd(nc, [arrays], core_ids=[0])
    return r.results[0]["out_0"]
```

```python
from contextlib import ExitStack
import math

import concourse.bass as bass
from concourse import mybir

ALU = mybir.AluOpType
ACT = mybir.ActivationFunctionType
AX = mybir.AxisListType
F32 = mybir.dt.float32
FR = mybir.dt.float32r
BF16 = mybir.dt.bfloat16
I32 = mybir.dt.int32
U32 = mybir.dt.uint32
P = 128

B, S_SSM, N_STATE = 8, 256, 64
S_TXT, D = 128, 256
SEQ = S_SSM + S_TXT
TB = SEQ // P
NT = B * TB
DC = D // P

NA, NB = 4, 64
HP = S_SSM // 2
HC = 16
NCHUNK = HP // HC
POOL_CHUNKS = 2
CA = B * NA

F_ATT = 1024
FB = F_ATT // P
NE = 8
EPS = 1e-5
RSQRT_SEED = float(0xdf3759df)

TOK = B * SEQ
TOPK = 2
CAP = math.ceil(1.25 * TOK * TOPK / NE)
HALF = CAP // 2
XP = 120
XT = HALF // XP
I_EXP, I_SH = 256, 512
EB, SB = I_EXP // P, I_SH // P
OUT_OF_RANGE = 1 << 17
UNITS = 2 * NE
W_EX = 2 * DC * I_EXP + EB * D
W_SH = 2 * DC * I_SH + SB * D
SH_FIRST = 4
ZERO_PARTS = 10
assert XT * XP == HALF and 2 * HALF == CAP


def ssm_phase(nc, io, scratch, per, xs):
    with ExitStack() as ctx:
        sb = lambda name, shape, dt=F32: ctx.enter_context(nc.sbuf_tensor(name, shape, dt))
        sem = lambda name: ctx.enter_context(nc.semaphore(name))
        dt_bc = sb("dt_bc", [P, HP])
        inv_a = sb("inv_a", [P, HP])
        a_im = sb("a_im", [P, HP])
        b_re = sb("b_re", [P, HP])
        b_im = sb("b_im", [P, HP])
        c_in = sb("c_in", [P, 2, HP, B])
        u = sb("u", [P, HP])
        v = sb("v", [P, HP])
        s1 = sb("s1", [P, HP])
        s2 = sb("s2", [P, HP])
        s3 = sb("s3", [P, HP])
        s4 = sb("s4", [P, HP])
        pw_re = sb("pw_re", [P, HP, NB + 1])
        pw_im = sb("pw_im", [P, HP, NB + 1])
        w_re = sb("w_re", [P, HP, NA])
        w_im = sb("w_im", [P, HP, NA])
        g_re = sb("g_re", [P, HP, B])
        g_im = sb("g_im", [P, HP, B])
        gn_re = sb("gn_re", [P, HP, B])
        gn_im = sb("gn_im", [P, HP, B])
        l_re = sb("l_re", [P, HP, B, NA])
        l_im = sb("l_im", [P, HP, B, NA])
        tv = [sb(f"tv{j}", [P, HP * 8]) for j in range(4)]
        tp = [sb(f"tp{j}", [P, HC * 32]) for j in range(4)]
        k_out = sb("k_out", [P, 2, 2, HC * NB // 4])
        psK = ctx.enter_context(nc.psum_tensor("psK", [P, 2, 4, 512], F32))

        ident, raw = per["ident"], per["raw"]
        zero = sb("zero", [P, NE * CAP * D // P // ZERO_PARTS])

        raw_loaded, zero_made, zeroed = sem("raw_loaded"), sem("zero_made"), sem("zeroed")
        ident_made = sem("ident_made")
        loads = [sem(f"ssm_load{j}") for j in range(6)]
        exps = sem("exps")
        base = sem("base")
        dve_c = sem("dve_chain")
        pool_c = sem("pool_chain")
        tab = [sem(f"tables{k}") for k in range(NCHUNK)]
        summed = sem("summed")
        evac = sem("evac")
        stored = [sem(f"k_stored{q}") for q in range(2)]
        block = ctx.enter_context(nc.Block())

        def cmul(eng, link, wait, tmp, ore, oim, are, aim, bre, bim):
            t = tmp
            link(eng.tensor_tensor(t[0], are, bre, ALU.mult))
            link(eng.tensor_tensor(t[1], aim, bim, ALU.mult))
            link(eng.tensor_tensor(t[2], are, bim, ALU.mult))
            link(eng.tensor_tensor(t[3], aim, bre, ALU.mult))
            wait()
            link(eng.tensor_tensor(ore, t[0], t[1], ALU.subtract))
            link(eng.tensor_tensor(oim, t[2], t[3], ALU.add))
            wait()

        def powers(eng, link, wait, tmp, h, k, n):
            tt = [x[:, 0:n * k].rearrange("p (h k) -> p h k", h=n) for x in tmp]
            cre = pw_re[:, h, k:k + 1].to_broadcast([P, n, k])
            cim = pw_im[:, h, k:k + 1].to_broadcast([P, n, k])
            cmul(eng, link, wait, tt, pw_re[:, h, k + 1:2 * k + 1], pw_im[:, h, k + 1:2 * k + 1],
                 pw_re[:, h, 1:k + 1], pw_im[:, h, 1:k + 1], cre, cim)

        def tables(eng, link, wait, tmp, k):
            h = slice(k * HC, (k + 1) * HC)
            for w in (8, 16, 32):
                powers(eng, link, wait, tmp, h, w, HC)
            s = [x[:, 0:HC].rearrange("p (h k) -> p h k", k=1) for x in tmp]
            one, two, three = slice(1, 2), slice(2, 3), slice(3, 4)
            link(eng.tensor_copy(w_re[:, h, one], pw_re[:, h, NB:NB + 1]))
            link(eng.tensor_copy(w_im[:, h, one], pw_im[:, h, NB:NB + 1]))
            wait()
            cmul(eng, link, wait, s, w_re[:, h, two], w_im[:, h, two], w_re[:, h, one], w_im[:, h, one],
                 w_re[:, h, one], w_im[:, h, one])
            cmul(eng, link, wait, s, w_re[:, h, three], w_im[:, h, three], w_re[:, h, two], w_im[:, h, two],
                 w_re[:, h, one], w_im[:, h, one])
            t4 = [x[:, 0:HC * 32].rearrange("p (h c a) -> p h c a", h=HC, c=B) for x in tmp]
            gb = lambda g: g[:, h, :].unsqueeze(3).to_broadcast([P, HC, B, NA])
            wb = lambda w: w[:, h, :].unsqueeze(2).to_broadcast([P, HC, B, NA])
            link(eng.tensor_tensor(t4[0], gb(g_re), wb(w_re), ALU.mult))
            link(eng.tensor_tensor(t4[1], gb(g_im), wb(w_im), ALU.mult))
            link(eng.tensor_tensor(t4[2], gb(gn_re), wb(w_im), ALU.mult))
            link(eng.tensor_tensor(t4[3], gb(gn_im), wb(w_re), ALU.mult))
            wait()
            eng.tensor_tensor(l_re[:, h], t4[0], t4[1], ALU.subtract).then_inc(tab[k], 1)
            link(eng.tensor_tensor(l_im[:, h], t4[2], t4[3], ALU.add))
            wait()

        @block.sync
        def _(sp):
            sp.dma_start(dt_bc[0:64, :], io["log_dt"][0:1, 0:HP].to_broadcast([64, HP])).then_inc(loads[0], 16)
            sp.dma_start(dt_bc[64:128, :], io["log_dt"][0:1, HP:2 * HP].to_broadcast([64, HP])).then_inc(loads[0], 16)
            sp.dma_start(inv_a[:], io["inv_a"]).then_inc(loads[1], 16)
            sp.dma_start(a_im[:], io["a_im"]).then_inc(loads[2], 16)
            sp.dma_start(b_re[:], io["b_ri"][0]).then_inc(loads[3], 16)
            sp.dma_start(b_im[:], io["b_ri"][1]).then_inc(loads[4], 16)
            sp.dma_start(c_in[:], io["c_ri"].rearrange("p r h c -> p (r h c)")).then_inc(loads[5], 16)
            sp.dma_start(raw[:], io["raw_w"]).then_inc(raw_loaded, 16)
            sp.wait_ge(zero_made, 1)
            xs_flat = xs.rearrange("(p r) d -> p (r d)", p=P)
            w = xs_flat.shape[1] // ZERO_PARTS
            for j in range(ZERO_PARTS):
                sp.dma_start(xs_flat[:, j * w:(j + 1) * w], zero[:]).then_inc(zeroed, 16)
            for k in range(NCHUNK):
                sp.wait_ge(evac, 2 * (k + 1))
                for half in range(2):
                    h0 = half * HP + k * HC
                    dst = scratch[h0:h0 + HC].rearrange("(g j) c (a b) -> (j c a) g b", j=4, b=NB)
                    sp.dma_start(dst, k_out[:, k % 2, half, :].rearrange("p (g b) -> p g b", b=NB)).then_inc(stored[k % 2], 16)
            for q in range(2):
                sp.wait_ge(stored[q], 16 * NCHUNK)
            sp.wait_ge(raw_loaded, 16)
            sp.wait_ge(zeroed, 16 * ZERO_PARTS)

        @block.scalar
        def _(act):
            act.wait_ge(loads[0], 32)
            nc.scalar.activation(dt_bc[:], dt_bc[:], ACT.Exp).then_inc(exps, 1)
            act.wait_ge(loads[1], 16)
            nc.scalar.activation(inv_a[:], inv_a[:], ACT.Exp).then_inc(exps, 1)
            for k in range(NCHUNK):
                for half in range(2):
                    act.wait_ge(summed, 2 * k + half + 1)
                    if k >= 2:
                        act.wait_ge(stored[k % 2], 32 * (k // 2))
                    nc.scalar.activation(k_out[:, k % 2, half, :], psK[:, half, k % 4, 0:HC * NB // 4], ACT.Copy).then_inc(evac, 1)

        @block.vector
        def _(dve):
            n = [0]

            def link(ins):
                n[0] += 1
                ins.then_inc(dve_c, 1)

            def wait():
                dve.wait_ge(dve_c, n[0])

            V = nc.vector
            link(V.memset(pw_re[:, :, 0:1], 1.0))
            link(V.memset(pw_im[:, :, 0:1], 0.0))
            link(V.memset(w_re[:, :, 0:1], 1.0))
            link(V.memset(w_im[:, :, 0:1], 0.0))
            dve.wait_ge(exps, 2)
            dve.wait_ge(loads[2], 16)
            link(V.scalar_tensor_tensor(out=u[:], in0=inv_a[:], scalar=-0.5, in1=dt_bc[:], op0=ALU.mult, op1=ALU.mult))
            link(V.scalar_tensor_tensor(out=v[:], in0=a_im[:], scalar=0.5, in1=dt_bc[:], op0=ALU.mult, op1=ALU.mult))
            wait()
            link(V.tensor_tensor(s1[:], u[:], u[:], ALU.mult))
            link(V.tensor_tensor(s2[:], v[:], v[:], ALU.mult))
            link(V.tensor_scalar(s3[:], u[:], -1.0, 1.0, ALU.mult, ALU.add))
            wait()
            link(V.tensor_tensor(s1[:], s1[:], s2[:], ALU.add))
            link(V.tensor_tensor(s4[:], s3[:], s3[:], ALU.mult))
            wait()
            link(V.tensor_tensor(s4[:], s4[:], s2[:], ALU.add))
            link(V.tensor_scalar(s1[:], s1[:], -1.0, 1.0, ALU.mult, ALU.add))
            wait()
            link(V.reciprocal(s4[:], s4[:]))
            wait()
            one = lambda x: x[:].unsqueeze(2)
            link(V.tensor_tensor(pw_re[:, :, 1:2], one(s1), one(s4), ALU.mult))
            link(V.scalar_tensor_tensor(out=pw_im[:, :, 1:2], in0=one(v), scalar=2.0, in1=one(s4), op0=ALU.mult, op1=ALU.mult))
            for j in range(3, 6):
                dve.wait_ge(loads[j], 16)
            link(V.tensor_scalar(b_re[:], b_re[:], 2.0, None, ALU.mult))
            link(V.tensor_scalar(b_im[:], b_im[:], 2.0, None, ALU.mult))
            wait()
            bb = lambda x: x[:].unsqueeze(2).to_broadcast([P, HP, B])
            t8 = [x[:].rearrange("p (h c) -> p h c", c=B) for x in tv]
            cmul(V, link, wait, t8, g_re[:], g_im[:], c_in[:, 0], c_in[:, 1], bb(b_re), bb(b_im))
            link(V.tensor_scalar(gn_re[:], g_re[:], -1.0, None, ALU.mult))
            link(V.tensor_scalar(gn_im[:], g_im[:], -1.0, None, ALU.mult))
            for k in (1, 2, 4):
                powers(V, link, wait, tv, slice(0, HP), k, HP)
            dve.sem_inc(base, 1)
            for k in range(NCHUNK - POOL_CHUNKS):
                tables(V, link, wait, tv, k)
                dve.sem_inc(tab[k], 1)

        @block.gpsimd
        def _(pool):
            n = [0]

            def link(ins):
                n[0] += 1
                ins.then_inc(pool_c, 1)

            def wait():
                pool.wait_ge(pool_c, n[0])

            nc.gpsimd.memset(zero[:], 0.0).then_inc(zero_made, 1)
            nc.gpsimd.memset(ident[:], 0.0).then_inc(ident_made, 1)
            pool.wait_ge(ident_made, 1)
            nc.gpsimd.affine_select(out=ident[:], in_=ident[:], compare_op=ALU.not_equal, fill=1.0, base=0,
                                    pattern=[[-1, P]], channel_multiplier=1).then_inc(ident_made, 1)
            pool.wait_ge(base, 1)
            for k in range(NCHUNK - POOL_CHUNKS, NCHUNK):
                tables(nc.gpsimd, link, wait, tp, k)
                pool.sem_inc(tab[k], 1)

        @block.tensor
        def _(pe):
            for k in range(NCHUNK):
                pe.wait_ge(tab[k], 2)
                if k >= 4:
                    pe.wait_ge(evac, 2 * (k - 3))
                for half in range(2):
                    r = slice(64 * half, 64 * half + 64)
                    for i in range(HC):
                        h, j, g = k * HC + i, i % 4, i // 4
                        out = psK[32 * j:32 * j + 32, half, k % 4, g * NB:(g + 1) * NB]
                        pe.matmul(out, l_re[r, h].rearrange("p c a -> p (c a)"), pw_re[r, h, 0:NB],
                                  start=True, stop=False)
                        mm = pe.matmul(out, l_im[r, h].rearrange("p c a -> p (c a)"), pw_im[r, h, 0:NB],
                                       start=False, stop=True)
                    mm.then_inc(summed, 1)


def ln_stats(V, dve, sem, seen, tiles, st, mv, rstd, nmr, fillers=()):
    n = len(tiles)
    fillers = list(fillers)
    rstd, nmr = rstd[:, 0:n], nmr[:, 0:n]
    diff, total, sq, var, half = (mv[:, j, 0:n] for j in range(5))
    mean_e, sq_e, mean_o, sq_o = (st[:, 0:n, j] for j in (1, 2, 4, 5))
    for j, x in enumerate(tiles):
        V.bn_stats(st[:, j, :], x).then_inc(sem, 1)

    def after_last(k):
        if fillers:
            fillers.pop(0)()
        dve.wait_ge(sem, seen + k)

    after_last(n)
    V.tensor_tensor(diff, mean_e, mean_o, ALU.subtract).then_inc(sem, 1)
    V.tensor_tensor(total, mean_e, mean_o, ALU.add).then_inc(sem, 1)
    V.tensor_tensor(sq, sq_e, sq_o, ALU.add).then_inc(sem, 1)
    after_last(n + 3)
    V.scalar_tensor_tensor(out=diff, in0=diff, scalar=0.25, in1=diff, op0=ALU.mult, op1=ALU.mult).then_inc(sem, 1)
    V.tensor_scalar(sq, sq, 1.0 / D, EPS, ALU.mult, ALU.add).then_inc(sem, 1)
    k = n + 5
    after_last(k)
    V.tensor_tensor(var, sq, diff, ALU.add).then_inc(sem, 1)
    after_last(k + 1)
    V.tensor_scalar(half.bitcast(I32), var.bitcast(I32), 1, None, ALU.logical_shift_right).then_inc(sem, 1)
    after_last(k + 2)
    V.tensor_scalar(rstd.bitcast(U32), half.bitcast(I32), -1.0, RSQRT_SEED, ALU.mult, ALU.add).then_inc(sem, 1)
    k += 3
    for _ in range(3):
        after_last(k)
        V.scalar_tensor_tensor(out=half, in0=rstd, scalar=0.5, in1=rstd, op0=ALU.mult, op1=ALU.mult).then_inc(sem, 1)
        after_last(k + 1)
        V.tensor_tensor(half, half, var, ALU.mult).then_inc(sem, 1)
        after_last(k + 2)
        V.scalar_tensor_tensor(out=rstd, in0=half, scalar=1.5, in1=rstd, op0=ALU.subtract, op1=ALU.mult).then_inc(sem, 1)
        k += 3
    after_last(k)
    V.scalar_tensor_tensor(out=nmr, in0=total, scalar=-0.5, in1=rstd, op0=ALU.mult, op1=ALU.mult).then_inc(sem, 1)
    assert k + 1 == ln_signals(n) and not fillers


def ln_signals(n):
    return n + 18


FILL_B, LOWS_MID, SPLIT_T3, W1_T2 = 0, 4, 7, 4
ONE, TWO = ln_signals(TB), ln_signals(2 * TB)


def attn_phase(nc, io, scratch, per):
    H, zT, ident, gate_w = per["H"], per["zT"], per["ident"], per["gate_w"]
    rz, nmz, lg_rows = per["rz"], per["nmz"], per["lg_rows"]
    with ExitStack() as ctx:
        sb = lambda name, shape, dt=F32: ctx.enter_context(nc.sbuf_tensor(name, shape, dt))
        sem = lambda name: ctx.enter_context(nc.semaphore(name))
        raw = per["raw"]
        ret_raw, w1_raw, w2_raw = (raw[:, a:b].rearrange("p (k n) -> p k n", n=n)
                                   for a, b, n in ((0, 512, D), (512, 2560, F_ATT), (2560, 4608, D)))
        ret_w = [sb(f"ret_w{j}", [P, DC, D], FR) for j in range(2)]
        w1 = [sb(f"w1_{j}", [P, DC, F_ATT], FR) for j in range(2)]
        w2 = [sb(f"w2_{j}", [P, FB, D], FR) for j in range(2)]
        cols = sb("cols", [P, 5, DC])
        b1 = sb("b1", [P, FB])
        ln2s = sb("ln2s", [P, D])
        ln2b = sb("ln2b", [P, D])
        halves = sb("halves", [P, SEQ])
        primer = sb("primer", [1, 1])
        xn = sb("xn", [P, TB, D])
        xT = sb("xT", [P, DC, SEQ])
        x_hi = sb("x_hi", [P, DC, SEQ], FR)
        x_lo = sb("x_lo", [P, DC, SEQ], FR)
        th = sb("th", [P, DC, SEQ])
        ret = sb("ret", [P, DC, SEQ])
        h1n = sb("h1n", [P, TB, D])
        h1T = [sb(f"h1T{q}", [P, DC, SEQ]) for q in range(2)]
        h1_hi = sb("h1_hi", [P, DC, SEQ], FR)
        h1_lo = sb("h1_lo", [P, DC, SEQ], FR)
        NG = 6
        g = [sb(f"g{j}", [P, SEQ]) for j in range(NG)]
        g_hi = sb("g_hi", [P, FB, SEQ], FR)
        g_lo = sb("g_lo", [P, FB, SEQ], FR)
        r2T = sb("r2T", [P, DC, SEQ])
        n2 = sb("n2", [P, TB, D])
        zn = sb("zn", [P, TB, D])
        lg_feat = sb("lg_feat", [NE, SEQ])
        st = [sb(f"st{j}", [P, 2 * TB, 6]) for j in range(2)]
        mv = [sb(f"mv{j}", [P, 5, 2 * TB]) for j in range(2)]
        rs = [sb(f"rs{j}", [P, 2 * TB]) for j in range(2)]
        nm = [sb(f"nm{j}", [P, 2 * TB]) for j in range(2)]

        pm = lambda name: ctx.enter_context(nc.psum_tensor(name, [P, 2, 512], F32))
        psX, psY, psF, psG = pm("psX"), pm("psY"), pm("psF"), pm("psG")
        rowsY = psY[:].rearrange("p a b -> p (a b)")
        tokY = [rowsY[:, D * t:D * (t + 1)] for t in range(TB)]
        X = psX[:, :, 0:SEQ]
        Y = psY[:, :, 0:SEQ]
        LG = psG[:, 0, 0:TB * NE].rearrange("p (t e) -> p t e", e=NE)

        consts = [sem(f"const{j}") for j in range(9)]
        h_loaded = sem("h_loaded")
        next_loaded = sem("next_loaded")
        w_split = sem("w_split")
        w_pool = sem("w_pool")
        half_b = sem("half_b")
        ln_a, ln_b, kept = sem("ln_a"), sem("ln_b"), sem("kept")
        x_ready, t1, x_copied, x_split = sem("x_ready"), sem("t1"), sem("x_copied"), sem("x_split")
        ret_mm, tanh_done, scan, r_ready = sem("ret_mm"), sem("tanh_done"), sem("scan"), sem("r_ready")
        t2, h1n_ready, t3, h1_copied = sem("t2"), sem("h1n_ready"), sem("t3"), sem("h1_copied")
        h1_hi_s, h1_lo_s = sem("h1_hi_s"), sem("h1_lo_s")
        w1_mm, gelu, g_hi_s, g_lo_s = sem("w1_mm"), sem("gelu"), sem("g_hi_s"), sem("g_lo_s")
        w2_mm, r2, t4, n2_ready = sem("w2_mm"), sem("r2"), sem("t4"), sem("n2_ready")
        n2_scaled, h_biased, h_new = sem("n2_scaled"), sem("h_biased"), sem("h_new")
        z_ready, t5, z_copied = sem("z_ready"), sem("t5"), sem("z_copied")
        lg_mm, lg_copied, lg_turned, lg_kept = sem("lg_mm"), sem("lg_copied"), sem("lg_turned"), sem("lg_kept")
        block = ctx.enter_context(nc.Block())
        V, A, G, T = nc.vector, nc.scalar, nc.gpsimd, nc.tensor

        Ht = lambda b, t: H[:, bass.ds(b * TB + t, 1), :].rearrange("p o d -> p (o d)")
        Hb = lambda b: H[:, bass.ds(b * TB, TB), :]

        slice_of = lambda x, b: x[:, bass.ds(b * TB, TB)]

        def iterations(eng, step):
            step(0, 0), step(1, 1), step(2, 0)
            with eng.Fori(0, (B - 4) // 2) as pair:
                step(pair * 2 + 3, 1)
                step(pair * 2 + 4, 0)
            for i in range(B - 1, B + 3):
                step(i, i % 2)

        def parts(i):
            if type(i) is not int:
                return (True,) * 5
            return tuple(0 <= i + d < B for d in (0, -1, -2, -3, 1))

        def signals_a(i):
            if type(i) is not int:
                return i * TWO + (2 * ONE - 2 * TWO)
            return sum(ln_signals(TB * (parts(j)[0] + parts(j)[2])) if parts(j)[0] or parts(j)[2] else 0
                       for j in range(i))

        def signals_b(i):
            if type(i) is not int:
                return i * TWO + (3 * ONE - 2 * TWO)
            return ONE + sum(ln_signals(TB * (parts(j)[4] + parts(j)[2])) if parts(j)[4] or parts(j)[2] else 0
                             for j in range(i))

        @block.sync
        def _(sp):
            sp.dma_start(ln2s[:], io["ln2_scale"].to_broadcast([P, D])).then_inc(consts[0], 16)
            for b in range(B):
                for t in range(S_SSM // P):
                    sp.dma_start(H[:, b * TB + t, :], scratch[t * P:(t + 1) * P, b, :]).then_inc(h_loaded, 16)
                sp.dma_start(H[:, b * TB + TB - 1, :], io["txt"][b]).then_inc(h_loaded, 16)
                sp.wait_ge(h_loaded, 16 * TB * (b + 1))
                if b == 0:
                    sp.dma_start(ln2b[:], io["ln2_bias"].to_broadcast([P, D])).then_inc(consts[1], 16)
            sp.wait_ge(w_split, 3)
            sp.wait_ge(half_b, 2)
            sp.wait_ge(w_pool, 2)
            sp.dma_start(raw[:, 0:W_SH], io["sh_w"]).then_inc(next_loaded, 16)
            sp.dma_start(raw[:, W_SH:W_SH + W_EX], io["ex_w"][0]).then_inc(next_loaded, 16)
            sp.wait_ge(next_loaded, 32)

        @block.gpsimd
        def _(pool):
            G.memset(halves[:], 0.5).then_inc(w_pool, 1)
            pool.wait_ge(w_split, 3)
            G.tensor_tensor(w2[1][:], w2_raw, w2[0][:].bitcast(F32), ALU.subtract).then_inc(w_pool, 1)
            pool.wait_ge(consts[0], 16)
            pool.wait_ge(consts[1], 16)

            def step(i, q):
                front, mid, tail, last, more = parts(i)
                f, m, t = i, i - 1, i - 2
                if front:
                    pool.wait_ge(x_ready, f + 1)
                    pool.wait_ge(consts[1], 16)
                    G.tensor_tensor(Hb(f), Hb(f), ln2b[:].unsqueeze(1).to_broadcast([P, TB, D]), ALU.add)\
                        .then_inc(h_biased, 1)
                if tail:
                    pool.wait_ge(n2_ready, t + 1)
                    G.tensor_tensor(n2[:], n2[:], ln2s[:].unsqueeze(1).to_broadcast([P, TB, D]), ALU.mult)\
                        .then_inc(n2_scaled, 1)

            iterations(pool, step)

        @block.vector
        def _(dve):
            dve.wait_ge(w_split, 1)
            V.tensor_tensor(ret_w[1][:], ret_raw, ret_w[0][:].bitcast(F32), ALU.subtract).then_inc(half_b, 1)
            dve.wait_ge(w_split, 2)
            V.tensor_tensor(w1[1][:], w1_raw, w1[0][:].bitcast(F32), ALU.subtract).then_inc(half_b, 1)
            dve.wait_ge(consts[2], 16)
            V.tensor_scalar(cols[:, 4, :], cols[:, 0, :], 0.5, None, ALU.mult).then_inc(half_b, 1)

            def g_low(b, f):
                dve.wait_ge(gelu, b * (2 * FB) + (2 * f + 2))
                V.tensor_tensor(g_lo[:, f, :], g[f % NG][:], g_hi[:, f, :].bitcast(F32), ALU.subtract)\
                    .then_inc(g_lo_s, 1)

            def residual(b, q, k):
                dve.wait_ge(w2_mm, b * DC + k + 1)
                V.scalar_tensor_tensor(out=r2T[:, k, :], in0=psG[:, k, 0:SEQ], scalar=cols[:, 3, k:k + 1],
                                       in1=h1T[q][:, k, :], op0=ALU.add, op1=ALU.add).then_inc(r2, 1)

            def x_low(b):
                dve.wait_ge(x_copied, (b + 1) * 2)
                V.tensor_tensor(x_lo[:], X, x_hi[:].bitcast(F32), ALU.subtract).then_inc(x_split, 1)

            def h1_low(b, q, k):
                dve.wait_ge(h1_copied, b * (2 * DC) + (2 * k + 2))
                V.tensor_tensor(h1_lo[:, k, :], h1T[q][:, k, :], h1_hi[:, k, :].bitcast(F32), ALU.subtract).then_inc(h1_lo_s, 1)

            def step(i, q):
                front, mid, tail, last, more = parts(i)
                f, m, t = i, i - 1, i - 2
                lows = [lambda k=k: g_low(m, k) for k in range(FB)] if mid else []
                take = lambda n: [lows.pop(0) for _ in range(n if mid else 0)]
                if tail or more:
                    tiles = []
                    if tail:
                        dve.wait_ge(t4, t + 1)
                        tiles += tokY
                    if more:
                        dve.wait_ge(h_loaded, (f + 2) * (16 * TB))
                        tiles += [Ht(f + 1, j) for j in range(TB)]
                    ln_stats(V, dve, ln_b, signals_b(i), tiles, st[1], mv[1], rs[1], nm[1], take(FILL_B))
                if front:
                    for k in range(DC):
                        dve.wait_ge(tanh_done, f * DC + (k + 1))
                        V.tensor_tensor_scan(ret[:, k, :], halves[:], th[:, k, :], -2.0, ALU.mult, ALU.add).then_inc(scan, 1)
                    dve.wait_ge(scan, (f + 1) * DC)
                    V.scalar_tensor_tensor(out=ret[:], in0=ret[:], scalar=0.25, in1=xT[:], op0=ALU.mult, op1=ALU.add)\
                        .then_inc(r_ready, 1)
                for low in take(LOWS_MID):
                    low()
                if tail:
                    dve.wait_ge(n2_scaled, t + 1)
                    dve.wait_ge(h_biased, t + 1)
                    V.tensor_tensor(Hb(t), Hb(t), n2[:], ALU.add).then_inc(h_new, 1)
                if front or tail:
                    tiles = []
                    if front:
                        dve.wait_ge(t2, f + 1)
                        tiles += tokY
                    if tail:
                        tiles += [Ht(t, j) for j in range(TB)]
                        dve.wait_ge(w_pool, 1)
                        dve.wait_ge(h_new, t + 1)
                    ln_stats(V, dve, ln_a, signals_a(i), tiles, st[0], mv[0], rs[0], nm[0], take(len(lows)))
                else:
                    for low in take(len(lows)):
                        low()
                if more:
                    x_low(f + 1)
                if mid:
                    residual(m, 1 - q, 0)
                if tail:
                    o = TB if front else 0
                    dve.wait_ge(ln_a, signals_a(i) + (TWO if front else ONE))
                    V.tensor_copy(slice_of(rz, t), rs[0][:, o:o + TB])
                    V.tensor_copy(slice_of(nmz, t), nm[0][:, o:o + TB]).then_inc(kept, 1)
                if front:
                    h1_low(f, q, 0)
                if mid:
                    residual(m, 1 - q, 1)
                if front:
                    h1_low(f, q, 1)

            dve.wait_ge(w_pool, 1)
            dve.wait_ge(h_loaded, 16 * TB)
            ln_stats(V, dve, ln_b, 0, [Ht(0, j) for j in range(TB)], st[1], mv[1], rs[1], nm[1])
            x_low(0)
            iterations(dve, step)

        @block.scalar
        def _(act):
            act.dma_start(cols[:, 0:4, :], io["cols"]).then_inc(consts[2], 16)
            act.dma_start(b1[:], io["b1"]).then_inc(consts[3], 16)
            act.dma_start(gate_w[:], io["gate_w"]).then_inc(consts[4], 16)
            A.activation(primer[:], ident[0:1, 0:1], ACT.Gelu_apprx_tanh)
            A.activation(ret_w[0][:], ret_raw, ACT.Copy).then_inc(w_split, 1)
            A.activation(w1[0][:], w1_raw, ACT.Copy).then_inc(w_split, 1)
            A.activation(w2[0][:], w2_raw, ACT.Copy).then_inc(w_split, 1)

            def normalise(out, src, group, j):
                return A.activation(out, src, ACT.Identity, bias=nm[group][:, j:j + 1], scale=rs[group][:, j:j + 1])

            def x_of(b, signals, o):
                act.wait_ge(ln_b, signals)
                if type(b) is not int or b >= 1:
                    act.wait_ge(t1, b)
                for j in range(TB):
                    a = normalise(xn[:, j, :], Ht(b, j), 1, o + j)
                a.then_inc(x_ready, 1)

            def gelu_of(b, f, first):
                act.wait_ge(w1_mm, b * FB + f + 1)
                if f >= NG or not first:
                    act.wait_ge(g_lo_s, b * FB + (f - NG + 1))
                for out in (g[f % NG][:], g_hi[:, f, :]):
                    A.activation(out, psF[:, f % 2, 0:SEQ], ACT.Gelu_apprx_tanh, bias=b1[:, f:f + 1]).then_inc(gelu, 1)

            def x_copies(b):
                act.wait_ge(t1, b + 1)
                A.activation(x_hi[:], X, ACT.Copy).then_inc(x_copied, 1)
                A.activation(xT[:], X, ACT.Copy, bias=0.5).then_inc(x_copied, 1)

            def h1_of(q, k):
                for out in (h1T[q][:, k, :], h1_hi[:, k, :]):
                    A.activation(out, X[:, k, :], ACT.Identity, bias=cols[:, 2, k:k + 1],
                                 scale=cols[:, 1, k:k + 1]).then_inc(h1_copied, 1)

            def step(i, q):
                front, mid, tail, last, more = parts(i)
                f, m, t = i, i - 1, i - 2
                first = type(i) is int and i == 1
                if front:
                    act.wait_ge(ret_mm, f + 1)
                    for k in range(DC):
                        A.activation(th[:, k, :], X[:, k, :], ACT.Tanh, bias=cols[:, 4, k:k + 1], scale=0.5)\
                            .then_inc(tanh_done, 1)
                if mid:
                    for k in range(3):
                        gelu_of(m, k, first)
                if tail:
                    act.wait_ge(ln_b, signals_b(i) + (TWO if more else ONE))
                    for j in range(TB):
                        a = normalise(n2[:, j, :], tokY[j], 1, j)
                    a.then_inc(n2_ready, 1)
                if mid:
                    gelu_of(m, 3, first)
                if more:
                    x_of(f + 1, signals_b(i) + (TWO if tail else ONE), TB if tail else 0)
                if mid:
                    for k in (4, 5):
                        gelu_of(m, k, first)
                if more:
                    x_copies(f + 1)
                if mid:
                    for k in (6, 7):
                        gelu_of(m, k, first)
                if front:
                    act.wait_ge(ln_a, signals_a(i) + (TWO if tail else ONE))
                    for j in range(TB):
                        a = normalise(h1n[:, j, :], tokY[j], 0, j)
                    a.then_inc(h1n_ready, 1)
                if tail:
                    if not front:
                        act.wait_ge(ln_a, signals_a(i) + ONE)
                    if type(i) is not int or i >= 3:
                        act.wait_ge(t5, t)
                    for j in range(TB):
                        a = normalise(zn[:, j, :], Ht(t, j), 0, (TB if front else 0) + j)
                    a.then_inc(z_ready, 1)
                if front:
                    act.wait_ge(t3, f + 1)
                    h1_of(q, 0)
                if tail:
                    act.wait_ge(t5, t + 1)
                    A.activation(zT[:, :, bass.ds(t * SEQ, SEQ)], Y, ACT.Copy).then_inc(z_copied, 1)
                if last:
                    act.wait_ge(lg_mm, t)
                    A.activation(lg_feat[:], psG[0:NE, 0, 0:SEQ], ACT.Copy).then_inc(lg_copied, 1)
                if front:
                    h1_of(q, 1)
                if last:
                    act.wait_ge(lg_turned, t)
                    A.activation(lg_rows[:, bass.ds((t - 1) * TB, TB), :], LG, ACT.Copy).then_inc(lg_kept, 1)

            act.wait_ge(half_b, 3)
            for j in (3, 4):
                act.wait_ge(consts[j], 16)
            x_of(0, ONE, 0)
            x_copies(0)
            iterations(act, step)

        @block.tensor
        def _(pe):
            def to_features(src, ps):
                for t in range(TB):
                    for k in range(DC):
                        mm = T.transpose(ps[:, k, t * P:(t + 1) * P], src[:, t, k * P:(k + 1) * P], ident[:])
                return mm

            def to_tokens(src):
                for t in range(TB):
                    for k in range(DC):
                        mm = T.transpose(rowsY[:, t * D + k * P:t * D + (k + 1) * P], src[:, k, t * P:(t + 1) * P], ident[:])
                return mm

            def product(out, w, cols_, act_hi, act_lo, first, last):
                T.matmul(out, w[0][cols_], act_hi, start=first, stop=False)
                T.matmul(out, w[0][cols_], act_lo, start=False, stop=False)
                return T.matmul(out, w[1][cols_], act_hi, start=False, stop=last)

            def hidden(b, f, first):
                if f >= 2 or not first:
                    pe.wait_ge(gelu, b * (2 * FB) + (2 * f - 2))
                for k in range(DC):
                    mm = product(psF[:, f % 2, 0:SEQ], w1, (slice(None), k, slice(f * P, (f + 1) * P)),
                                 h1_hi[:, k, :], h1_lo[:, k, :], k == 0, k == DC - 1)
                mm.then_inc(w1_mm, 1)

            def down(b, n, ks):
                for k in ks:
                    if n == 0:
                        pe.wait_ge(g_lo_s, b * FB + k + 1)
                    mm = product(psG[:, n, 0:SEQ], w2, (slice(None), k, slice(n * P, (n + 1) * P)),
                                 g_hi[:, k, :], g_lo[:, k, :], k == 0, k == FB - 1)
                if k == FB - 1:
                    mm.then_inc(w2_mm, 1)

            def step(i, q):
                front, mid, tail, last, more = parts(i)
                f, m, t = i, i - 1, i - 2
                first = type(i) is int and i == 1
                if front:
                    pe.wait_ge(x_split, f + 1)
                    if mid:
                        pe.wait_ge(h1_copied, f * (2 * DC))
                    for n in range(DC):
                        for k in range(DC):
                            mm = product(psX[:, n, 0:SEQ], ret_w, (slice(None), k, slice(n * P, (n + 1) * P)),
                                         x_hi[:, k, :], x_lo[:, k, :], k == 0, k == DC - 1)
                    mm.then_inc(ret_mm, 1)
                if mid:
                    pe.wait_ge(h1_lo_s, (m + 1) * DC)
                    for k in range(W1_T2):
                        hidden(m, k, first)
                if front:
                    pe.wait_ge(r_ready, f + 1)
                    if tail:
                        pe.wait_ge(n2_ready, t + 1)
                    to_tokens(ret).then_inc(t2, 1)
                if mid:
                    for k in range(W1_T2, 5):
                        hidden(m, k, first)
                if more:
                    pe.wait_ge(x_ready, f + 2)
                    if front:
                        pe.wait_ge(tanh_done, (f + 1) * DC)
                    to_features(xn, psX).then_inc(t1, 1)
                if mid:
                    if tail:
                        pe.wait_ge(r2, m * DC)
                    if parts(i - 1)[3]:
                        pe.wait_ge(lg_kept, t - 1)
                    hidden(m, 5, first)
                    down(m, 0, range(0, 3))
                    hidden(m, 6, first)
                    down(m, 0, range(3, 5))
                    hidden(m, 7, first)
                    down(m, 0, range(5, 8))
                    down(m, 1, range(0, SPLIT_T3))
                if front:
                    pe.wait_ge(h1n_ready, f + 1)
                    if more:
                        pe.wait_ge(x_split, f + 2)
                    to_features(h1n, psX).then_inc(t3, 1)
                if mid:
                    down(m, 1, range(SPLIT_T3, 8))
                if tail:
                    pe.wait_ge(z_ready, t + 1)
                    to_features(zn, psY).then_inc(t5, 1)
                if last:
                    pe.wait_ge(z_copied, t)
                    if mid:
                        pe.wait_ge(r2, m * DC + 1)
                    else:
                        pe.wait_ge(lg_kept, t - 1)
                    for k in range(DC):
                        mm = T.matmul(psG[0:NE, 0, 0:SEQ], gate_w[:, k, :], zT[:, k, bass.ds((t - 1) * SEQ, SEQ)],
                                      start=(k == 0), stop=(k == DC - 1))
                    mm.then_inc(lg_mm, 1)
                if last:
                    pe.wait_ge(lg_copied, t)
                if mid:
                    pe.wait_ge(r2, (m + 1) * DC)
                    if tail:
                        pe.wait_ge(z_copied, t + 1)
                    elif front:
                        pe.wait_ge(h1n_ready, f + 1)
                    to_tokens(r2T).then_inc(t4, 1)
                if last:
                    for j in range(TB):
                        mm = T.transpose(LG[:, j, :], lg_feat[:, j * P:(j + 1) * P], ident[0:NE, 0:NE])
                    mm.then_inc(lg_turned, 1)

            pe.wait_ge(half_b, 2)
            pe.wait_ge(consts[4], 16)
            pe.wait_ge(w_pool, 2)
            pe.wait_ge(x_ready, 1)
            to_features(xn, psX).then_inc(t1, 1)
            iterations(pe, step)


def moe_phase(nc, io, per, xs, eo, out):
    H, zT, ident, raw, lg = per["H"], per["zT"], per["ident"], per["raw"], per["lg_rows"]
    rz, nmz = per["rz"], per["nmz"]
    with ExitStack() as ctx:
        sb = lambda name, shape, dt=F32: ctx.enter_context(nc.sbuf_tensor(name, shape, dt))
        sem = lambda name: ctx.enter_context(nc.semaphore(name))
        ps = lambda name, n: ctx.enter_context(nc.psum_tensor(name, [P, n, 512], F32))
        psGU, psX, psO = ps("psGU", 4), ps("psT", 2), ps("psO", 2)
        rowsO = psO[:].rearrange("p a b -> p (a b)")
        rowsX = psX[:, 1, 0:NT * NE].rearrange("p (t e) -> p t e", e=NE)

        sh_w = [sb(f"sh_w{j}", [P, W_SH], FR) for j in range(2)]
        ex_w = [[sb(f"ex_w{q}{j}", [P, W_EX], FR) for j in range(2)] for q in range(2)]
        sh_raw = raw[:, 0:W_SH]
        ex_raw = [raw[:, W_SH:W_SH + W_EX], raw[:, 0:W_EX]]

        xin = [sb(f"xin{q}", [XP, 2 * XT, D]) for q in range(2)]
        x_hi = [sb(f"job_x_hi{q}", [P, DC, HALF], FR) for q in range(2)]
        x_lo = [sb(f"job_x_lo{q}", [P, DC, HALF], FR) for q in range(2)]
        silu_g = [sb(f"silu_g{q}", [P, HALF]) for q in range(2)]
        act_a = [sb(f"act_a{q}", [P, HALF]) for q in range(2)]
        a_hi = sb("a_hi", [P, 2 * SB * SEQ], FR)
        a_lo = sb("a_lo", [P, 2 * SB * SEQ], FR)
        y_out = [sb(f"y_out{q}", [XP, XT, D]) for q in range(2)]
        ring = [sb(f"ring{q}", [P, TB, TOPK, D]) for q in range(2)]

        sc = sb("sc", [P, NT, NE])
        tmp = sb("r_tmp", [P, NT, NE])
        oh = [sb(f"oh{k}", [P, NT, NE]) for k in range(TOPK)]
        desc = sb("desc", [P, NT, NE])
        cnt = sb("cnt", [P, NT, NE], BF16)
        below = sb("below", [P, P], BF16)
        ones = sb("ones", [P, P], BF16)
        col = lambda name: sb(name, [P, NT])
        mx, sm, den = col("r_max"), col("r_sum"), col("r_den")
        top = [col(f"top{k}") for k in range(TOPK)]
        who = [col(f"who{k}") for k in range(TOPK)]
        pos = [col(f"pos{k}") for k in range(TOPK)]
        keep = [col(f"keep{k}") for k in range(TOPK)]
        wgt = [col(f"wgt{k}") for k in range(TOPK)]
        slot_in = sb("slot_in", [P, TOPK, NT], U32)
        slot_out = sb("slot_out", [P, TOPK, NT], U32)

        sh_hi, sh_lo = sem("sh_hi"), sem("sh_lo")
        ex_loaded = [sem(f"ex_loaded{q}") for q in range(2)]
        ex_hi, ex_lo = sem("ex_hi"), sem("ex_lo")
        made, route, r_exp, counted, prefix = (sem("made"), sem("route"), sem("r_exp"), sem("counted"),
                                               sem("prefix"))
        routed, z_rows = sem("routed"), sem("z_rows")
        scat = [sem(f"scattered{q}") for q in range(4)]
        xin_loaded = [sem(f"xin_loaded{q}") for q in range(2)]
        turned = sem("turned")
        xhi_ready, xlo_ready = sem("xhi_ready"), sem("xlo_ready")
        gu_ready, silu_ready, a_ready, ahi_ready, alo_ready = (
            sem(f"{n}_ready") for n in ("gu", "silu", "a", "ahi", "alo"))
        rows_ready, rows_read = sem("rows_ready"), sem("rows_read")
        y_stored = [sem(f"y_stored{q}") for q in range(2)]
        gath = [sem(f"gathered{q}") for q in range(2)]
        comb, stored = sem("combined"), sem("out_stored")
        block = ctx.enter_context(nc.Block())
        V, A, G, T = nc.vector, nc.scalar, nc.gpsimd, nc.tensor
        gate = lambda w, n: w[:, 0:DC * n].rearrange("p (k i) -> p k i", k=DC)
        up = lambda w, n: w[:, DC * n:2 * DC * n].rearrange("p (k i) -> p k i", k=DC)
        down = lambda w, n: w[:, 2 * DC * n:].rearrange("p (k d) -> p k d", d=D)
        SH_IN = 2 * DC * I_SH
        zT_of = lambda b: zT[:, :, b * SEQ:(b + 1) * SEQ]
        flat_h = H[:].rearrange("p t d -> p (t d)")
        Hb = lambda b: flat_h[:, b * TB * D:(b + 1) * TB * D]
        z_ring = lambda b, t: ring[b % 2][:, t, (b // 2) % 2, :]
        xs_rows = xs.rearrange("(e t p) d -> e p t d", p=XP, t=2 * XT)
        eo_rows = eo.rearrange("(u t p) d -> u p t d", p=XP, t=XT)

        unit = lambda i, r: i * 4 + r
        expert = lambda i, r: i * 2 + r // 2
        exists = lambda i, r: type(i) is not int or 0 <= unit(i, r) < UNITS
        xin_of = lambda r: r // 2 % 2
        job_s = lambda b: b if b < SH_FIRST else b + UNITS
        job_e = lambda i, r: unit(i, r) + SH_FIRST
        block_s = lambda b: SB * b if b < SH_FIRST else SB * b + EB * UNITS
        block_e = lambda i, r: unit(i, r) * EB + SB * SH_FIRST
        job_q = lambda r: (r + SH_FIRST) % 2

        def units(eng, step):
            step(0, 0), step(0, 1)
            with eng.Fori(0, UNITS // 4 - 1) as i:
                for r in range(2, 6):
                    step(i, r)
            step(UNITS // 4 - 1, 2), step(UNITS // 4 - 1, 3)

        def a_at(blk, width):
            slot = blk % (2 * SB if width == SEQ else 2 * EB)
            return slice(slot * width, (slot + 1) * width)

        def block_slots(r):
            return [(block_e(0, r) + j) % (2 * EB) for j in range(EB)]

        @block.sync
        def _(sp):
            def load_weights(e, q, before):
                if before:
                    sp.wait_ge(ex_lo, e - 1)
                sp.dma_start(ex_raw[q], io["ex_w"][e]).then_inc(ex_loaded[q], 16)

            def load_tokens(e, q, before):
                if before:
                    sp.wait_ge(turned, 2 * e - 2)
                sp.dma_start(xin[q][:], xs_rows[e]).then_inc(xin_loaded[q], 16)

            sp.wait_ge(sh_lo, 3)
            load_weights(1, 1, False)
            for q in range(4):
                sp.wait_ge(scat[q], 16 * TB * TOPK * (B // 4))
            load_tokens(0, 0, False)
            load_tokens(1, 1, False)
            for u in range(UNITS):
                e = u // 2 + 2
                if u % 2 == 0 and e < NE:
                    load_weights(e, e % 2, True)
                    load_tokens(e, e % 2, True)
                sp.wait_ge(rows_read, job_e(0, u) + 1)
                sp.dma_start(eo_rows[u], y_out[u % 2][:]).then_inc(y_stored[u % 2], 16)
            for b in range(B):
                sp.wait_ge(comb, TB * TOPK * (b + 1))
                sp.dma_start(out[b].rearrange("(t p) d -> p t d", p=P), H[:, b * TB:(b + 1) * TB, :]).then_inc(stored, 16)
            sp.wait_ge(stored, 16 * B)

        @block.gpsimd
        def _(pool):
            for e in range(NE):
                G.memset(desc[:, :, e:e + 1], float(NE - e)).then_inc(made, 1)
            G.memset(ones[:], 1.0).then_inc(made, 1)
            G.memset(below[:], 1.0).then_inc(made, 1)
            pool.wait_ge(made, NE + 2)
            G.affine_select(out=below[:], in_=below[:], compare_op=ALU.is_gt, fill=0.0, base=0,
                            pattern=[[1, P]], channel_multiplier=-1).then_inc(made, 1)
            pool.wait_ge(routed, 1)
            for b in range(B):
                pool.wait_ge(z_rows, b + 1)
                for t in range(TB):
                    for k in range(TOPK):
                        G.indirect_dma_start(
                            out=xs[:, :], out_offset=bass.IndirectOffsetOnAxis(ap=slot_in[:, k, b * TB + t:b * TB + t + 1], axis=0),
                            in_=z_ring(b, t), in_offset=None,
                            bounds_check=NE * CAP - 1, oob_is_err=False).then_inc(scat[b % 4], 16)
            for q in range(2):
                pool.wait_ge(y_stored[q], 16 * (UNITS // 2))
            for b in range(B):
                if b >= 2:
                    pool.wait_ge(comb, TB * TOPK * (b - 1))
                for t in range(TB):
                    for k in range(TOPK):
                        G.indirect_dma_start(
                            out=ring[b % 2][:, t, k, :], out_offset=None,
                            in_=eo[:, :], in_offset=bass.IndirectOffsetOnAxis(ap=slot_out[:, k, b * TB + t:b * TB + t + 1], axis=0))\
                            .then_inc(gath[b % 2], 16)

        @block.vector
        def _(dve):
            n = [0]

            def link(ins):
                n[0] += 1
                ins.then_inc(route, 1)
                dve.wait_ge(route, n[0])

            bc = lambda x: x[:].unsqueeze(2).to_broadcast([P, NT, NE])

            def choose():
                link(V.tensor_reduce(mx[:], lg[:], AX.X, ALU.max))
                link(V.tensor_tensor(lg[:], lg[:], bc(mx), ALU.subtract))
                dve.wait_ge(r_exp, 1)
                link(V.tensor_reduce(sm[:], sc[:], AX.X, ALU.add))
                link(V.reciprocal(sm[:], sm[:]))
                link(V.tensor_tensor(sc[:], sc[:], bc(sm), ALU.mult))
                dve.wait_ge(made, NE + 3)
                for k in range(TOPK):
                    link(V.tensor_reduce(top[k][:], sc[:], AX.X, ALU.max))
                    link(V.tensor_tensor(tmp[:], sc[:], bc(top[k]), ALU.is_equal))
                    link(V.tensor_tensor(tmp[:], tmp[:], desc[:], ALU.mult))
                    link(V.tensor_reduce(who[k][:], tmp[:], AX.X, ALU.max))
                    link(V.tensor_tensor(oh[k][:], tmp[:], bc(who[k]), ALU.is_equal))
                    if k == 0:
                        link(V.scalar_tensor_tensor(out=sc[:], in0=oh[0][:], scalar=-2.0, in1=sc[:], op0=ALU.mult, op1=ALU.add))
                V.tensor_tensor(cnt[:], oh[0][:], oh[1][:], ALU.add).then_inc(counted, 1)
                link(V.tensor_tensor(den[:], top[0][:], top[1][:], ALU.add))
                link(V.tensor_scalar(den[:], den[:], 1e-20, None, ALU.add))
                link(V.reciprocal(den[:], den[:]))

            def place(k):
                link(V.tensor_tensor(tmp[:], oh[k][:], rowsX, ALU.mult))
                link(V.tensor_reduce(pos[k][:], tmp[:], AX.X, ALU.add))
                link(V.tensor_scalar(keep[k][:], pos[k][:], float(CAP), None, ALU.is_lt))
                link(V.tensor_tensor(wgt[k][:], top[k][:], den[:], ALU.mult))
                link(V.tensor_tensor(wgt[k][:], wgt[k][:], keep[k][:], ALU.mult))
                link(V.scalar_tensor_tensor(out=pos[k][:], in0=who[k][:], scalar=-float(CAP), in1=pos[k][:], op0=ALU.mult, op1=ALU.add))
                link(V.tensor_scalar(pos[k][:], pos[k][:], float(NE * CAP), None, ALU.add))
                link(V.tensor_tensor(pos[k][:], pos[k][:], keep[k][:], ALU.mult))
                link(V.tensor_scalar(keep[k][:], keep[k][:], -float(OUT_OF_RANGE), float(OUT_OF_RANGE), ALU.mult, ALU.add))
                link(V.tensor_copy(slot_out[:, k, :], pos[k][:]))
                link(V.tensor_tensor(slot_in[:, k, :], pos[k][:], keep[k][:], ALU.add))

            def hidden(blk, par, at, w):
                dve.wait_ge(silu_ready, blk + 1)
                V.tensor_tensor(act_a[par][:, 0:w], silu_g[par][:, 0:w], psGU[:, 2 * par + 1, 0:w], ALU.mult).then_inc(a_ready, 1)
                dve.wait_ge(a_ready, blk + 1)
                V.tensor_copy(a_hi[:, at], act_a[par][:, 0:w]).then_inc(ahi_ready, 1)
                dve.wait_ge(ahi_ready, blk + 1)
                V.tensor_tensor(a_lo[:, at], act_a[par][:, 0:w], a_hi[:, at].bitcast(F32), ALU.subtract).then_inc(alo_ready, 1)

            def hidden_s(b, j):
                blk = block_s(b) + j
                hidden(blk, blk % 2, a_at(blk, SEQ), SEQ)

            def x_low_s(b):
                q = job_s(b) % 2
                dve.wait_ge(xhi_ready, job_s(b) + 1)
                V.tensor_tensor(x_lo[q][:, :, 0:SEQ], zT_of(b), x_hi[q][:, :, 0:SEQ].bitcast(F32), ALU.subtract)\
                    .then_inc(xlo_ready, 1)

            def x_low_e(i, r):
                q = job_q(r)
                dve.wait_ge(xhi_ready, job_e(i, r) + 1)
                V.tensor_tensor(x_lo[q][:], psX[:, :, 0:HALF], x_hi[q][:].bitcast(F32), ALU.subtract).then_inc(xlo_ready, 1)

            def add(b):
                dve.wait_ge(rows_ready, job_s(b) + 1)
                dve.wait_ge(z_rows, b + 1)
                V.tensor_tensor(Hb(b), Hb(b), rowsO[:, 0:TB * D], ALU.add).then_inc(rows_read, 1)

            def shared_weights(j, a, b):
                dve.wait_ge(sh_hi, j + 1)
                V.tensor_tensor(sh_w[1][:, a:b], sh_raw[:, a:b], sh_w[0][:, a:b].bitcast(F32), ALU.subtract).then_inc(sh_lo, 1)

            def expert_weights(e, q):
                dve.wait_ge(ex_hi, e + 1)
                V.tensor_tensor(ex_w[q][1][:], ex_raw[q], ex_w[q][0][:].bitcast(F32), ALU.subtract).then_inc(ex_lo, 1)

            def combine(b):
                dve.wait_ge(gath[b % 2], 16 * TB * TOPK * (b // 2 + 1))
                dve.wait_ge(rows_read, job_s(b) + 1)
                for k in range(TOPK):
                    if k:
                        dve.wait_ge(comb, TB * (TOPK * b + k))
                    for t in range(TB):
                        i = b * TB + t
                        V.scalar_tensor_tensor(out=H[:, i, :], in0=ring[b % 2][:, t, k, :], scalar=wgt[k][:, i:i + 1],
                                               in1=H[:, i, :], op0=ALU.mult, op1=ALU.add).then_inc(comb, 1)

            x_low_s(0)
            shared_weights(0, 0, SH_IN // 2)
            shared_weights(1, SH_IN // 2, SH_IN)
            choose()
            hidden_s(0, 0)
            dve.wait_ge(prefix, 1)
            place(0)
            place(1)
            dve.sem_inc(routed, 1)
            hidden_s(0, 1)
            shared_weights(2, SH_IN, W_SH)
            x_low_s(1)
            for j in (2, 3):
                hidden_s(0, j)
            expert_weights(0, 0)
            for b in range(1, SH_FIRST):
                if b + 1 < SH_FIRST:
                    x_low_s(b + 1)
                for j in range(SB):
                    hidden_s(b, j)
                add(b - 1)
            x_low_e(0, 0)
            add(SH_FIRST - 1)

            def step(i, r):
                if exists(i, r + 1):
                    x_low_e(i, r + 1)
                else:
                    x_low_s(SH_FIRST)
                for j, slot in enumerate(block_slots(r)):
                    hidden(block_e(i, r) + j, slot % 2, a_at(slot, HALF), HALF)
                    if j == 0 and r % 2 == 1 and exists(i, r + 1):
                        expert_weights(expert(i, r + 1), xin_of(r + 1))

            units(dve, step)
            done = 0
            for b in range(SH_FIRST, B):
                if b + 1 < B:
                    x_low_s(b + 1)
                for j in range(SB):
                    hidden_s(b, j)
                    if j == 1 and b > SH_FIRST:
                        combine(done)
                        done += 1
                if b > SH_FIRST:
                    add(b - 1)
                combine(done)
                done += 1
            add(B - 1)
            for b in range(done, B):
                combine(b)

        @block.scalar
        def _(act):
            def shared_weights(a, b):
                A.activation(sh_w[0][:, a:b], sh_raw[:, a:b], ACT.Copy).then_inc(sh_hi, 1)

            def expert_weights(i, r):
                q = xin_of(r)
                if exists(i, r - 3):
                    act.wait_ge(rows_ready, job_e(i, r - 3) + 1)
                if type(i) is not int or unit(i, r) >= 2:
                    act.wait_ge(ex_loaded[q], (i + (r // 4 if q == 0 else r // 4 + 1)) * 16)
                A.activation(ex_w[q][0][:], ex_raw[q], ACT.Copy).then_inc(ex_hi, 1)

            def z_of(b):
                if b >= 4:
                    act.wait_ge(scat[b % 4], 16 * TB * TOPK * (b // 4))
                for t in range(TB):
                    i = b * TB + t
                    a = A.activation(z_ring(b, t), H[:, i, :], ACT.Identity, bias=nmz[:, i:i + 1], scale=rz[:, i:i + 1])
                a.then_inc(z_rows, 1)

            def silu(blk, par, w, first=False):
                act.wait_ge(gu_ready, blk + 1)
                if not first:
                    act.wait_ge(a_ready, blk - 1)
                A.activation(silu_g[par][:, 0:w], psGU[:, 2 * par, 0:w], ACT.Silu).then_inc(silu_ready, 1)

            def x_high_s(b):
                if b >= 2:
                    act.wait_ge(gu_ready, block_s(b) - (EB if b == SH_FIRST else SB))
                q = job_s(b) % 2
                A.activation(x_hi[q][:, :, 0:SEQ], zT_of(b), ACT.Copy).then_inc(xhi_ready, 1)

            def x_high_e(i, r):
                act.wait_ge(turned, unit(i, r) + 1)
                A.activation(x_hi[job_q(r)][:], psX[:, :, 0:HALF], ACT.Copy).then_inc(xhi_ready, 1)

            def silu_s(b, j):
                blk = block_s(b) + j
                silu(blk, blk % 2, SEQ, blk < 2)

            def y_of(i, r):
                act.wait_ge(rows_ready, job_e(i, r) + 1)
                act.wait_ge(y_stored[r % 2], (i * 2 + r // 2) * 16)
                A.activation(y_out[r % 2][:].rearrange("p t d -> p (t d)"), rowsO[0:XP, 0:XT * D], ACT.Copy).then_inc(rows_read, 1)

            shared_weights(0, SH_IN // 2)
            x_high_s(0)
            shared_weights(SH_IN // 2, SH_IN)
            z_of(0)
            act.wait_ge(route, 2)
            A.activation(sc[:], lg[:], ACT.Exp).then_inc(r_exp, 1)
            shared_weights(SH_IN, W_SH)
            silu_s(0, 0)
            z_of(1)
            x_high_s(1)
            silu_s(0, 1)
            expert_weights(0, 0)
            z_of(2)
            z_of(3)
            silu_s(0, 2)
            silu_s(0, 3)
            z_next = 4
            for b in range(1, SH_FIRST):
                if b + 1 < SH_FIRST:
                    x_high_s(b + 1)
                for j in range(SB):
                    silu_s(b, j)
                while z_next < B and z_next < b + 4 + (b == SH_FIRST - 1) * B:
                    z_of(z_next)
                    z_next += 1
            x_high_e(0, 0)

            def step(i, r):
                if exists(i, r + 1):
                    x_high_e(i, r + 1)
                else:
                    x_high_s(SH_FIRST)
                if exists(i, r - 2):
                    y_of(i, r - 2)
                for j, slot in enumerate(block_slots(r)):
                    silu(block_e(i, r) + j, slot % 2, HALF)
                    if j == 0 and r % 2 == 1 and exists(i, r + 1):
                        expert_weights(i, r + 1)

            units(act, step)
            y_of(0, UNITS - 2)
            y_of(0, UNITS - 1)
            for b in range(SH_FIRST, B):
                if b + 1 < B:
                    x_high_s(b + 1)
                for j in range(SB):
                    silu_s(b, j)

        @block.tensor
        def _(pe):
            def product(out, w, at, hi, lo, first, last):
                T.matmul(out, w[0][at], hi, start=first, stop=False)
                T.matmul(out, w[0][at], lo, start=False, stop=False)
                return T.matmul(out, w[1][at], hi, start=False, stop=last)

            def hidden(blk, par, j, q, n, w, ws, first=False):
                if not first:
                    pe.wait_ge(a_ready, blk - 1)
                for o, part in ((0, gate), (1, up)):
                    wg = [part(x, n) for x in ws]
                    for k in range(DC):
                        mm = product(psGU[:, 2 * par + o, 0:w], wg, (slice(None), k, slice(j * P, (j + 1) * P)),
                                     x_hi[q][:, k, 0:w], x_lo[q][:, k, 0:w], k == 0, k == DC - 1)
                mm.then_inc(gu_ready, 1)

            def down_rows(job, last_blk, n, ws, tiles, rows, cols_):
                wd = [down(x, n) for x in ws]
                pe.wait_ge(alo_ready, last_blk + 1)
                if type(job) is not int or job >= 1:
                    pe.wait_ge(rows_read, job)
                for t in range(tiles):
                    o = rowsO[0:rows, t * D:(t + 1) * D]
                    for k, c in enumerate(cols_):
                        r = slice(c.start + t * rows, c.start + (t + 1) * rows)
                        T.matmul(o, a_hi[:, r], wd[0][:, k, :], start=(k == 0), stop=False)
                        T.matmul(o, a_lo[:, r], wd[0][:, k, :], start=False, stop=False)
                        mm = T.matmul(o, a_hi[:, r], wd[1][:, k, :], start=False, stop=(k == len(cols_) - 1))
                mm.then_inc(rows_ready, 1)

            def hidden_s(b, j):
                blk = block_s(b) + j
                hidden(blk, blk % 2, j, job_s(b) % 2, I_SH, SEQ, sh_w, blk < 2)

            def down_s(b):
                blk = block_s(b)
                down_rows(job_s(b), blk + SB - 1, I_SH, sh_w, TB, P, [a_at(blk + k, SEQ) for k in range(SB)])

            def turn(i, r):
                q = xin_of(r)
                if r % 2 == 0:
                    pe.wait_ge(xin_loaded[q], (i + (r // 4 + 1)) * 16)
                if exists(i, r - 1):
                    pe.wait_ge(xlo_ready, job_e(i, r))
                for t in range(XT):
                    for k in range(DC):
                        mm = T.transpose(psX[:, k, t * XP:(t + 1) * XP], xin[q][:, (r % 2) * XT + t, k * P:(k + 1) * P],
                                         ident[0:XP, 0:XP])
                mm.then_inc(turned, 1)

            def hidden_e(i, r):
                pe.wait_ge(xlo_ready, job_e(i, r) + 1)
                if r % 2 == 0:
                    pe.wait_ge(ex_lo, expert(i, r) + 1)
                for j, slot in enumerate(block_slots(r)):
                    hidden(block_e(i, r) + j, slot % 2, j, job_q(r), I_EXP, HALF, ex_w[xin_of(r)])

            def down_e(i, r):
                down_rows(job_e(i, r), block_e(i, r) + EB - 1, I_EXP, ex_w[xin_of(r)], XT, XP,
                          [a_at(slot, HALF) for slot in block_slots(r)])

            pe.wait_ge(sh_lo, 2)
            pe.wait_ge(xlo_ready, 1)
            hidden_s(0, 0)
            pe.wait_ge(counted, 1)
            T.matmul(psX[:, 1, 0:NT * NE], below[:], cnt[:].rearrange("p t e -> p (t e)"), start=True, stop=False)
            for t in range(NT - 1):
                mm = T.matmul(psX[:, 1, (t + 1) * NE:NT * NE], ones[:], cnt[:, t:t + 1, :].to_broadcast([P, NT - 1 - t, NE]),
                              start=False, stop=(t == NT - 2))
            mm.then_inc(prefix, 1)
            for j in range(1, SB):
                hidden_s(0, j)
            for b in range(1, SH_FIRST):
                pe.wait_ge(xlo_ready, job_s(b) + 1)
                for j in range(SB):
                    hidden_s(b, j)
                down_s(b - 1)
            turn(0, 0)
            down_s(SH_FIRST - 1)

            def step(i, r):
                if exists(i, r + 1):
                    turn(i, r + 1)
                hidden_e(i, r)
                if exists(i, r - 1):
                    down_e(i, r - 1)

            units(pe, step)
            down_e(0, UNITS - 1)
            for b in range(SH_FIRST, B):
                pe.wait_ge(xlo_ready, job_s(b) + 1)
                for j in range(SB):
                    hidden_s(b, j)
                if b > SH_FIRST:
                    down_s(b - 1)
            down_s(B - 1)


def fusion_program(nc, log_dt, inv_a, a_im, b_ri, c_ri, txt, raw_w, cols, b1, ln2_scale, ln2_bias, gate_w,
                   sh_w, ex_w, out):
    io = dict(log_dt=log_dt, inv_a=inv_a, a_im=a_im, b_ri=b_ri, c_ri=c_ri, txt=txt, raw_w=raw_w, cols=cols, b1=b1,
              ln2_scale=ln2_scale, ln2_bias=ln2_bias, gate_w=gate_w, sh_w=sh_w, ex_w=ex_w)
    scratch = nc.dram_tensor("ssm_kernel", (S_SSM, B, D), F32, kind="Internal").ap()
    xs = nc.dram_tensor("expert_rows", (NE * CAP, D), F32, kind="Internal").ap()
    eo = nc.dram_tensor("expert_out", (NE * CAP, D), F32, kind="Internal").ap()
    with ExitStack() as ctx:
        sb = lambda name, shape: ctx.enter_context(nc.sbuf_tensor(name, shape, F32))
        per = dict(ident=sb("ident", [P, P]), raw=sb("raw", [P, W_SH + W_EX]), H=sb("H", [P, NT, D]))
        ssm_phase(nc, io, scratch, per, xs)
        per.update(zT=sb("zT", [P, DC, TOK]), gate_w=sb("gate_w", [P, DC, NE]), lg_rows=sb("lg_rows", [P, NT, NE]), rz=sb("rz", [P, NT]), nmz=sb("nmz", [P, NT]))
        attn_phase(nc, io, scratch, per)
        moe_phase(nc, io, per, xs, eo, out)


def _half(a):
    return a.reshape(2, HP, N_STATE).transpose(0, 2, 1).reshape(P, HP)


def _blocks(w):
    return w.reshape(-1, P, w.shape[-1]).transpose(1, 0, 2).reshape(P, -1)


def kernel(**inputs):
    import numpy as np
    import concourse.bacc as bacc
    from concourse.bass_utils import run_bass_kernel_spmd

    a = {k: np.asarray(v) for k, v in inputs.items()}
    tok = lambda n: a["L0_tok_" + n]
    att = lambda n: a["L0_attn_" + n]
    ffn = lambda n: a["L0_ffn_" + n]
    column = lambda v: v.reshape(-1, P).T
    swiglu = lambda g, u, d: np.concatenate([_blocks(g.T), _blocks(u.T), _blocks(d.T)], 1)
    laid = dict(
        log_dt=tok("log_dt")[None],
        inv_a=_half(tok("inv_A_real")),
        a_im=_half(tok("A_imag")),
        b_ri=np.stack([_half(tok("B_ri")[..., i]) for i in range(2)]),
        c_ri=a["x"].reshape(B, 2, HP, N_STATE, 2).transpose(1, 3, 4, 2, 0).reshape(P, 2, HP, B),
        txt=a["txt"],
        raw_w=np.concatenate([_blocks(att(n)) for n in ("W_ret", "W1", "W2")], 1),
        cols=np.stack([column(att(n)) for n in ("b_ret", "ln1_scale", "ln1_bias", "b2")], 1),
        b1=column(att("b1")),
        ln2_scale=att("ln2_scale")[None],
        ln2_bias=att("ln2_bias")[None],
        gate_w=_blocks(ffn("gate_w").T).reshape(P, DC, NE),
        sh_w=swiglu(ffn("ws_gate"), ffn("ws_up"), ffn("ws_down")),
        ex_w=np.stack([swiglu(ffn("we_gate")[e], ffn("we_up")[e], ffn("we_down")[e]) for e in range(NE)]),
    )
    nc = bacc.Bacc("TRN2", target_bir_lowering=False, num_devices=1)
    arrays, args = {}, []
    for name, v in laid.items():
        v = np.ascontiguousarray(v)
        arrays[f"in_{name}"] = v
        args.append(nc.dram_tensor(f"in_{name}", v.shape, mybir.dt.from_np(v.dtype), kind="ExternalInput").ap())
    args.append(nc.dram_tensor("out_0", (B, SEQ, D), F32, kind="ExternalOutput").ap())
    fusion_program(nc, *args)
    r = run_bass_kernel_spmd(nc, [arrays], core_ids=[0])
    return r.results[0]["out_0"]
```

```python
from contextlib import ExitStack
import math

import concourse.bass as bass
from concourse import mybir

ALU = mybir.AluOpType
ACT = mybir.ActivationFunctionType
AX = mybir.AxisListType
F32 = mybir.dt.float32
FR = mybir.dt.float32r
BF16 = mybir.dt.bfloat16
I32 = mybir.dt.int32
U32 = mybir.dt.uint32
P = 128

B, S_SSM, N_STATE = 8, 256, 64
S_TXT, D = 128, 256
SEQ = S_SSM + S_TXT
TB = SEQ // P
NT = B * TB
DC = D // P

NA, NB = 4, 64
HP = S_SSM // 2
HC = 16
NCHUNK = HP // HC
POOL_CHUNKS = (2, 5)
LEVELS = (8, 16, 32)
DVE_PAIRS = [(0, 1), (3, 4), (6, 7)]
DVE_STEPS = [(k, w) for pair in DVE_PAIRS for w in LEVELS for k in pair]

F_ATT = 1024
FB = F_ATT // P
NE = 8
EPS = 1e-5
RSQRT_SEED = float(0xdf3759df)

TOK = B * SEQ
TOPK = 2
CAP = math.ceil(1.25 * TOK * TOPK / NE)
HALF = CAP // 2
XP = 120
XT = HALF // XP
I_EXP, I_SH = 256, 512
EB, SB = I_EXP // P, I_SH // P
OUT_OF_RANGE = 1 << 17
UNITS = 2 * NE
W_EX = 2 * DC * I_EXP + EB * D
W_SH = 2 * DC * I_SH + SB * D
ROUTED_FIRST = 4
SCATTERED_FIRST = 2
COMBINE_AFTER = (1, 3)
SH_FIRST = 3
ZERO_PARTS = 10
assert W_SH == FB * SEQ
assert W_SH + W_EX == DC * (D + F_ATT) + FB * D
assert XT * XP == HALF and 2 * HALF == CAP


def ssm_phase(nc, io, scratch, per, xs):
    with ExitStack() as ctx:
        sb = lambda name, shape, dt=F32: ctx.enter_context(nc.sbuf_tensor(name, shape, dt))
        sem = lambda name: ctx.enter_context(nc.semaphore(name))
        dt_bc = sb("dt_bc", [P, HP])
        inv_a = sb("inv_a", [P, HP])
        a_im = sb("a_im", [P, HP])
        b_re = sb("b_re", [P, HP])
        b_im = sb("b_im", [P, HP])
        c_in = sb("c_in", [P, 2, HP, B])
        u = sb("u", [P, HP])
        v = sb("v", [P, HP])
        s1 = sb("s1", [P, HP])
        s2 = sb("s2", [P, HP])
        s3 = sb("s3", [P, HP])
        s4 = sb("s4", [P, HP])
        pw_re = sb("pw_re", [P, HP, NB + 1])
        pw_im = sb("pw_im", [P, HP, NB + 1])
        w_re = sb("w_re", [P, HP, NA])
        w_im = sb("w_im", [P, HP, NA])
        g_re = sb("g_re", [P, HP, B])
        g_im = sb("g_im", [P, HP, B])
        gn_re = sb("gn_re", [P, HP, B])
        gn_im = sb("gn_im", [P, HP, B])
        l_re = sb("l_re", [P, HP, B, NA])
        l_im = sb("l_im", [P, HP, B, NA])
        tv = [sb(f"tv{j}", [P, HP * 8]) for j in range(4)]
        tp = [sb(f"tp{j}", [P, HC * 32]) for j in range(4)]
        sq_re = sb("sq_re", [P, 2, HC * NB // 4])
        sq_im = sb("sq_im", [P, 2, HC * NB // 4])
        k_out = sb("k_out", [P, 2, 2, HC * NB // 4])
        psK = ctx.enter_context(nc.psum_tensor("psK", [P, 2, 4, 512], F32))

        ident, raw = per["ident"], per["raw"]
        zero = per["H"][:].rearrange("p t d -> p (t d)")[:, 0:NE * CAP * D // P // ZERO_PARTS]

        raw_loaded, zero_made, zeroed = sem("raw_loaded"), sem("zero_made"), sem("zeroed")
        ident_made = sem("ident_made")
        loads = [sem(f"ssm_load{j}") for j in range(6)]
        exps = sem("exps")
        squared, evens, level = sem("squared"), sem("evens"), sem("level")
        b_doubled, g_made, g_negated, g_copied = sem("b_doubled"), sem("g_made"), sem("g_negated"), sem("g_copied")
        base = sem("base")
        dve_c = sem("dve_chain")
        pool_c = sem("pool_chain")
        tab = [sem(f"tables{k}") for k in range(NCHUNK)]
        summed = sem("summed")
        evac = sem("evac")
        stored = [sem(f"k_stored{q}") for q in range(2)]
        block = ctx.enter_context(nc.Block())

        def cmul(eng, link, wait, tmp, ore, oim, are, aim, bre, bim):
            products(eng, link, tmp, are, aim, bre, bim)
            wait()
            link(eng.tensor_tensor(ore, tmp[0], tmp[1], ALU.subtract))
            link(eng.tensor_tensor(oim, tmp[2], tmp[3], ALU.add))
            wait()

        def products(eng, link, t, are, aim, bre, bim):
            link(eng.tensor_tensor(t[0], are, bre, ALU.mult))
            link(eng.tensor_tensor(t[1], aim, bim, ALU.mult))
            link(eng.tensor_tensor(t[2], are, bim, ALU.mult))
            link(eng.tensor_tensor(t[3], aim, bre, ALU.mult))

        def powers(eng, link, wait, tmp, h, k, n):
            tt = [x[:, 0:n * k].rearrange("p (h k) -> p h k", h=n) for x in tmp]
            cre = pw_re[:, h, k:k + 1].to_broadcast([P, n, k])
            cim = pw_im[:, h, k:k + 1].to_broadcast([P, n, k])
            cmul(eng, link, wait, tt, pw_re[:, h, k + 1:2 * k + 1], pw_im[:, h, k + 1:2 * k + 1],
                 pw_re[:, h, 1:k + 1], pw_im[:, h, 1:k + 1], cre, cim)

        def chunk(k):
            return slice(k * HC, (k + 1) * HC)

        def powers_of_squares(s, k, w):
            h, half, even = chunk(k), slice(w // 2 + 1, w + 1), slice(w + 2, 2 * w + 1, 2)
            sq = [x[:, s % 2, 0:HC * w // 2].rearrange("p (h k) -> p h k", h=HC) for x in (sq_re, sq_im)]
            nc.vector.wait_ge(squared, 2 * (s + 1))
            nc.vector.tensor_tensor(pw_re[:, h, even], sq[0], sq[1], ALU.subtract).then_inc(evens, 1)
            nc.vector.scalar_tensor_tensor(out=pw_im[:, h, even], in0=pw_re[:, h, half], scalar=2.0, in1=pw_im[:, h, half],
                                           op0=ALU.mult, op1=ALU.mult).then_inc(evens, 1)

        def odd_tmp(w, tmp):
            return [x[:, 0:HC * w // 2].rearrange("p (h k) -> p h k", h=HC) for x in tmp]

        def powers_of_w(eng, link, wait, tmp, h, n):
            s = [x[:, 0:n].rearrange("p (h k) -> p h k", k=1) for x in tmp]
            one, two, three = slice(1, 2), slice(2, 3), slice(3, 4)
            link(eng.tensor_copy(w_re[:, h, one], pw_re[:, h, NB:NB + 1]))
            link(eng.tensor_copy(w_im[:, h, one], pw_im[:, h, NB:NB + 1]))
            wait()
            cmul(eng, link, wait, s, w_re[:, h, two], w_im[:, h, two], w_re[:, h, one], w_im[:, h, one],
                 w_re[:, h, one], w_im[:, h, one])
            cmul(eng, link, wait, s, w_re[:, h, three], w_im[:, h, three], w_re[:, h, two], w_im[:, h, two],
                 w_re[:, h, one], w_im[:, h, one])

        def left_factors(eng, link, wait, tmp, k):
            powers_of_w(eng, link, wait, tmp, chunk(k), HC)
            factor_products(eng, link, tmp, k)
            wait()
            factor_sums(eng, link, tmp, k)
            wait()

        def factor_tmp(tmp):
            return [x[:, 0:HC * B * (NA - 1)].rearrange("p (h c a) -> p h c a", h=HC, c=B) for x in tmp]

        def factor_products(eng, link, tmp, k):
            h, t4 = chunk(k), factor_tmp(tmp)
            gb = lambda g: g[:, h, :].unsqueeze(3).to_broadcast([P, HC, B, NA - 1])
            wb = lambda w: w[:, h, 1:].unsqueeze(2).to_broadcast([P, HC, B, NA - 1])
            link(eng.tensor_tensor(t4[0], gb(g_re), wb(w_re), ALU.mult))
            link(eng.tensor_tensor(t4[1], gb(g_im), wb(w_im), ALU.mult))
            link(eng.tensor_tensor(t4[2], gb(gn_re), wb(w_im), ALU.mult))
            link(eng.tensor_tensor(t4[3], gb(gn_im), wb(w_re), ALU.mult))

        def factor_sums(eng, link, tmp, k):
            h, t4 = chunk(k), factor_tmp(tmp)
            link(eng.tensor_tensor(l_re[:, h, :, 1:], t4[0], t4[1], ALU.subtract))
            link(eng.tensor_tensor(l_im[:, h, :, 1:], t4[2], t4[3], ALU.add))

        @block.sync
        def _(sp):
            sp.dma_start(dt_bc[0:64, :], io["log_dt"][0:1, 0:HP].to_broadcast([64, HP])).then_inc(loads[0], 16)
            sp.dma_start(dt_bc[64:128, :], io["log_dt"][0:1, HP:2 * HP].to_broadcast([64, HP])).then_inc(loads[0], 16)
            sp.dma_start(inv_a[:], io["inv_a"]).then_inc(loads[1], 16)
            sp.dma_start(a_im[:], io["a_im"]).then_inc(loads[2], 16)
            sp.dma_start(b_re[:], io["b_ri"][0]).then_inc(loads[3], 16)
            sp.dma_start(b_im[:], io["b_ri"][1]).then_inc(loads[4], 16)
            sp.dma_start(c_in[:], io["c_ri"].rearrange("p r h c -> p (r h c)")).then_inc(loads[5], 16)
            sp.dma_start(raw[:], io["raw_w"]).then_inc(raw_loaded, 16)
            sp.wait_ge(zero_made, 1)
            xs_flat = xs.rearrange("(p r) d -> p (r d)", p=P)
            w = xs_flat.shape[1] // ZERO_PARTS
            for j in range(ZERO_PARTS):
                sp.dma_start(xs_flat[:, j * w:(j + 1) * w], zero).then_inc(zeroed, 16)
            for k in range(NCHUNK):
                sp.wait_ge(evac, 2 * (k + 1))
                for half in range(2):
                    h0 = half * HP + k * HC
                    dst = scratch[h0:h0 + HC].rearrange("(g j) c (a b) -> (j c a) g b", j=4, b=NB)
                    sp.dma_start(dst, k_out[:, k % 2, half, :].rearrange("p (g b) -> p g b", b=NB)).then_inc(stored[k % 2], 16)
            for q in range(2):
                sp.wait_ge(stored[q], 16 * NCHUNK)
            sp.wait_ge(raw_loaded, 16)
            sp.wait_ge(zeroed, 16 * ZERO_PARTS)

        @block.scalar
        def _(act):
            act.wait_ge(loads[0], 32)
            nc.scalar.activation(dt_bc[:], dt_bc[:], ACT.Exp).then_inc(exps, 1)
            act.wait_ge(loads[1], 16)
            nc.scalar.activation(inv_a[:], inv_a[:], ACT.Exp).then_inc(exps, 1)

            def evacuate(k):
                for half in range(2):
                    act.wait_ge(summed, 2 * k + half + 1)
                    if k >= 2:
                        act.wait_ge(stored[k % 2], 32 * (k // 2))
                    nc.scalar.activation(k_out[:, k % 2, half, :], psK[:, half, k % 4, 0:HC * NB // 4], ACT.Copy).then_inc(evac, 1)

            for j, x in ((3, b_re), (4, b_im)):
                act.wait_ge(loads[j], 16)
                nc.scalar.activation(x[:], x[:], ACT.Copy, scale=2.0).then_inc(b_doubled, 1)
            chunks = iter(range(NCHUNK))

            def evacuate_next(n):
                for _ in range(n):
                    evacuate(next(chunks))

            act.wait_ge(base, 1)
            for s, (k, w) in enumerate(DVE_STEPS):
                if s >= 2:
                    act.wait_ge(level, 2 * (s - 1))
                half = slice(w // 2 + 1, w + 1)
                for x, sq in ((pw_re, sq_re), (pw_im, sq_im)):
                    nc.scalar.activation(sq[:, s % 2, 0:HC * w // 2].rearrange("p (h k) -> p h k", h=HC), x[:, chunk(k), half],
                                         ACT.Square).then_inc(squared, 1)
                if s == 5:
                    act.wait_ge(g_made, 1)
                    for g, neg in ((g_re, gn_re), (g_im, gn_im)):
                        nc.scalar.activation(neg[:], g[:], ACT.Copy, scale=-1.0).then_inc(g_negated, 1)
                    act.wait_ge(g_negated, 2)
                    for g, left in ((g_re, l_re), (gn_im, l_im)):
                        nc.scalar.activation(left[:, :, :, 0:1], g[:].unsqueeze(3), ACT.Copy).then_inc(g_copied, 1)
                if w == NB // 2 and k in DVE_PAIRS[1]:
                    evacuate_next(1 if k == DVE_PAIRS[1][0] else 2)
                if w == NB // 2 and k in DVE_PAIRS[2]:
                    evacuate_next(1 if k == DVE_PAIRS[2][0] else 2)
            for k in DVE_PAIRS[2]:
                evacuate_next(1)

        @block.vector
        def _(dve):
            n = [0]

            def link(ins):
                n[0] += 1
                ins.then_inc(dve_c, 1)

            def wait():
                dve.wait_ge(dve_c, n[0])

            V = nc.vector
            link(V.memset(pw_re[:, :, 0:1], 1.0))
            link(V.memset(pw_im[:, :, 0:1], 0.0))
            link(V.memset(w_re[:, :, 0:1], 1.0))
            link(V.memset(w_im[:, :, 0:1], 0.0))
            dve.wait_ge(exps, 2)
            dve.wait_ge(loads[2], 16)
            link(V.scalar_tensor_tensor(out=u[:], in0=inv_a[:], scalar=-0.5, in1=dt_bc[:], op0=ALU.mult, op1=ALU.mult))
            link(V.scalar_tensor_tensor(out=v[:], in0=a_im[:], scalar=0.5, in1=dt_bc[:], op0=ALU.mult, op1=ALU.mult))
            wait()
            link(V.tensor_tensor(s1[:], u[:], u[:], ALU.mult))
            link(V.tensor_tensor(s2[:], v[:], v[:], ALU.mult))
            link(V.tensor_scalar(s3[:], u[:], -1.0, 1.0, ALU.mult, ALU.add))
            wait()
            link(V.tensor_tensor(s1[:], s1[:], s2[:], ALU.add))
            link(V.tensor_tensor(s4[:], s3[:], s3[:], ALU.mult))
            wait()
            link(V.tensor_tensor(s4[:], s4[:], s2[:], ALU.add))
            link(V.tensor_scalar(s1[:], s1[:], -1.0, 1.0, ALU.mult, ALU.add))
            wait()
            link(V.reciprocal(s4[:], s4[:]))
            wait()
            one = lambda x: x[:].unsqueeze(2)
            link(V.tensor_tensor(pw_re[:, :, 1:2], one(s1), one(s4), ALU.mult))
            link(V.scalar_tensor_tensor(out=pw_im[:, :, 1:2], in0=one(v), scalar=2.0, in1=one(s4), op0=ALU.mult, op1=ALU.mult))
            wait()
            for k in (1, 2, 4):
                powers(V, link, wait, tv, slice(0, HP), k, HP)
            dve.sem_inc(base, 1)
            both = [[x[:, j * 512:(j + 1) * 512] for x in tv] for j in range(2)]
            s = 0
            for pair in DVE_PAIRS:
                for w in LEVELS:
                    below, odd = slice(w, 2 * w - 1, 2), slice(w + 1, 2 * w, 2)
                    for j, k in enumerate(pair):
                        powers_of_squares(s + j, k, w)
                    for j, k in enumerate(pair):
                        z = [x[:, chunk(k), 1:2].to_broadcast([P, HC, w // 2]) for x in (pw_re, pw_im)]
                        dve.wait_ge(evens, 2 * (s + j + 1))
                        products(V, link, odd_tmp(w, both[j]), pw_re[:, chunk(k), below], pw_im[:, chunk(k), below], *z)
                    for j, k in enumerate(pair):
                        t = odd_tmp(w, both[j])
                        dve.wait_ge(dve_c, n[0] - 4 * (1 - j))
                        V.tensor_tensor(pw_re[:, chunk(k), odd], t[0], t[1], ALU.subtract).then_inc(level, 1)
                        V.tensor_tensor(pw_im[:, chunk(k), odd], t[2], t[3], ALU.add).then_inc(level, 1)
                    s += 2
                h = slice(pair[0] * HC, (pair[1] + 1) * HC)
                dve.wait_ge(level, 2 * s)
                powers_of_w(V, link, wait, tv, h, 2 * HC)
                if s == len(LEVELS) * 2:
                    dve.wait_ge(g_negated, 2)
                for j, k in enumerate(pair):
                    factor_products(V, link, both[j], k)
                for j, k in enumerate(pair):
                    dve.wait_ge(dve_c, n[0] - (4 if j == 0 else 2))
                    factor_sums(V, link, both[j], k)
                    dve.wait_ge(dve_c, n[0])
                    dve.sem_inc(tab[k], 1)

        @block.gpsimd
        def _(pool):
            n = [0]

            def link(ins):
                n[0] += 1
                ins.then_inc(pool_c, 1)

            def wait():
                pool.wait_ge(pool_c, n[0])

            nc.gpsimd.memset(zero, 0.0).then_inc(zero_made, 1)
            nc.gpsimd.memset(ident[:], 0.0).then_inc(ident_made, 1)
            pool.wait_ge(ident_made, 1)
            nc.gpsimd.affine_select(out=ident[:], in_=ident[:], compare_op=ALU.not_equal, fill=1.0, base=0,
                                    pattern=[[-1, P]], channel_multiplier=1).then_inc(ident_made, 1)
            pool.wait_ge(b_doubled, 2)
            pool.wait_ge(loads[5], 16)
            n_half = HP // 2
            t8 = [x[:, 0:n_half * B].rearrange("p (h c) -> p h c", c=B) for x in tp]
            for h in (slice(0, n_half), slice(n_half, HP)):
                bb = lambda x: x[:, h].unsqueeze(2).to_broadcast([P, n_half, B])
                cmul(nc.gpsimd, link, wait, t8, g_re[:, h], g_im[:, h], c_in[:, 0, h], c_in[:, 1, h], bb(b_re), bb(b_im))
            pool.sem_inc(g_made, 1)
            pool.wait_ge(base, 1)
            for k in POOL_CHUNKS:
                for w in LEVELS:
                    powers(nc.gpsimd, link, wait, tp, chunk(k), w, HC)
                pool.wait_ge(g_negated, 2)
                left_factors(nc.gpsimd, link, wait, tp, k)
                pool.sem_inc(tab[k], 1)

        @block.tensor
        def _(pe):
            for k in range(NCHUNK):
                pe.wait_ge(tab[k], 1)
                if k == 0:
                    pe.wait_ge(g_copied, 2)
                if k >= 4:
                    pe.wait_ge(evac, 2 * (k - 3))
                for half in range(2):
                    r = slice(64 * half, 64 * half + 64)
                    for i in range(HC):
                        h, j, g = k * HC + i, i % 4, i // 4
                        out = psK[32 * j:32 * j + 32, half, k % 4, g * NB:(g + 1) * NB]
                        pe.matmul(out, l_re[r, h].rearrange("p c a -> p (c a)"), pw_re[r, h, 0:NB],
                                  start=True, stop=False)
                        mm = pe.matmul(out, l_im[r, h].rearrange("p c a -> p (c a)"), pw_im[r, h, 0:NB],
                                       start=False, stop=True)
                    mm.then_inc(summed, 1)


def ln_stats(V, dve, sem, seen, tiles, st, mv, rstd, nmr, fillers=0, filler=None, between=None):
    n = len(tiles)
    left = [fillers]
    rstd, nmr = rstd[:, 0:n], nmr[:, 0:n]
    diff, total, sq, var, half = (mv[:, j, 0:n] for j in range(5))
    mean_e, sq_e, mean_o, sq_o = (st[:, 0:n, j] for j in (1, 2, 4, 5))
    for j, x in enumerate(tiles):
        if j == TB and between:
            between()
        V.bn_stats(st[:, j, :], x).then_inc(sem, 1)

    def after_last(k):
        if left[0]:
            left[0] -= 1
            filler()
        dve.wait_ge(sem, seen + k)

    after_last(n)
    V.tensor_tensor(diff, mean_e, mean_o, ALU.subtract).then_inc(sem, 1)
    V.tensor_tensor(total, mean_e, mean_o, ALU.add).then_inc(sem, 1)
    V.tensor_tensor(sq, sq_e, sq_o, ALU.add).then_inc(sem, 1)
    after_last(n + 3)
    V.scalar_tensor_tensor(out=diff, in0=diff, scalar=0.25, in1=diff, op0=ALU.mult, op1=ALU.mult).then_inc(sem, 1)
    V.tensor_scalar(sq, sq, 1.0 / D, EPS, ALU.mult, ALU.add).then_inc(sem, 1)
    k = n + 5
    after_last(k)
    V.tensor_tensor(var, sq, diff, ALU.add).then_inc(sem, 1)
    after_last(k + 1)
    V.tensor_scalar(half.bitcast(I32), var.bitcast(I32), 1, None, ALU.logical_shift_right).then_inc(sem, 1)
    after_last(k + 2)
    V.tensor_scalar(rstd.bitcast(U32), half.bitcast(I32), -1.0, RSQRT_SEED, ALU.mult, ALU.add).then_inc(sem, 1)
    k += 3
    for _ in range(3):
        after_last(k)
        V.scalar_tensor_tensor(out=half, in0=rstd, scalar=0.5, in1=rstd, op0=ALU.mult, op1=ALU.mult).then_inc(sem, 1)
        after_last(k + 1)
        V.tensor_tensor(half, half, var, ALU.mult).then_inc(sem, 1)
        after_last(k + 2)
        V.scalar_tensor_tensor(out=rstd, in0=half, scalar=1.5, in1=rstd, op0=ALU.subtract, op1=ALU.mult).then_inc(sem, 1)
        k += 3
    after_last(k)
    V.scalar_tensor_tensor(out=nmr, in0=total, scalar=-0.5, in1=rstd, op0=ALU.mult, op1=ALU.mult).then_inc(sem, 1)
    assert k + 1 == ln_signals(n) and left[0] == 0


def ln_signals(n):
    return n + 18


W1_BEFORE_RET, W1_BEFORE_R, W2_BEFORE_H1 = 1, 4, 4
GELU_BEFORE_TANH, GELU_BEFORE_N2, GELU_BEFORE_X, GELU_BEFORE_COPIES = 1, 2, 3, 5
SPLITS_AFTER_SCAN, SPLITS_IN_LN = 2, 3
ONE, TWO = ln_signals(TB), ln_signals(2 * TB)


def attn_phase(nc, io, scratch, per, xs):
    H, zT, ident, gate_w = per["H"], per["zT"], per["ident"], per["gate_w"]
    rz, nmz, rt, scat = per["rz"], per["nmz"], per["route"], per["scattered"]
    lg_rows, ring = rt["lg"], rt["ring"]
    with ExitStack() as ctx:
        sb = lambda name, shape, dt=F32: ctx.enter_context(nc.sbuf_tensor(name, shape, dt))
        sem = lambda name: ctx.enter_context(nc.semaphore(name))
        raw = per["raw"]
        ret_raw, w1_raw, w2_raw = (raw[:, a:b].rearrange("p (k n) -> p k n", n=n)
                                   for a, b, n in ((0, DC * D, D), (DC * D, DC * (D + F_ATT), F_ATT),
                                                   (DC * (D + F_ATT), DC * (D + F_ATT) + FB * D, D)))
        ret_w = [sb(f"ret_w{j}", [P, DC, D], FR) for j in range(2)]
        w1 = [sb(f"w1_{j}", [P, DC, F_ATT], FR) for j in range(2)]
        w2 = [sb(f"w2_{j}", [P, FB, D], FR) for j in range(2)]
        cols = sb("cols", [P, 5, DC])
        b1 = sb("b1", [P, FB])
        ln2s = sb("ln2s", [P, D])
        ln2b = sb("ln2b", [P, D])
        halves = sb("halves", [P, SEQ])
        primer = sb("primer", [1, 1])
        xn = sb("xn", [P, TB, D])
        xT = sb("xT", [P, DC, SEQ])
        x_hi = sb("x_hi", [P, DC, SEQ], FR)
        x_lo = sb("x_lo", [P, DC, SEQ], FR)
        th = sb("th", [P, DC, SEQ])
        ret = sb("ret", [P, DC, SEQ])
        h1n = sb("h1n", [P, TB, D])
        h1T = [sb(f"h1T{q}", [P, DC, SEQ]) for q in range(2)]
        h1_hi = sb("h1_hi", [P, DC, SEQ], FR)
        h1_lo = sb("h1_lo", [P, DC, SEQ], FR)
        NG = 6
        g = [sb(f"g{j}", [P, SEQ]) for j in range(NG)]
        sh_w = per["sh_w"]
        g_hi, g_lo = (w[:].rearrange("p (f s) -> p f s", f=FB) for w in sh_w)
        r2T = sb("r2T", [P, DC, SEQ])
        n2 = sb("n2", [P, TB, D])
        zn = sb("zn", [P, TB, D])
        lg_feat = sb("lg_feat", [NE, SEQ])
        st = [sb(f"st{j}", [P, 2 * TB, 6]) for j in range(2)]
        mv = [sb(f"mv{j}", [P, 5, 2 * TB]) for j in range(2)]
        rs = [sb(f"rs{j}", [P, 2 * TB]) for j in range(2)]
        nm = [sb(f"nm{j}", [P, 2 * TB]) for j in range(2)]

        pm = lambda name: ctx.enter_context(nc.psum_tensor(name, [P, 2, 512], F32))
        psX, psY, psF, psG = pm("psX"), pm("psY"), pm("psF"), pm("psG")
        rowsY = psY[:].rearrange("p a b -> p (a b)")
        tokY = [rowsY[:, D * t:D * (t + 1)] for t in range(TB)]
        X = psX[:, :, 0:SEQ]
        Y = psY[:, :, 0:SEQ]
        LG = psG[:, 0, 0:TB * NE].rearrange("p (t e) -> p t e", e=NE)

        consts = [sem(f"const{j}") for j in range(5)]
        h_loaded = sem("h_loaded")
        next_loaded, sh_high = sem("next_loaded"), sem("sh_high")
        w_high, w_low = sem("w_high"), sem("w_low")
        b_ret_halved, halves_made = sem("b_ret_halved"), sem("halves_made")
        ln_a, ln_b, stats_kept = sem("ln_a"), sem("ln_b"), sem("stats_kept")
        x_ready, x_turned, x_copied, x_split = sem("x_ready"), sem("x_turned"), sem("x_copied"), sem("x_split")
        ret_mm, tanh_done, scanned, r_ready = sem("ret_mm"), sem("tanh_done"), sem("scanned"), sem("r_ready")
        r_turned, h1n_ready, h1_turned, h1_copied = sem("r_turned"), sem("h1n_ready"), sem("h1_turned"), sem("h1_copied")
        h1_split, w1_mm, gelu, g_split = sem("h1_split"), sem("w1_mm"), sem("gelu"), sem("g_split")
        w2_mm, r2_ready, r2_turned, n2_ready = sem("w2_mm"), sem("r2_ready"), sem("r2_turned"), sem("n2_ready")
        n2_scaled, h_biased, h_new = sem("n2_scaled"), sem("h_biased"), sem("h_new")
        z_ready, z_turned, z_copied = sem("z_ready"), sem("z_turned"), sem("z_copied")
        masks_made, route_step, r_exp, counted, prefix = sem("masks_made"), sem("route"), sem("r_exp"), sem("counted"), sem("prefix")
        routed, z_rows = sem("routed_first"), sem("z_rows_first")
        lg_mm, lg_copied, lg_turned, lg_kept = sem("lg_mm"), sem("lg_copied"), sem("lg_turned"), sem("lg_kept")
        block = ctx.enter_context(nc.Block())
        V, A, G, T = nc.vector, nc.scalar, nc.gpsimd, nc.tensor

        Ht = lambda b, t: H[:, bass.ds(b * TB + t, 1), :].rearrange("p o d -> p (o d)")
        Hb = lambda b: H[:, bass.ds(b * TB, TB), :]

        slice_of = lambda x, b: x[:, bass.ds(b * TB, TB)]

        def iterations(eng, step):
            step(0, 0), step(1, 1), step(2, 0)
            with eng.Fori(0, (B - 4) // 2) as pair:
                step(pair * 2 + 3, 1)
                step(pair * 2 + 4, 0)
            for i in range(B - 1, B + 3):
                step(i, i % 2)

        at = lambda i, n: type(i) is int and i == n

        def parts(i):
            if type(i) is not int:
                return (True,) * 5
            return tuple(0 <= i + d < B for d in (0, -1, -2, -3, 1))

        def signals_a(i):
            if type(i) is not int:
                return i * TWO + (2 * ONE - 2 * TWO)
            return sum(ln_signals(TB * (parts(j)[0] + parts(j)[2])) if parts(j)[0] or parts(j)[2] else 0
                       for j in range(i))

        def signals_b(i):
            if type(i) is not int:
                return i * TWO + (3 * ONE - 2 * TWO)
            return ONE + sum(ln_signals(TB * (parts(j)[4] + parts(j)[2])) if parts(j)[4] or parts(j)[2] else 0
                             for j in range(i))

        @block.sync
        def _(sp):
            sp.dma_start(ln2s[:], io["ln2_scale"].to_broadcast([P, D])).then_inc(consts[0], 16)
            for b in range(B):
                for t in range(S_SSM // P):
                    sp.dma_start(H[:, b * TB + t, :], scratch[t * P:(t + 1) * P, b, :]).then_inc(h_loaded, 16)
                sp.dma_start(H[:, b * TB + TB - 1, :], io["txt"][b]).then_inc(h_loaded, 16)
                sp.wait_ge(h_loaded, 16 * TB * (b + 1))
                if b == 0:
                    sp.dma_start(ln2b[:], io["ln2_bias"].to_broadcast([P, D])).then_inc(consts[1], 16)
            sp.wait_ge(w_low, 3)
            sp.dma_start(raw[:, 0:W_SH], io["sh_w"]).then_inc(next_loaded, 16)
            sp.dma_start(raw[:, W_SH:W_SH + W_EX], io["ex_w"][0]).then_inc(next_loaded, 16)
            sp.wait_ge(next_loaded, 32)

        @block.gpsimd
        def _(pool):
            G.memset(halves[:], 0.5).then_inc(halves_made, 1)
            for e in range(NE):
                G.memset(rt["desc"][:, :, e:e + 1], float(NE - e)).then_inc(masks_made, 1)
            G.memset(rt["ones"][:], 1.0).then_inc(masks_made, 1)
            G.memset(rt["below"][:], 1.0).then_inc(masks_made, 1)
            pool.wait_ge(masks_made, NE + 2)
            G.affine_select(out=rt["below"][:], in_=rt["below"][:], compare_op=ALU.is_gt, fill=0.0, base=0,
                            pattern=[[1, P]], channel_multiplier=-1).then_inc(masks_made, 1)
            pool.wait_ge(consts[0], 16)
            pool.wait_ge(consts[1], 16)

            def scatter_rows(b):
                pool.wait_ge(z_rows, b + 1)
                scatter(G, xs, ring, rt["slot_in"], b, scat)

            def step(i, q):
                front, mid, tail, last, more = parts(i)
                f, m, t = i, i - 1, i - 2
                if front:
                    pool.wait_ge(x_ready, f + 1)
                    pool.wait_ge(consts[1], 16)
                    G.tensor_tensor(Hb(f), Hb(f), ln2b[:].unsqueeze(1).to_broadcast([P, TB, D]), ALU.add)\
                        .then_inc(h_biased, 1)
                if tail:
                    pool.wait_ge(n2_ready, t + 1)
                    G.tensor_tensor(n2[:], n2[:], ln2s[:].unsqueeze(1).to_broadcast([P, TB, D]), ALU.mult)\
                        .then_inc(n2_scaled, 1)
                if at(i, B + 1):
                    pool.wait_ge(routed, 1)
                    scatter_rows(0)

            iterations(pool, step)
            for b in range(1, SCATTERED_FIRST):
                scatter_rows(b)

        @block.vector
        def _(dve):
            def weights_low(n, w, w_raw):
                dve.wait_ge(w_high, n)
                V.tensor_tensor(w[1][:], w_raw, w[0][:].bitcast(F32), ALU.subtract).then_inc(w_low, 1)

            def g_low(b, f):
                dve.wait_ge(gelu, b * (2 * FB) + (2 * f + 2))
                V.tensor_tensor(g_lo[:, f, :], g[f % NG][:], g_hi[:, f, :].bitcast(F32), ALU.subtract)\
                    .then_inc(g_split, 1)

            def residual(b, q, k):
                dve.wait_ge(w2_mm, b * DC + k + 1)
                V.scalar_tensor_tensor(out=r2T[:, k, :], in0=psG[:, k, 0:SEQ], scalar=cols[:, 3, k:k + 1],
                                       in1=h1T[q][:, k, :], op0=ALU.add, op1=ALU.add).then_inc(r2_ready, 1)

            links = [0]

            def link(ins):
                links[0] += 1
                ins.then_inc(route_step, 1)
                dve.wait_ge(route_step, links[0])

            scores, choose, place = router(V, dve, link, rt, 0, ROUTED_FIRST * TB, psF[:, 0, :], r_exp, counted, prefix)

            def shared_low():
                dve.wait_ge(sh_high, 1)
                V.tensor_tensor(sh_w[1][:], raw[:, 0:W_SH], sh_w[0][:].bitcast(F32), ALU.subtract)

            def x_low(b):
                dve.wait_ge(x_copied, b + 1)
                V.tensor_tensor(x_lo[:], X, x_hi[:].bitcast(F32), ALU.subtract).then_inc(x_split, 1)
                V.tensor_scalar(xT[:], X, 0.5, None, ALU.add).then_inc(x_split, 1)

            def h1_low(b, q, k):
                dve.wait_ge(h1_copied, b * (2 * DC) + (2 * k + 2))
                V.tensor_tensor(h1_lo[:, k, :], h1T[q][:, k, :], h1_hi[:, k, :].bitcast(F32), ALU.subtract).then_inc(h1_split, 1)

            def step(i, q):
                front, mid, tail, last, more = parts(i)
                f, m, t = i, i - 1, i - 2
                split = [0]

                def splits(n=1):
                    if mid:
                        for k in range(split[0], min(FB, split[0] + n)):
                            g_low(m, k)
                        split[0] += n

                if at(i, B - 1):
                    dve.wait_ge(lg_kept, ROUTED_FIRST)
                    scores()
                if at(i, B):
                    dve.wait_ge(masks_made, NE + 3)
                    choose()
                if tail or more:
                    tiles = []
                    if tail:
                        dve.wait_ge(r2_turned, t + 1)
                        tiles += tokY
                    if more:
                        dve.wait_ge(h_loaded, (f + 2) * (16 * TB))
                        tiles += [Ht(f + 1, j) for j in range(TB)]
                    ln_stats(V, dve, ln_b, signals_b(i), tiles, st[1], mv[1], rs[1], nm[1],
                             3 if mid and not front else 0, splits)
                if front:
                    for k in range(DC):
                        dve.wait_ge(tanh_done, f * DC + (k + 1))
                        V.tensor_tensor_scan(ret[:, k, :], halves[:], th[:, k, :], -2.0, ALU.mult, ALU.add).then_inc(scanned, 1)
                    dve.wait_ge(x_split, (f + 1) * 2)
                    dve.wait_ge(scanned, (f + 1) * DC)
                    V.scalar_tensor_tensor(out=ret[:], in0=ret[:], scalar=0.25, in1=xT[:], op0=ALU.mult, op1=ALU.add)\
                        .then_inc(r_ready, 1)
                if at(i, 0):
                    weights_low(2, w1, w1_raw)
                if at(i, 1):
                    weights_low(3, w2, w2_raw)
                splits(SPLITS_AFTER_SCAN if front else FB)
                if at(i, B + 1):
                    place(0)
                    place(1)
                    dve.sem_inc(routed, 1)

                def new_h():
                    dve.wait_ge(n2_scaled, t + 1)
                    dve.wait_ge(h_biased, t + 1)
                    V.tensor_tensor(Hb(t), Hb(t), n2[:], ALU.add).then_inc(h_new, 1)
                    dve.wait_ge(h_new, t + 1)
                    if front:
                        splits()

                if front or tail:
                    tiles = []
                    if front:
                        dve.wait_ge(r_turned, f + 1)
                        tiles += tokY
                    if tail:
                        tiles += [Ht(t, j) for j in range(TB)]
                        if not front:
                            new_h()
                    ln_stats(V, dve, ln_a, signals_a(i), tiles, st[0], mv[0], rs[0], nm[0], 
                             SPLITS_IN_LN if mid and front else 0, splits, new_h if tail and front else None)
                splits(FB)
                if more:
                    x_low(f + 1)
                if mid:
                    residual(m, 1 - q, 0)
                if tail:
                    o = TB if front else 0
                    dve.wait_ge(ln_a, signals_a(i) + (TWO if front else ONE))
                    V.tensor_copy(slice_of(rz, t), rs[0][:, o:o + TB])
                    V.tensor_copy(slice_of(nmz, t), nm[0][:, o:o + TB]).then_inc(stats_kept, 1)
                if front:
                    h1_low(f, q, 0)
                if front:
                    h1_low(f, q, 1)
                if mid:
                    residual(m, 1 - q, 1)

            dve.wait_ge(h_loaded, 16 * TB)
            ln_stats(V, dve, ln_b, 0, [Ht(0, j) for j in range(TB)], st[1], mv[1], rs[1], nm[1])
            weights_low(1, ret_w, ret_raw)
            dve.wait_ge(consts[2], 16)
            V.tensor_scalar(cols[:, 4, :], cols[:, 0, :], 0.5, None, ALU.mult).then_inc(b_ret_halved, 1)
            dve.wait_ge(halves_made, 1)
            x_low(0)
            iterations(dve, step)
            shared_low()

        @block.scalar
        def _(act):
            act.dma_start(cols[:, 0:4, :], io["cols"]).then_inc(consts[2], 16)
            act.dma_start(b1[:], io["b1"]).then_inc(consts[3], 16)
            act.dma_start(gate_w[:], io["gate_w"]).then_inc(consts[4], 16)
            A.activation(primer[:], ident[0:1, 0:1], ACT.Gelu_apprx_tanh)
            A.activation(ret_w[0][:], ret_raw, ACT.Copy).then_inc(w_high, 1)

            def normalise(out, src, group, j):
                return A.activation(out, src, ACT.Identity, bias=nm[group][:, j:j + 1], scale=rs[group][:, j:j + 1])

            def x_of(b, signals, o):
                act.wait_ge(ln_b, signals)
                if type(b) is not int or b >= 1:
                    act.wait_ge(x_turned, b)
                for j in range(TB):
                    a = normalise(xn[:, j, :], Ht(b, j), 1, o + j)
                a.then_inc(x_ready, 1)

            def gelu_of(b, f, first):
                act.wait_ge(w1_mm, b * FB + f + 1)
                if f >= NG or not first:
                    act.wait_ge(g_split, b * FB + (f - NG + 1))
                for out in (g[f % NG][:], g_hi[:, f, :]):
                    A.activation(out, psF[:, f % 2, 0:SEQ], ACT.Gelu_apprx_tanh, bias=b1[:, f:f + 1]).then_inc(gelu, 1)

            def x_high(b):
                act.wait_ge(x_turned, b + 1)
                A.activation(x_hi[:], X, ACT.Copy).then_inc(x_copied, 1)

            def h1_of(q, k):
                for out in (h1T[q][:, k, :], h1_hi[:, k, :]):
                    A.activation(out, X[:, k, :], ACT.Identity, bias=cols[:, 2, k:k + 1],
                                 scale=cols[:, 1, k:k + 1]).then_inc(h1_copied, 1)

            def step(i, q):
                front, mid, tail, last, more = parts(i)
                f, m, t = i, i - 1, i - 2
                first = at(i, 1)
                if at(i, B - 1):
                    act.wait_ge(route_step, 2)
                    A.activation(rt["sc"][:, 0:ROUTED_FIRST * TB, :], lg_rows[:, 0:ROUTED_FIRST * TB, :], ACT.Exp).then_inc(r_exp, 1)
                    A.activation(primer[:], ident[0:1, 0:1], ACT.Gelu_apprx_tanh)
                if mid:
                    for k in range(GELU_BEFORE_TANH if front else 0):
                        gelu_of(m, k, first)
                if front:
                    act.wait_ge(ret_mm, f + 1)
                    for k in range(DC):
                        A.activation(th[:, k, :], X[:, k, :], ACT.Tanh, bias=cols[:, 4, k:k + 1], scale=0.5)\
                            .then_inc(tanh_done, 1)
                if at(i, 0):
                    A.activation(w2[0][:], w2_raw, ACT.Copy).then_inc(w_high, 1)
                if mid:
                    for k in range(GELU_BEFORE_TANH if front else 0, GELU_BEFORE_N2 if front else FB):
                        gelu_of(m, k, first)
                if tail:
                    act.wait_ge(ln_b, signals_b(i) + (TWO if more else ONE))
                    for j in range(TB):
                        a = normalise(n2[:, j, :], tokY[j], 1, j)
                    a.then_inc(n2_ready, 1)
                if at(i, B + 1):
                    act.wait_ge(next_loaded, 32)
                    act.wait_ge(w2_mm, B * DC)
                    A.activation(sh_w[0][:], raw[:, 0:W_SH], ACT.Copy).then_inc(sh_high, 1)
                if mid and front:
                    for k in range(GELU_BEFORE_N2, GELU_BEFORE_X):
                        gelu_of(m, k, first)
                if more:
                    x_of(f + 1, signals_b(i) + (TWO if tail else ONE), TB if tail else 0)
                if mid and front:
                    for k in range(GELU_BEFORE_X, GELU_BEFORE_COPIES):
                        gelu_of(m, k, first)
                if more:
                    x_high(f + 1)
                if mid and front:
                    for k in range(GELU_BEFORE_COPIES, FB):
                        gelu_of(m, k, first)
                if at(i, B):
                    z_staging()
                if front:
                    act.wait_ge(ln_a, signals_a(i) + (TWO if tail else ONE))
                    for j in range(TB):
                        a = normalise(h1n[:, j, :], tokY[j], 0, j)
                    a.then_inc(h1n_ready, 1)
                if tail:
                    if not front:
                        act.wait_ge(ln_a, signals_a(i) + ONE)
                    if type(i) is not int or i >= 3:
                        act.wait_ge(z_turned, t)
                    for j in range(TB):
                        a = normalise(zn[:, j, :], Ht(t, j), 0, (TB if front else 0) + j)
                    a.then_inc(z_ready, 1)
                if front:
                    act.wait_ge(h1_turned, f + 1)
                    h1_of(q, 0)
                    h1_of(q, 1)
                if tail:
                    act.wait_ge(z_turned, t + 1)
                    A.activation(zT[:, :, bass.ds(t * SEQ, SEQ)], Y if front else X, ACT.Copy).then_inc(z_copied, 1)
                if last:
                    act.wait_ge(lg_mm, t)
                    A.activation(lg_feat[:], psG[0:NE, 0, 0:SEQ], ACT.Copy).then_inc(lg_copied, 1)
                if last:
                    act.wait_ge(lg_turned, t)
                    A.activation(lg_rows[:, bass.ds((t - 1) * TB, TB), :], LG, ACT.Copy).then_inc(lg_kept, 1)

            def z_staging():
                for b in range(ROUTED_FIRST):
                    act.wait_ge(stats_kept, b + 1)
                    for j in range(TB):
                        n = b * TB + j
                        a = A.activation(z_staged(ring, b, j), H[:, n, :], ACT.Identity, bias=nmz[:, n:n + 1], scale=rz[:, n:n + 1])
                    a.then_inc(z_rows, 1)

            for j in (3, 4):
                act.wait_ge(consts[j], 16)
            x_of(0, ONE, 0)
            x_high(0)
            A.activation(w1[0][:], w1_raw, ACT.Copy).then_inc(w_high, 1)
            act.wait_ge(b_ret_halved, 1)
            iterations(act, step)

        @block.tensor
        def _(pe):
            def to_features(src, ps):
                for t in range(TB):
                    for k in range(DC):
                        mm = T.transpose(ps[:, k, t * P:(t + 1) * P], src[:, t, k * P:(k + 1) * P], ident[:])
                return mm

            def to_tokens(src):
                for t in range(TB):
                    for k in range(DC):
                        mm = T.transpose(rowsY[:, t * D + k * P:t * D + (k + 1) * P], src[:, k, t * P:(t + 1) * P], ident[:])
                return mm

            def product(out, w, cols_, act_hi, act_lo, first, last):
                T.matmul(out, w[0][cols_], act_hi, start=first, stop=False)
                T.matmul(out, w[0][cols_], act_lo, start=False, stop=False)
                return T.matmul(out, w[1][cols_], act_hi, start=False, stop=last)

            def hidden(b, f, first):
                if f >= 2 or not first:
                    pe.wait_ge(gelu, b * (2 * FB) + (2 * f - 2))
                for k in range(DC):
                    mm = product(psF[:, f % 2, 0:SEQ], w1, (slice(None), k, slice(f * P, (f + 1) * P)),
                                 h1_hi[:, k, :], h1_lo[:, k, :], k == 0, k == DC - 1)
                mm.then_inc(w1_mm, 1)

            def down(b, n, ks):
                for k in ks:
                    if n == 0:
                        pe.wait_ge(g_split, b * FB + k + 1)
                    mm = product(psG[:, n, 0:SEQ], w2, (slice(None), k, slice(n * P, (n + 1) * P)),
                                 g_hi[:, k, :], g_lo[:, k, :], k == 0, k == FB - 1)
                if k == FB - 1:
                    mm.then_inc(w2_mm, 1)

            def step(i, q):
                front, mid, tail, last, more = parts(i)
                f, m, t = i, i - 1, i - 2
                first = at(i, 1)
                if mid:
                    if at(i, 1):
                        pe.wait_ge(w_low, 2)
                    pe.wait_ge(h1_split, (m + 1) * DC)
                    for k in range(W1_BEFORE_RET):
                        hidden(m, k, first)
                if front:
                    pe.wait_ge(x_split, (f + 1) * 2)
                    if mid:
                        pe.wait_ge(h1_copied, f * (2 * DC))
                    for n in range(DC):
                        for k in range(DC):
                            mm = product(psX[:, n, 0:SEQ], ret_w, (slice(None), k, slice(n * P, (n + 1) * P)),
                                         x_hi[:, k, :], x_lo[:, k, :], k == 0, k == DC - 1)
                    mm.then_inc(ret_mm, 1)
                if mid:
                    for k in range(W1_BEFORE_RET, W1_BEFORE_R):
                        hidden(m, k, first)
                if front:
                    pe.wait_ge(r_ready, f + 1)
                    if tail:
                        pe.wait_ge(n2_ready, t + 1)
                    to_tokens(ret).then_inc(r_turned, 1)
                if mid:
                    for k in range(W1_BEFORE_R, 5):
                        hidden(m, k, first)
                if more:
                    pe.wait_ge(x_ready, f + 2)
                    if front:
                        pe.wait_ge(tanh_done, (f + 1) * DC)
                    to_features(xn, psX).then_inc(x_turned, 1)
                if mid:
                    if tail:
                        pe.wait_ge(r2_ready, m * DC)
                    if parts(i - 1)[3]:
                        pe.wait_ge(lg_kept, t - 1)
                    hidden(m, 5, first)
                    if at(i, 1):
                        pe.wait_ge(w_low, 3)
                    down(m, 0, range(0, 3))
                    hidden(m, 6, first)
                    down(m, 0, range(3, 5))
                    hidden(m, 7, first)
                    down(m, 0, range(5, 8))
                    if at(i, B):
                        pe.wait_ge(gelu, (m + 1) * (2 * FB))
                        pe.wait_ge(counted, 1)
                        places(T, psF[:, 0, :], rt, 0, ROUTED_FIRST * TB).then_inc(prefix, 1)
                    down(m, 1, range(0, W2_BEFORE_H1))
                if front:
                    pe.wait_ge(h1n_ready, f + 1)
                    if more:
                        pe.wait_ge(x_split, (f + 2) * 2)
                    to_features(h1n, psX).then_inc(h1_turned, 1)
                if mid:
                    down(m, 1, range(W2_BEFORE_H1, FB))

                def ffn_rows():
                    pe.wait_ge(r2_ready, (m + 1) * DC)
                    if tail and front:
                        pe.wait_ge(z_copied, t + 1)
                    elif tail:
                        pe.wait_ge(n2_ready, t + 1)
                    elif front:
                        pe.wait_ge(h1n_ready, f + 1)
                    to_tokens(r2T).then_inc(r2_turned, 1)

                if mid and not front:
                    ffn_rows()
                if tail:
                    if not front and not mid:
                        pe.wait_ge(z_copied, t)
                    pe.wait_ge(z_ready, t + 1)
                    to_features(zn, psY if front else psX).then_inc(z_turned, 1)
                if last:
                    pe.wait_ge(z_copied, t)
                    if mid:
                        pe.wait_ge(r2_ready, m * DC + 1)
                    else:
                        pe.wait_ge(lg_kept, t - 1)
                    for k in range(DC):
                        mm = T.matmul(psG[0:NE, 0, 0:SEQ], gate_w[:, k, :], zT[:, k, bass.ds((t - 1) * SEQ, SEQ)],
                                      start=(k == 0), stop=(k == DC - 1))
                    mm.then_inc(lg_mm, 1)
                    pe.wait_ge(lg_copied, t)
                if mid and front:
                    ffn_rows()
                if last:
                    for j in range(TB):
                        mm = T.transpose(LG[:, j, :], lg_feat[:, j * P:(j + 1) * P], ident[0:NE, 0:NE])
                    mm.then_inc(lg_turned, 1)

            pe.wait_ge(consts[4], 16)
            pe.wait_ge(x_ready, 1)
            to_features(xn, psX).then_inc(x_turned, 1)
            pe.wait_ge(w_low, 1)
            iterations(pe, step)


def route_buffers(sb):
    row = lambda name, dt=F32: sb(name, [P, NT, NE], dt)
    col = lambda name: sb(name, [P, NT])
    return dict(
        lg=row("lg"), sc=row("sc"), tmp=row("r_tmp"), oh=[row(f"oh{k}") for k in range(TOPK)], desc=row("desc"),
        cnt=row("cnt", BF16), below=sb("below", [P, P], BF16), ones=sb("ones", [P, P], BF16),
        mx=col("r_max"), sm=col("r_sum"), den=col("r_den"),
        top=[col(f"top{k}") for k in range(TOPK)], who=[col(f"who{k}") for k in range(TOPK)],
        pos=[col(f"pos{k}") for k in range(TOPK)], keep=[col(f"keep{k}") for k in range(TOPK)],
        wgt=[col(f"wgt{k}") for k in range(TOPK)],
        slot_in=sb("slot_in", [P, TOPK, NT], U32), slot_out=sb("slot_out", [P, TOPK, NT], U32),
        ring=[sb(f"ring{q}", [P, TB, TOPK, D]) for q in range(2)])


def router(V, dve, link, rt, t0, t1, ps, exp_done, counted, prefix):
    n = t1 - t0
    row = lambda name: rt[name][:, t0:t1, :]
    col = lambda x: x[:, t0:t1]
    bc = lambda x: col(x).unsqueeze(2).to_broadcast([P, n, NE])
    lg, sc, tmp = row("lg"), row("sc"), row("tmp")
    oh = [x[:, t0:t1, :] for x in rt["oh"]]
    sm, den = rt["sm"], rt["den"]
    top, who, pos, keep, wgt = (rt[x] for x in ("top", "who", "pos", "keep", "wgt"))

    def scores():
        link(V.tensor_reduce(col(rt["mx"]), lg, AX.X, ALU.max))
        link(V.tensor_tensor(lg, lg, bc(rt["mx"]), ALU.subtract))

    def choose():
        dve.wait_ge(exp_done, 1)
        link(V.tensor_reduce(col(sm), sc, AX.X, ALU.add))
        link(V.reciprocal(col(sm), col(sm)))
        link(V.tensor_tensor(sc, sc, bc(sm), ALU.mult))
        for k in range(TOPK):
            link(V.tensor_reduce(col(top[k]), sc, AX.X, ALU.max))
            link(V.tensor_tensor(tmp, sc, bc(top[k]), ALU.is_equal))
            link(V.tensor_tensor(tmp, tmp, row("desc"), ALU.mult))
            link(V.tensor_reduce(col(who[k]), tmp, AX.X, ALU.max))
            link(V.tensor_tensor(oh[k], tmp, bc(who[k]), ALU.is_equal))
            if k == 0:
                link(V.scalar_tensor_tensor(out=sc, in0=oh[0], scalar=-2.0, in1=sc, op0=ALU.mult, op1=ALU.add))
        V.tensor_tensor(row("cnt"), oh[0], oh[1], ALU.add).then_inc(counted, 1)
        link(V.tensor_tensor(col(den), col(top[0]), col(top[1]), ALU.add))
        link(V.tensor_scalar(col(den), col(den), 1e-20, None, ALU.add))
        link(V.reciprocal(col(den), col(den)))

    def place(k):
        dve.wait_ge(prefix, 1)
        p, kp, w = col(pos[k]), col(keep[k]), col(wgt[k])
        link(V.tensor_tensor(tmp, oh[k], ps[:, 0:n * NE].rearrange("p (t e) -> p t e", e=NE), ALU.mult))
        link(V.tensor_reduce(p, tmp, AX.X, ALU.add))
        link(V.tensor_scalar(kp, p, float(CAP), None, ALU.is_lt))
        link(V.scalar_tensor_tensor(out=p, in0=col(who[k]), scalar=-float(CAP), in1=p, op0=ALU.mult, op1=ALU.add))
        link(V.tensor_scalar(p, p, float(NE * CAP), None, ALU.add))
        link(V.tensor_tensor(p, p, kp, ALU.mult))
        link(V.tensor_tensor(w, col(top[k]), col(den), ALU.mult))
        link(V.tensor_tensor(w, w, kp, ALU.mult))
        link(V.tensor_copy(rt["slot_out"][:, k, t0:t1], p))
        link(V.tensor_scalar(kp, kp, -float(OUT_OF_RANGE), float(OUT_OF_RANGE), ALU.mult, ALU.add))
        link(V.tensor_tensor(rt["slot_in"][:, k, t0:t1], p, kp, ALU.add))

    return scores, choose, place


def places(T, ps, rt, t0, t1):
    n, cnt = t1 - t0, rt["cnt"]
    mm = T.matmul(ps[:, 0:n * NE], rt["below"][:], cnt[:, t0:t1, :].rearrange("p t e -> p (t e)"), start=True, stop=False)
    for t in range(t1 - 1):
        a = max(t + 1, t0) - t0
        mm = T.matmul(ps[:, a * NE:n * NE], rt["ones"][:], cnt[:, t:t + 1, :].to_broadcast([P, n - a, NE]),
                      start=False, stop=(t == t1 - 2))
    return mm


def z_staged(ring, b, t):
    return ring[b % 2][:, t, (b // 2) % 2, :]


def scatter(G, xs, ring, slot_in, b, done):
    for t in range(TB):
        for k in range(TOPK):
            G.indirect_dma_start(
                out=xs[:, :], out_offset=bass.IndirectOffsetOnAxis(ap=slot_in[:, k, b * TB + t:b * TB + t + 1], axis=0),
                in_=z_staged(ring, b, t), in_offset=None,
                bounds_check=NE * CAP - 1, oob_is_err=False).then_inc(done[b % 4], 16)


def moe_phase(nc, io, per, xs, eo, out):
    H, zT, ident, raw, rt = per["H"], per["zT"], per["ident"], per["raw"], per["route"]
    rz, nmz, ring, scat = per["rz"], per["nmz"], rt["ring"], per["scattered"]
    slot_in, slot_out, wgt = rt["slot_in"], rt["slot_out"], rt["wgt"]
    with ExitStack() as ctx:
        sb = lambda name, shape, dt=F32: ctx.enter_context(nc.sbuf_tensor(name, shape, dt))
        sem = lambda name: ctx.enter_context(nc.semaphore(name))
        ps = lambda name, n: ctx.enter_context(nc.psum_tensor(name, [P, n, 512], F32))
        psGU, psX, psO = ps("psGU", 4), ps("psT", 2), ps("psO", 2)
        rowsO = psO[:].rearrange("p a b -> p (a b)")

        sh_w = per["sh_w"]
        ex_w = [[sb(f"ex_w{q}{j}", [P, W_EX], FR) for j in range(2)] for q in range(2)]
        ex_raw = [raw[:, W_SH:W_SH + W_EX], raw[:, 0:W_EX]]

        rows_of = [x[:] for x in ring] + [raw[:, a:a + TB * TOPK * D].rearrange("p (t k d) -> p t k d", t=TB, k=TOPK)
                                          for a in range(0, W_SH + W_EX, TB * TOPK * D)]
        GATHERS = len(rows_of)

        xin = [sb(f"xin{q}", [XP, 2 * XT, D]) for q in range(2)]
        x_hi = [sb(f"job_x_hi{q}", [P, DC, HALF], FR) for q in range(2)]
        x_lo = [sb(f"job_x_lo{q}", [P, DC, HALF], FR) for q in range(2)]
        silu_g = [sb(f"silu_g{q}", [P, HALF]) for q in range(2)]
        act_a = [sb(f"act_a{q}", [P, HALF]) for q in range(2)]
        a_hi = sb("a_hi", [P, 2 * SB * SEQ], FR)
        a_lo = sb("a_lo", [P, 2 * SB * SEQ], FR)
        y_out = [sb(f"y_out{q}", [XP, XT, D]) for q in range(2)]
        ex_loaded = [sem(f"ex_loaded{q}") for q in range(2)]
        ex_hi, ex_lo = sem("ex_hi"), sem("ex_lo")
        route, r_exp, counted, prefix = sem("route"), sem("r_exp"), sem("counted"), sem("prefix")
        routed, z_rows = sem("routed"), sem("z_rows")
        xin_loaded = [sem(f"xin_loaded{q}") for q in range(2)]
        turned = sem("turned")
        xhi_ready, xlo_ready = sem("xhi_ready"), sem("xlo_ready")
        gu_ready, silu_ready, a_ready, ahi_ready, alo_ready = (
            sem(f"{n}_ready") for n in ("gu", "silu", "a", "ahi", "alo"))
        rows_ready, rows_read = sem("rows_ready"), sem("rows_read")
        y_stored = [sem(f"y_stored{q}") for q in range(2)]
        gath = [sem(f"gathered{q}") for q in range(GATHERS)]
        comb, stored = sem("combined"), sem("out_stored")
        block = ctx.enter_context(nc.Block())
        V, A, G, T = nc.vector, nc.scalar, nc.gpsimd, nc.tensor
        gate = lambda w, n: w[:, 0:DC * n].rearrange("p (k i) -> p k i", k=DC)
        up = lambda w, n: w[:, DC * n:2 * DC * n].rearrange("p (k i) -> p k i", k=DC)
        down = lambda w, n: w[:, 2 * DC * n:].rearrange("p (k d) -> p k d", d=D)
        zT_of = lambda b: zT[:, :, b * SEQ:(b + 1) * SEQ]
        flat_h = H[:].rearrange("p t d -> p (t d)")
        Hb = lambda b: flat_h[:, b * TB * D:(b + 1) * TB * D]
        xs_rows = xs.rearrange("(e t p) d -> e p t d", p=XP, t=2 * XT)
        eo_rows = eo.rearrange("(u t p) d -> u p t d", p=XP, t=XT)

        unit = lambda i, r: i * 4 + r
        expert = lambda i, r: i * 2 + r // 2
        exists = lambda i, r: type(i) is not int or 0 <= unit(i, r) < UNITS
        xin_of = lambda r: r // 2 % 2
        job_s = lambda b: b if b < SH_FIRST else b + UNITS
        job_e = lambda i, r: unit(i, r) + SH_FIRST
        block_s = lambda b: SB * b if b < SH_FIRST else SB * b + EB * UNITS
        block_e = lambda i, r: unit(i, r) * EB + SB * SH_FIRST
        job_q = lambda r: (r + SH_FIRST) % 2

        def units(eng, step):
            step(0, 0), step(0, 1)
            with eng.Fori(0, UNITS // 4 - 1) as i:
                for r in range(2, 6):
                    step(i, r)
            step(UNITS // 4 - 1, 2), step(UNITS // 4 - 1, 3)

        def a_at(blk, width):
            slot = blk % (2 * SB if width == SEQ else 2 * EB)
            return slice(slot * width, (slot + 1) * width)

        def block_slots(r):
            return [(block_e(0, r) + j) % (2 * EB) for j in range(EB)]

        @block.sync
        def _(sp):
            def load_weights(e, q, before):
                if before:
                    sp.wait_ge(ex_lo, e - 1)
                sp.dma_start(ex_raw[q], io["ex_w"][e]).then_inc(ex_loaded[q], 16)

            def load_tokens(e, q, before):
                if before:
                    sp.wait_ge(turned, 2 * e - 2)
                sp.dma_start(xin[q][:], xs_rows[e]).then_inc(xin_loaded[q], 16)

            load_weights(1, 1, False)
            for q in range(4):
                sp.wait_ge(scat[q], 16 * TB * TOPK * (B // 4))
            load_tokens(0, 0, False)
            load_tokens(1, 1, False)
            for u in range(UNITS):
                e = u // 2 + 2
                if u % 2 == 0 and e < NE:
                    load_weights(e, e % 2, True)
                    load_tokens(e, e % 2, True)
                sp.wait_ge(rows_read, job_e(0, u) + 1)
                sp.dma_start(eo_rows[u], y_out[u % 2][:]).then_inc(y_stored[u % 2], 16)
            for b in range(B):
                sp.wait_ge(comb, TB * TOPK * (b + 1))
                sp.dma_start(out[b].rearrange("(t p) d -> p t d", p=P), H[:, b * TB:(b + 1) * TB, :]).then_inc(stored, 16)
            sp.wait_ge(stored, 16 * B)

        @block.gpsimd
        def _(pool):
            for b in range(SCATTERED_FIRST, B):
                if b == ROUTED_FIRST:
                    pool.wait_ge(routed, 1)
                if b >= ROUTED_FIRST:
                    pool.wait_ge(z_rows, b - ROUTED_FIRST + 1)
                scatter(G, xs, ring, slot_in, b, scat)
            for q in range(2):
                pool.wait_ge(y_stored[q], 16 * (UNITS // 2))
            for b in range(B):
                if b >= GATHERS:
                    pool.wait_ge(comb, TB * TOPK * (b - GATHERS + 1))
                for t in range(TB):
                    for k in range(TOPK):
                        G.indirect_dma_start(
                            out=rows_of[b % GATHERS][:, t, k, :], out_offset=None,
                            in_=eo[:, :], in_offset=bass.IndirectOffsetOnAxis(ap=slot_out[:, k, b * TB + t:b * TB + t + 1], axis=0))\
                            .then_inc(gath[b % GATHERS], 16)

        @block.vector
        def _(dve):
            n = [0]

            def link(ins):
                n[0] += 1
                ins.then_inc(route, 1)
                dve.wait_ge(route, n[0])

            scores, choose, place = router(V, dve, link, rt, ROUTED_FIRST * TB, NT, psX[:, 1, :], r_exp, counted, prefix)

            def hidden(blk, par, at, w):
                dve.wait_ge(silu_ready, blk + 1)
                V.tensor_tensor(act_a[par][:, 0:w], silu_g[par][:, 0:w], psGU[:, 2 * par + 1, 0:w], ALU.mult).then_inc(a_ready, 1)
                dve.wait_ge(a_ready, blk + 1)
                V.tensor_copy(a_hi[:, at], act_a[par][:, 0:w]).then_inc(ahi_ready, 1)
                dve.wait_ge(ahi_ready, blk + 1)
                V.tensor_tensor(a_lo[:, at], act_a[par][:, 0:w], a_hi[:, at].bitcast(F32), ALU.subtract).then_inc(alo_ready, 1)

            def hidden_s(b, j):
                blk = block_s(b) + j
                hidden(blk, blk % 2, a_at(blk, SEQ), SEQ)

            def x_low_s(b):
                q = job_s(b) % 2
                dve.wait_ge(xhi_ready, job_s(b) + 1)
                V.tensor_tensor(x_lo[q][:, :, 0:SEQ], zT_of(b), x_hi[q][:, :, 0:SEQ].bitcast(F32), ALU.subtract)\
                    .then_inc(xlo_ready, 1)

            def x_low_e(i, r):
                q = job_q(r)
                dve.wait_ge(xhi_ready, job_e(i, r) + 1)
                V.tensor_tensor(x_lo[q][:], psX[:, :, 0:HALF], x_hi[q][:].bitcast(F32), ALU.subtract).then_inc(xlo_ready, 1)

            def add(b):
                dve.wait_ge(rows_ready, job_s(b) + 1)
                if b >= ROUTED_FIRST:
                    dve.wait_ge(z_rows, b - ROUTED_FIRST + 1)
                V.tensor_tensor(Hb(b), Hb(b), rowsO[:, 0:TB * D], ALU.add).then_inc(rows_read, 1)

            def expert_weights(e, q):
                dve.wait_ge(ex_hi, e + 1)
                V.tensor_tensor(ex_w[q][1][:], ex_raw[q], ex_w[q][0][:].bitcast(F32), ALU.subtract).then_inc(ex_lo, 1)

            def combine(b):
                dve.wait_ge(gath[b % GATHERS], 16 * TB * TOPK * (b // GATHERS + 1))
                dve.wait_ge(rows_read, job_s(b) + 1)
                for k in range(TOPK):
                    if k:
                        dve.wait_ge(comb, TB * (TOPK * b + k))
                    for t in range(TB):
                        i = b * TB + t
                        V.scalar_tensor_tensor(out=H[:, i, :], in0=rows_of[b % GATHERS][:, t, k, :], scalar=wgt[k][:, i:i + 1],
                                               in1=H[:, i, :], op0=ALU.mult, op1=ALU.add).then_inc(comb, 1)

            scores()
            x_low_s(0)
            choose()
            hidden_s(0, 0)
            place(0)
            place(1)
            dve.sem_inc(routed, 1)
            hidden_s(0, 1)
            hidden_s(0, 2)
            x_low_s(1)
            hidden_s(0, 3)
            expert_weights(0, 0)
            for b in range(1, SH_FIRST):
                if b + 1 < SH_FIRST:
                    x_low_s(b + 1)
                for j in range(SB):
                    hidden_s(b, j)
                add(b - 1)
            x_low_e(0, 0)
            add(SH_FIRST - 1)

            def step(i, r):
                if exists(i, r + 1):
                    x_low_e(i, r + 1)
                else:
                    x_low_s(SH_FIRST)
                for j, slot in enumerate(block_slots(r)):
                    hidden(block_e(i, r) + j, slot % 2, a_at(slot, HALF), HALF)
                    if j == 0 and r % 2 == 1 and exists(i, r + 1):
                        expert_weights(expert(i, r + 1), xin_of(r + 1))

            units(dve, step)
            done = 0
            for b in range(SH_FIRST, B):
                if b + 1 < B:
                    x_low_s(b + 1)
                for j in range(SB):
                    hidden_s(b, j)
                    if j in COMBINE_AFTER and b > SH_FIRST and done < b - 1:
                        combine(done)
                        done += 1
                if b > SH_FIRST:
                    add(b - 1)
            for b in range(done, B - 1):
                combine(b)
            add(B - 1)
            combine(B - 1)

        @block.scalar
        def _(act):
            def expert_weights(i, r):
                q = xin_of(r)
                if exists(i, r - 3):
                    act.wait_ge(rows_ready, job_e(i, r - 3) + 1)
                if type(i) is not int or unit(i, r) >= 2:
                    act.wait_ge(ex_loaded[q], (i + (r // 4 if q == 0 else r // 4 + 1)) * 16)
                A.activation(ex_w[q][0][:], ex_raw[q], ACT.Copy).then_inc(ex_hi, 1)

            def z_of(b):
                act.wait_ge(scat[b % 4], 16 * TB * TOPK * (b // 4))
                for t in range(TB):
                    i = b * TB + t
                    a = A.activation(z_staged(ring, b, t), H[:, i, :], ACT.Identity, bias=nmz[:, i:i + 1], scale=rz[:, i:i + 1])
                a.then_inc(z_rows, 1)

            def silu(blk, par, w, first=False):
                act.wait_ge(gu_ready, blk + 1)
                if not first:
                    act.wait_ge(a_ready, blk - 1)
                A.activation(silu_g[par][:, 0:w], psGU[:, 2 * par, 0:w], ACT.Silu).then_inc(silu_ready, 1)

            def x_high_s(b):
                if b >= 2:
                    act.wait_ge(gu_ready, block_s(b) - (EB if b == SH_FIRST else SB))
                q = job_s(b) % 2
                A.activation(x_hi[q][:, :, 0:SEQ], zT_of(b), ACT.Copy).then_inc(xhi_ready, 1)

            def x_high_e(i, r):
                act.wait_ge(turned, unit(i, r) + 1)
                A.activation(x_hi[job_q(r)][:], psX[:, :, 0:HALF], ACT.Copy).then_inc(xhi_ready, 1)

            def silu_s(b, j):
                blk = block_s(b) + j
                silu(blk, blk % 2, SEQ, blk < 2)

            def y_of(i, r):
                act.wait_ge(rows_ready, job_e(i, r) + 1)
                act.wait_ge(y_stored[r % 2], (i * 2 + r // 2) * 16)
                A.activation(y_out[r % 2][:].rearrange("p t d -> p (t d)"), rowsO[0:XP, 0:XT * D], ACT.Copy).then_inc(rows_read, 1)

            x_high_s(0)
            act.wait_ge(route, 2)
            A.activation(rt["sc"][:, ROUTED_FIRST * TB:, :], rt["lg"][:, ROUTED_FIRST * TB:, :], ACT.Exp).then_inc(r_exp, 1)
            silu_s(0, 0)
            z_of(ROUTED_FIRST)
            x_high_s(1)
            silu_s(0, 1)
            silu_s(0, 2)
            z_of(ROUTED_FIRST + 1)
            silu_s(0, 3)
            expert_weights(0, 0)
            z_of(ROUTED_FIRST + 2)
            z_of(ROUTED_FIRST + 3)
            for b in range(1, SH_FIRST):
                if b + 1 < SH_FIRST:
                    x_high_s(b + 1)
                for j in range(SB):
                    silu_s(b, j)
            x_high_e(0, 0)

            def step(i, r):
                if exists(i, r + 1):
                    x_high_e(i, r + 1)
                else:
                    x_high_s(SH_FIRST)
                if exists(i, r - 2):
                    y_of(i, r - 2)
                for j, slot in enumerate(block_slots(r)):
                    silu(block_e(i, r) + j, slot % 2, HALF)
                    if j == 0 and r % 2 == 1 and exists(i, r + 1):
                        expert_weights(i, r + 1)

            units(act, step)
            y_of(0, UNITS - 2)
            y_of(0, UNITS - 1)
            for b in range(SH_FIRST, B):
                if b + 1 < B:
                    x_high_s(b + 1)
                for j in range(SB):
                    silu_s(b, j)

        @block.tensor
        def _(pe):
            def product(out, w, at, hi, lo, first, last):
                T.matmul(out, w[0][at], hi, start=first, stop=False)
                T.matmul(out, w[0][at], lo, start=False, stop=False)
                return T.matmul(out, w[1][at], hi, start=False, stop=last)

            def hidden(blk, par, j, q, n, w, ws, first=False):
                if not first:
                    pe.wait_ge(a_ready, blk - 1)
                for o, part in ((0, gate), (1, up)):
                    wg = [part(x, n) for x in ws]
                    for k in range(DC):
                        mm = product(psGU[:, 2 * par + o, 0:w], wg, (slice(None), k, slice(j * P, (j + 1) * P)),
                                     x_hi[q][:, k, 0:w], x_lo[q][:, k, 0:w], k == 0, k == DC - 1)
                mm.then_inc(gu_ready, 1)

            def down_rows(job, last_blk, n, ws, tiles, rows, cols_):
                wd = [down(x, n) for x in ws]
                pe.wait_ge(alo_ready, last_blk + 1)
                if type(job) is not int or job >= 1:
                    pe.wait_ge(rows_read, job)
                for t in range(tiles):
                    o = rowsO[0:rows, t * D:(t + 1) * D]
                    for k, c in enumerate(cols_):
                        r = slice(c.start + t * rows, c.start + (t + 1) * rows)
                        T.matmul(o, a_hi[:, r], wd[0][:, k, :], start=(k == 0), stop=False)
                        T.matmul(o, a_lo[:, r], wd[0][:, k, :], start=False, stop=False)
                        mm = T.matmul(o, a_hi[:, r], wd[1][:, k, :], start=False, stop=(k == len(cols_) - 1))
                mm.then_inc(rows_ready, 1)

            def hidden_s(b, j):
                blk = block_s(b) + j
                hidden(blk, blk % 2, j, job_s(b) % 2, I_SH, SEQ, sh_w, blk < 2)

            def down_s(b):
                blk = block_s(b)
                down_rows(job_s(b), blk + SB - 1, I_SH, sh_w, TB, P, [a_at(blk + k, SEQ) for k in range(SB)])

            def turn(i, r):
                q = xin_of(r)
                if r % 2 == 0:
                    pe.wait_ge(xin_loaded[q], (i + (r // 4 + 1)) * 16)
                if exists(i, r - 1):
                    pe.wait_ge(xlo_ready, job_e(i, r))
                for t in range(XT):
                    for k in range(DC):
                        mm = T.transpose(psX[:, k, t * XP:(t + 1) * XP], xin[q][:, (r % 2) * XT + t, k * P:(k + 1) * P],
                                         ident[0:XP, 0:XP])
                mm.then_inc(turned, 1)

            def hidden_e(i, r):
                pe.wait_ge(xlo_ready, job_e(i, r) + 1)
                if r % 2 == 0:
                    pe.wait_ge(ex_lo, expert(i, r) + 1)
                for j, slot in enumerate(block_slots(r)):
                    hidden(block_e(i, r) + j, slot % 2, j, job_q(r), I_EXP, HALF, ex_w[xin_of(r)])

            def down_e(i, r):
                down_rows(job_e(i, r), block_e(i, r) + EB - 1, I_EXP, ex_w[xin_of(r)], XT, XP,
                          [a_at(slot, HALF) for slot in block_slots(r)])

            pe.wait_ge(xlo_ready, 1)
            hidden_s(0, 0)
            hidden_s(0, 1)
            pe.wait_ge(counted, 1)
            places(T, psX[:, 1, :], rt, ROUTED_FIRST * TB, NT).then_inc(prefix, 1)
            hidden_s(0, 2)
            hidden_s(0, 3)
            for b in range(1, SH_FIRST):
                pe.wait_ge(xlo_ready, job_s(b) + 1)
                for j in range(SB):
                    hidden_s(b, j)
                down_s(b - 1)
            turn(0, 0)
            down_s(SH_FIRST - 1)

            def step(i, r):
                if exists(i, r + 1):
                    turn(i, r + 1)
                hidden_e(i, r)
                if exists(i, r - 1):
                    down_e(i, r - 1)

            units(pe, step)
            down_e(0, UNITS - 1)
            for b in range(SH_FIRST, B):
                pe.wait_ge(xlo_ready, job_s(b) + 1)
                for j in range(SB):
                    hidden_s(b, j)
                if b > SH_FIRST:
                    down_s(b - 1)
            down_s(B - 1)


def fusion_program(nc, log_dt, inv_a, a_im, b_ri, c_ri, txt, raw_w, cols, b1, ln2_scale, ln2_bias, gate_w,
                   sh_w, ex_w, out):
    io = dict(log_dt=log_dt, inv_a=inv_a, a_im=a_im, b_ri=b_ri, c_ri=c_ri, txt=txt, raw_w=raw_w, cols=cols, b1=b1,
              ln2_scale=ln2_scale, ln2_bias=ln2_bias, gate_w=gate_w, sh_w=sh_w, ex_w=ex_w)
    scratch = nc.dram_tensor("ssm_kernel", (S_SSM, B, D), F32, kind="Internal").ap()
    xs = nc.dram_tensor("expert_rows", (NE * CAP, D), F32, kind="Internal").ap()
    eo = nc.dram_tensor("expert_out", (NE * CAP, D), F32, kind="Internal").ap()
    with ExitStack() as ctx:
        sb = lambda name, shape, dt=F32: ctx.enter_context(nc.sbuf_tensor(name, shape, dt))
        per = dict(ident=sb("ident", [P, P]), raw=sb("raw", [P, W_SH + W_EX]), H=sb("H", [P, NT, D]))
        ssm_phase(nc, io, scratch, per, xs)
        per.update(zT=sb("zT", [P, DC, TOK]), gate_w=sb("gate_w", [P, DC, NE]), rz=sb("rz", [P, NT]), nmz=sb("nmz", [P, NT]))
        per.update(sh_w=[sb(f"sh_w{j}", [P, W_SH], FR) for j in range(2)])
        per.update(route=route_buffers(sb), scattered=[ctx.enter_context(nc.semaphore(f"scattered{q}")) for q in range(4)])
        attn_phase(nc, io, scratch, per, xs)
        moe_phase(nc, io, per, xs, eo, out)


def _half(a):
    return a.reshape(2, HP, N_STATE).transpose(0, 2, 1).reshape(P, HP)


def _blocks(w):
    return w.reshape(-1, P, w.shape[-1]).transpose(1, 0, 2).reshape(P, -1)


def kernel(**inputs):
    import numpy as np
    import concourse.bacc as bacc
    from concourse.bass_utils import run_bass_kernel_spmd

    a = {k: np.asarray(v) for k, v in inputs.items()}
    tok = lambda n: a["L0_tok_" + n]
    att = lambda n: a["L0_attn_" + n]
    ffn = lambda n: a["L0_ffn_" + n]
    column = lambda v: v.reshape(-1, P).T
    swiglu = lambda g, u, d: np.concatenate([_blocks(g.T), _blocks(u.T), _blocks(d.T)], 1)
    laid = dict(
        log_dt=tok("log_dt")[None],
        inv_a=_half(tok("inv_A_real")),
        a_im=_half(tok("A_imag")),
        b_ri=np.stack([_half(tok("B_ri")[..., i]) for i in range(2)]),
        c_ri=a["x"].reshape(B, 2, HP, N_STATE, 2).transpose(1, 3, 4, 2, 0).reshape(P, 2, HP, B),
        txt=a["txt"],
        raw_w=np.concatenate([_blocks(att(n)) for n in ("W_ret", "W1", "W2")], 1),
        cols=np.stack([column(att(n)) for n in ("b_ret", "ln1_scale", "ln1_bias", "b2")], 1),
        b1=column(att("b1")),
        ln2_scale=att("ln2_scale")[None],
        ln2_bias=att("ln2_bias")[None],
        gate_w=_blocks(ffn("gate_w").T).reshape(P, DC, NE),
        sh_w=swiglu(ffn("ws_gate"), ffn("ws_up"), ffn("ws_down")),
        ex_w=np.stack([swiglu(ffn("we_gate")[e], ffn("we_up")[e], ffn("we_down")[e]) for e in range(NE)]),
    )
    nc = bacc.Bacc("TRN2", target_bir_lowering=False, num_devices=1)
    arrays, args = {}, []
    for name, v in laid.items():
        v = np.ascontiguousarray(v)
        arrays[f"in_{name}"] = v
        args.append(nc.dram_tensor(f"in_{name}", v.shape, mybir.dt.from_np(v.dtype), kind="ExternalInput").ap())
    args.append(nc.dram_tensor("out_0", (B, SEQ, D), F32, kind="ExternalOutput").ap())
    fusion_program(nc, *args)
    r = run_bass_kernel_spmd(nc, [arrays], core_ids=[0])
    return r.results[0]["out_0"]
```
